# Optimizing a Trainium2 kernel written in Bass

```python
import numpy as np
import jax
import jax.numpy as jnp

def _softmax(x, axis=-1):
    return jax.nn.softmax(x, axis=axis)

def _gelu(x):
    return jax.nn.gelu(x, approximate=True)

def _silu(x):
    return jax.nn.silu(x)

def _sigmoid(x):
    return jax.nn.sigmoid(x)

def _layernorm(x, axis=-1, eps=1e-05):
    m = jnp.mean(x, axis=axis, keepdims=True)
    v = jnp.var(x, axis=axis, keepdims=True)
    return (x - m) / jnp.sqrt(v + eps)

def _scatter_add(tgt, idx, src, axis=0):
    return tgt.at[idx].add(src)

def _segment_sum(src, seg, n):
    return jax.ops.segment_sum(src, seg, n)
kernel_name = 'mk_flamingo_gated_d2_seqx_r8_ba2725'

def setup_inputs(seed: int=0):
    np.random.seed(seed)
    _w = jnp.asarray

    def _rec_inputs():
        import jax
        import jax.numpy as jnp
        _rk = jax.random.key(seed)
        x = 7.22e-05 + 1 * jax.random.normal(jax.random.fold_in(_rk, 1), (4, 512, 128), jnp.float32)
        _lenS = 512 - jax.random.randint(jax.random.fold_in(_rk, 7), (4,), 0, max(1, 512 // 4) + 1, jnp.int32)
        _lenS2 = 32 - jax.random.randint(jax.random.fold_in(_rk, 8), (4,), 0, max(1, 32 // 4) + 1, jnp.int32)
        _ctx_1024P = jax.random.normal(jax.random.fold_in(_rk, 11), (4, 16, 128), jnp.float32)
        _ctx_1024c = jax.random.dirichlet(jax.random.fold_in(_rk, 511), 0.3 * jnp.ones((16,), jnp.float32), (4, 32))
        _ctx_1024t = jnp.einsum('bsk,bkd->bsd', _ctx_1024c, _ctx_1024P)
        _ctx_1024t = _ctx_1024t * jax.lax.rsqrt(jnp.mean(jnp.square(_ctx_1024t)) + 1e-12) * 0.953939
        ctx_1024 = 4.13588e-05 + 0.999923 * (_ctx_1024t + 0.3 * jax.random.normal(jax.random.fold_in(_rk, 611), (4, 32, 128), jnp.float32))
        _validS = jnp.arange(512)[None, :] < _lenS[:, None]
        _validS2 = jnp.arange(32)[None, :] < _lenS2[:, None]
        _causal = jnp.tril(jnp.ones((512, 512), dtype=bool))
        mask_SxS2_bk0 = jnp.logical_not(jnp.broadcast_to(_validS2[0:1, :], (512, 32)))
        _g = jax.random.normal(jax.random.fold_in(_rk, 9001), (2, 2), jnp.float32)
        _g = jnp.sign(_g) * jnp.maximum(jnp.abs(_g), 1.0) + (_g == 0) * 1.0
        g_xattn = _g[0]
        g_ffn = _g[1]
        return (x, ctx_1024, mask_SxS2_bk0, g_xattn, g_ffn)
    x, ctx_1024, mask_SxS2_bk0, g_xattn, g_ffn = _rec_inputs()

    def _L0_xattn_setup():
        import jax, jax.numpy as jnp
        import numpy as np
        EMBED_DIM = 128
        B, QL, KL = (4, 256, 256)
        key = jax.random.key(seed)
        k1, k2, k3, k4 = jax.random.split(key, 4)
        hidden_states = jax.random.normal(k1, (B, QL, EMBED_DIM), dtype=jnp.float32)
        decoder_hidden_states = jax.random.normal(k2, (B, KL, EMBED_DIM), dtype=jnp.float32)
        Wq = jax.random.normal(k3, (EMBED_DIM, EMBED_DIM), dtype=jnp.float32) * (1.0 / np.sqrt(EMBED_DIM))
        Wkv = jax.random.normal(k4, (EMBED_DIM, 2 * EMBED_DIM), dtype=jnp.float32) * (1.0 / np.sqrt(EMBED_DIM))
        return {'hidden_states': hidden_states, 'decoder_hidden_states': decoder_hidden_states, 'Wq': Wq, 'Wkv': Wkv}
    _L0_xattn_all = _L0_xattn_setup()
    _L0_xattn_in = {k: v for k, v in _L0_xattn_all.items() if k in ('Wq', 'Wkv')}
    del _L0_xattn_all

    def _L0_ffn_setup():
        import math
        import jax, jax.numpy as jnp
        import numpy as np
        E = 8
        H = 128
        HP = 128
        SPARSITY = 8
        N_ROTATE = 64
        ROPE_BASE = 10000.0

        def _rope(x, pos):
            half = N_ROTATE // 2
            inv_freq = 1.0 / ROPE_BASE ** (jnp.arange(half, dtype=jnp.float32) * 2.0 / N_ROTATE)
            ang = pos.astype(jnp.float32)[..., None] * inv_freq
            sin, cos = (jnp.sin(ang), jnp.cos(ang))
            x1, x2 = (x[..., :half], x[..., half:])
            return jnp.concatenate([x1 * cos - x2 * sin, x2 * cos + x1 * sin], axis=-1)
        key = jax.random.key(seed)
        k1, k2, k3, k4 = jax.random.split(key, 4)
        B, T = (4, 1024)
        X = jax.random.normal(k1, (B, T, H), dtype=jnp.float32)
        Wr = jax.random.uniform(k2, (E, H), minval=-1 / math.sqrt(H), maxval=1 / math.sqrt(H), dtype=jnp.float32)
        bq = 1 / math.sqrt(3 * HP)
        Wqkv = jax.random.uniform(k3, (E, H, 3 * HP), minval=-bq, maxval=bq, dtype=jnp.float32)
        bo = 1 / math.sqrt(H * E)
        Wo = jax.random.uniform(k4, (E, HP, H), minval=-bo, maxval=bo, dtype=jnp.float32)
        return {'X': X, 'Wr': Wr, 'Wqkv': Wqkv, 'Wo': Wo}
    _L0_ffn_all = _L0_ffn_setup()
    _L0_ffn_in = {k: v for k, v in _L0_ffn_all.items() if k in ('Wr', 'Wqkv', 'Wo')}
    del _L0_ffn_all

    def _L1_xattn_setup():
        import jax, jax.numpy as jnp
        import numpy as np
        B, S, DIM, H = (4, 256, 128, 16)
        HD = DIM // H
        SCALE = HD ** (-0.5)

        def _heads(x):
            b, s, _ = x.shape
            return x.reshape(b, s, H, HD).transpose(0, 2, 1, 3)
        key = jax.random.key(seed)
        ks = jax.random.split(key, 7)
        init = 0.02
        return {'query': jax.random.normal(ks[0], (B, S, DIM), dtype=jnp.float32), 'key': jax.random.normal(ks[1], (B, S, DIM), dtype=jnp.float32), 'value': jax.random.normal(ks[2], (B, S, DIM), dtype=jnp.float32), 'attn_mask': jnp.tril(jnp.ones((S, S), dtype=bool)), 'Wq': jax.random.normal(ks[3], (DIM, DIM), dtype=jnp.float32) * init, 'Wk': jax.random.normal(ks[4], (DIM, DIM), dtype=jnp.float32) * init, 'Wv': jax.random.normal(ks[5], (DIM, DIM), dtype=jnp.float32) * init, 'Wo': jax.random.normal(ks[6], (DIM, DIM), dtype=jnp.float32) * init}
    _L1_xattn_all = _L1_xattn_setup()
    _L1_xattn_in = {k: v for k, v in _L1_xattn_all.items() if k in ('Wq', 'Wk', 'Wv', 'Wo')}
    del _L1_xattn_all

    def _L1_ffn_setup():
        import jax, jax.numpy as jnp
        import numpy as np
        LN_EPS = 1e-05

        def _swiglu(h, w_gate_up, w_down):
            gu = h @ w_gate_up.T
            gate, up = jnp.split(gu, 2, axis=-1)
            return jax.nn.silu(gate) * up @ w_down.T
        key = jax.random.key(seed)
        ks = jax.random.split(key, 6)
        d_model, d_ff, E = (128, 512, 8)
        shared_d_ff = d_ff // 4
        routed_d_ff = d_ff - shared_d_ff
        B, S = (4, 256)
        x = jax.random.normal(ks[0], (B, S, d_model), dtype=jnp.float32)
        ln_gamma = jnp.ones((d_model,), jnp.float32)
        ln_beta = jnp.zeros((d_model,), jnp.float32)
        router_w = jax.random.normal(ks[1], (E, d_model), jnp.float32) * 0.02
        gate_up_w = jax.random.normal(ks[2], (E, 2 * routed_d_ff, d_model), jnp.float32) * (1.0 / np.sqrt(d_model))
        down_w = jax.random.normal(ks[3], (E, d_model, routed_d_ff), jnp.float32) * (1.0 / np.sqrt(routed_d_ff))
        shared_gate_up_w = jax.random.normal(ks[4], (2 * shared_d_ff, d_model), jnp.float32) * (1.0 / np.sqrt(d_model))
        shared_down_w = jax.random.normal(ks[5], (d_model, shared_d_ff), jnp.float32) * (1.0 / np.sqrt(shared_d_ff))
        return dict(x=x, ln_gamma=ln_gamma, ln_beta=ln_beta, router_w=router_w, gate_up_w=gate_up_w, down_w=down_w, shared_gate_up_w=shared_gate_up_w, shared_down_w=shared_down_w)
    _L1_ffn_all = _L1_ffn_setup()
    _L1_ffn_in = {k: v for k, v in _L1_ffn_all.items() if k in ('ln_gamma', 'ln_beta', 'router_w', 'gate_up_w', 'down_w', 'shared_gate_up_w', 'shared_down_w')}
    del _L1_ffn_all
    return {'x': x, 'ctx_1024': ctx_1024, 'mask_SxS2_bk0': mask_SxS2_bk0, 'g_xattn': g_xattn, 'g_ffn': g_ffn, 'L0_xattn_Wq': _L0_xattn_in['Wq'], 'L0_xattn_Wkv': _L0_xattn_in['Wkv'], 'L0_ffn_Wr': _L0_ffn_in['Wr'], 'L0_ffn_Wqkv': _L0_ffn_in['Wqkv'], 'L0_ffn_Wo': _L0_ffn_in['Wo'], 'L1_xattn_Wq': _L1_xattn_in['Wq'], 'L1_xattn_Wk': _L1_xattn_in['Wk'], 'L1_xattn_Wv': _L1_xattn_in['Wv'], 'L1_xattn_Wo': _L1_xattn_in['Wo'], 'L1_ffn_ln_gamma': _L1_ffn_in['ln_gamma'], 'L1_ffn_ln_beta': _L1_ffn_in['ln_beta'], 'L1_ffn_router_w': _L1_ffn_in['router_w'], 'L1_ffn_gate_up_w': _L1_ffn_in['gate_up_w'], 'L1_ffn_down_w': _L1_ffn_in['down_w'], 'L1_ffn_shared_gate_up_w': _L1_ffn_in['shared_gate_up_w'], 'L1_ffn_shared_down_w': _L1_ffn_in['shared_down_w']}

def reference(x, ctx_1024, mask_SxS2_bk0, g_xattn, g_ffn, L0_xattn_Wq, L0_xattn_Wkv, L0_ffn_Wr, L0_ffn_Wqkv, L0_ffn_Wo, L1_xattn_Wq, L1_xattn_Wk, L1_xattn_Wv, L1_xattn_Wo, L1_ffn_ln_gamma, L1_ffn_ln_beta, L1_ffn_router_w, L1_ffn_gate_up_w, L1_ffn_down_w, L1_ffn_shared_gate_up_w, L1_ffn_shared_down_w):
    import jax
    import jax.numpy as jnp

    def _L0_xattn_ref(hidden_states, decoder_hidden_states, Wq, Wkv):
        import jax, jax.numpy as jnp
        import numpy as np
        EMBED_DIM = 128
        B, QL, KL = (4, 256, 256)
        d = Wq.shape[0]
        scale = 1.0 / np.sqrt(d)
        query = hidden_states @ Wq
        kv = decoder_hidden_states @ Wkv
        key, value = jnp.split(kv, 2, axis=-1)
        scores = jnp.einsum('bqd,bkd->bqk', query, key) * scale
        w = jax.nn.softmax(scores, axis=-1)
        return jnp.einsum('bqk,bkd->bqd', w, value)

    def _L0_ffn_ref(X, Wr, Wqkv, Wo):
        import math
        import jax, jax.numpy as jnp
        import numpy as np
        E = 8
        H = 128
        HP = 128
        SPARSITY = 8
        N_ROTATE = 64
        ROPE_BASE = 10000.0

        def _rope(x, pos):
            half = N_ROTATE // 2
            inv_freq = 1.0 / ROPE_BASE ** (jnp.arange(half, dtype=jnp.float32) * 2.0 / N_ROTATE)
            ang = pos.astype(jnp.float32)[..., None] * inv_freq
            sin, cos = (jnp.sin(ang), jnp.cos(ang))
            x1, x2 = (x[..., :half], x[..., half:])
            return jnp.concatenate([x1 * cos - x2 * sin, x2 * cos + x1 * sin], axis=-1)
        B, T, _ = X.shape
        k = min(max(T // SPARSITY, 2), T)
        logits = jax.nn.sigmoid(jnp.einsum('bth,eh->bte', X, Wr))
        topk_vals, topk_I = jax.lax.top_k(logits.transpose(0, 2, 1), k)
        idx_flat = topk_I.reshape(B, E * k)
        Xg = jnp.take_along_axis(X, idx_flat[:, :, None], axis=1).reshape(B, E, k, H)
        QKV = jnp.einsum('beki,eij->bekj', Xg, Wqkv)
        Q, K, V = jnp.split(QKV, 3, axis=-1)
        Q = jnp.concatenate([_rope(Q[..., :N_ROTATE], topk_I), Q[..., N_ROTATE:]], axis=-1)
        K = jnp.concatenate([_rope(K[..., :N_ROTATE], topk_I), K[..., N_ROTATE:]], axis=-1)
        M = topk_I[..., :, None] >= topk_I[..., None, :]
        scores = jnp.einsum('bekd,bemd->bekm', Q, K) / math.sqrt(HP)
        scores = jnp.where(M, scores, -jnp.inf)
        A = jax.nn.softmax(scores, axis=-1)
        AV = jnp.einsum('bekm,bemd->bekd', A, V)
        AV = AV * topk_vals[..., None]
        Xpre = jnp.einsum('bekj,eji->beki', AV, Wo)
        out = jnp.zeros((B, T, H), dtype=X.dtype)
        out = out.at[jnp.arange(B)[:, None], idx_flat].add(Xpre.reshape(B, E * k, H))
        return out

    def _L1_xattn_ref(query, key, value, attn_mask, Wq, Wk, Wv, Wo):
        import jax, jax.numpy as jnp
        import numpy as np
        B, S, DIM, H = (4, 256, 128, 16)
        HD = DIM // H
        SCALE = HD ** (-0.5)

        def _heads(x):
            b, s, _ = x.shape
            return x.reshape(b, s, H, HD).transpose(0, 2, 1, 3)
        q = _heads(query @ Wq.T)
        k = _heads(key @ Wk.T)
        v = _heads(value @ Wv.T)
        logits = jnp.einsum('bhqd,bhkd->bhqk', q, k) * SCALE
        mask = attn_mask[None, None, :, :]
        masked = jnp.where(mask, logits, -1000000000.0)
        weights = jax.nn.softmax(masked, axis=-1)
        weights = weights * mask.astype(weights.dtype)
        denom = jnp.maximum(weights.sum(axis=-1, keepdims=True), 1e-09)
        weights = weights / denom
        out = jnp.einsum('bhqk,bhkd->bhqd', weights, v)
        out = out.transpose(0, 2, 1, 3).reshape(query.shape[0], query.shape[1], -1)
        return out @ Wo.T

    def _L1_ffn_ref(x, ln_gamma, ln_beta, router_w, gate_up_w, down_w, shared_gate_up_w, shared_down_w):
        import jax, jax.numpy as jnp
        import numpy as np
        LN_EPS = 1e-05

        def _swiglu(h, w_gate_up, w_down):
            gu = h @ w_gate_up.T
            gate, up = jnp.split(gu, 2, axis=-1)
            return jax.nn.silu(gate) * up @ w_down.T
        B, S, D = x.shape
        E = router_w.shape[0]
        top_k = 2
        xt = x.reshape(-1, D)
        mu = jnp.mean(xt, axis=-1, keepdims=True)
        var = jnp.mean(jnp.square(xt - mu), axis=-1, keepdims=True)
        normed = (xt - mu) * jax.lax.rsqrt(var + LN_EPS) * ln_gamma + ln_beta
        logits = normed.astype(jnp.float32) @ router_w.T
        probs = jax.nn.softmax(logits, axis=-1)
        top_v, top_i = jax.lax.top_k(probs, top_k)
        gates = jax.nn.softmax(top_v, axis=-1)
        comb = jnp.sum(jax.nn.one_hot(top_i, E, dtype=gates.dtype) * gates[..., None], axis=1)
        out = jnp.zeros_like(normed)
        for e in range(E):
            y = _swiglu(normed, gate_up_w[e], down_w[e])
            out = out + comb[:, e, None] * y
        out = out + _swiglu(normed, shared_gate_up_w, shared_down_w)
        return out.reshape(B, S, D)
    x = x + jnp.tanh(g_xattn[0]) * _L0_xattn_ref(_layernorm(x, axis=-1), ctx_1024, L0_xattn_Wq, L0_xattn_Wkv)
    x = x + jnp.tanh(g_ffn[0]) * _L0_ffn_ref(_layernorm(x, axis=-1), L0_ffn_Wr, L0_ffn_Wqkv, L0_ffn_Wo)
    x = x + jnp.tanh(g_xattn[1]) * _L1_xattn_ref(_layernorm(x, axis=-1), ctx_1024, ctx_1024, mask_SxS2_bk0, L1_xattn_Wq, L1_xattn_Wk, L1_xattn_Wv, L1_xattn_Wo)
    x = x + jnp.tanh(g_ffn[1]) * _L1_ffn_ref(_layernorm(x, axis=-1), L1_ffn_ln_gamma, L1_ffn_ln_beta, L1_ffn_router_w, L1_ffn_gate_up_w, L1_ffn_down_w, L1_ffn_shared_gate_up_w, L1_ffn_shared_down_w)
    return x

_drawn_inputs = setup_inputs


def setup_inputs(seed=0):
    import zlib

    import numpy as np

    out = dict(_drawn_inputs(seed))
    spreads = {'g_ffn': (-1.0, 0.2), 'L1_ffn_ln_gamma': (1.0, 0.2), 'L1_ffn_ln_beta': (0.0, 0.1)}
    factors = {}
    for name, (base, spread) in spreads.items():
        noise = np.random.default_rng([zlib.crc32(name.encode()), seed]).standard_normal(out[name].shape)
        drawn = base * np.exp(spread * noise) if base else spread * noise
        out[name] = jnp.asarray(drawn.astype(out[name].dtype))
    for name, factor in factors.items():
        out[name] = (out[name] * factor).astype(out[name].dtype)
    return out
```

```python
from contextlib import ExitStack

import numpy as np
import concourse.bass as bass
from concourse import mybir

F32 = mybir.dt.float32
F16 = mybir.dt.float16
BF16 = mybir.dt.bfloat16
I32 = mybir.dt.int32
U32 = mybir.dt.uint32
ALU = mybir.AluOpType
ACT = mybir.ActivationFunctionType
AX = mybir.AxisListType
ds = bass.ds

P = 128
B, S, D = 4, 512, 128
T = S // P
NT = B * T
KC = 32
E = 8
J = S // E
H = 16
HD = D // H
HC = P // KC
NC = H // HC
NROT = 64
FF = 384
FC = FF // P
NF = 2 * FC
WS = 256.0
REG = B * S + P
TILES = 40
PAY_W = D + 3
LN_EPS = 1e-5
TOPV = -3.0e38
NQ = 2 * D + D + 1

W_QK = 0
W_GU = W_QK + E * 2 * D
W_DN = W_GU + E * 2 * FF
W_SG = W_DN + E * FC * D
W_SD = W_SG + 2 * D
W_END = W_SD + D
CH = 512
CHUNKS = -(-W_END // CH)
WLOAD = 4
WRING = 3 * WLOAD

C_ID, C_HM, C_HR, C_S, C_S128, C_EREG, C_I8, C_2T = 0, 128, 144, 160, 201, 242, 250, 258
C_END = C_2T + NT
G_ID, G_IOTA, G_TRIG, G_COMB, G_TRI, G_ONE = 0, 128, 192, 704, 832, 960
G_END = 1088


def skewed(n, depth):
    for step in range(n + depth - 1):
        for stage in reversed(range(depth)):
            if 0 <= step - stage < n:
                yield stage, step - stage


def build(nc, x_in, ctx_in, mask_in, gx_in, gf_in, wq0_in, wkv0_in, wr0_in, wv0_in, wo0_in, wk1_in,
          wq1_in, wv1_in, wo1_in, gamma_in, beta_in, router_in, wbig_in, c32_in, c16_in, cbf_in,
          pad_in, out):
    disp = nc.dram_tensor("dispatched_rows", ((E + 1) * REG, PAY_W), F32).ap()
    ytok = nc.dram_tensor("expert_rows", (2 * B * S + TILES * P + 1, D), F32).ap()
    x_v = x_in.rearrange("b (t p) d -> p (b t) d", p=P)
    out_v = out.rearrange("b (t p) d -> p (b t) d", p=P)
    ytok_v = ytok[0:2 * B * S, :].rearrange("(n p k) d -> p n (k d)", p=P, k=2)

    with ExitStack() as ctx:
        def sb(name, shape, dt=F32):
            return ctx.enter_context(nc.sbuf_tensor(name, shape, dt))

        def sem(name):
            return ctx.enter_context(nc.semaphore(name))

        bank = [ctx.enter_context(nc.psum_tensor(f"bank{i}", [P, 512], F32)) for i in range(8)]

        x = sb("x", [P, NT, D])
        c32 = sb("c32", [P, C_END])
        c16 = sb("c16", [P, G_END], F16)
        cbf = sb("cbf", [P, 2 * P], BF16)
        ident = c32[:, C_ID:C_ID + P]
        ident16 = c16[:, G_ID:G_ID + P]
        identbf = cbf[:, 0:P]
        causal = cbf[:, P:2 * P]
        tg = sb("tanh_gates", [P, 4])
        graw = sb("graw", [P, 4])
        st = sb("bn_raw", [P, NT, 6])
        mv = sb("mean_var", [P, NT, 2])
        ve = sb("var_eps", [P, NT])
        rstd = sb("rstd", [P, NT])
        mhalf = sb("minus_half", [P, NT])
        ctxr = sb("ctx_t", [P, B, HC, KC])
        wq0 = sb("wq0", [P, D])
        wkv0 = sb("wkv0", [P, 2 * D])
        wr0 = sb("wr0", [P, E])
        region_w = sb("region_w", [P, 2 * E * D])
        wv0 = region_w[:, 0:E * D].rearrange("p (e d) -> p e d", d=D)
        wo0 = region_w[:, E * D:2 * E * D].rearrange("p (e d) -> p e d", d=D)
        qk = region_w[:, 0:8 * D].rearrange("p (q h d) -> p q h d", q=4, h=2)
        qkt = region_w[:, E * D:E * D + 8 * P].rearrange("p (q n) -> p q n", q=4)
        wk1 = sb("wk1", [P, D])
        wq1 = sb("wq1", [P, D])
        wv1 = sb("wv1", [P, D])
        wo1 = sb("wo1", [P, D])
        gamma = sb("gamma", [P, D])
        beta = sb("beta", [P, D])
        router = sb("router", [P, E])
        router16 = sb("router16", [P, 2, E], F16)
        mask8 = sb("mask8", [P, T, KC], mybir.dt.uint8)
        maskf = sb("maskf", [P, T, KC])
        maskbf = sb("mask_bias", [P, T, KC], BF16)
        anyk = sb("any_key", [P, T])
        k0t = sb("k0t", [P, B * KC])
        k1t = sb("k1t", [P, B, KC])
        wk0 = sb("wq_k0", [P, B, KC])
        v0 = sb("v0", [KC, B, D])
        vblk = sb("v_blocks", [P, B, H, HD + 1])
        wf = sb("w_scaled", [P, WRING * CH])
        wh = sb("w_high", [P, CHUNKS * CH], F16)
        wl = sb("w_low", [P, CHUNKS * CH], F16)
        vwh = sb("vwo_high", [P, E, D + 1], F16)
        vwl = sb("vwo_low", [P, E, D + 1], F16)
        xh = sb("x_hat", [P, NT, D])
        region_t = sb("region_t", [P, NT * PAY_W])
        xt = region_t[:, 0:B * S].rearrange("p (b s) -> p b s", b=B)
        tab = region_t[:, 0:E * 2 * D].rearrange("p (e h d) -> p e h d", e=E, h=2)
        pay = region_t[:, :].rearrange("p (n w) -> p n w", w=PAY_W)
        es = sb("cross_sub", [P, B, T, KC])
        nm = sb("neg_max", [P, B, T])
        zs = sb("z_sum", [P, B, T])
        rz = sb("r_z", [P, B, T])
        et0 = sb("cross_e_t", [KC, B, S])
        region_s = sb("region_s", [P, 2 * NT * D], F16)
        xs = region_s[:, :].rearrange("p (h n d) -> p h n d", h=2, n=NT)
        yh = region_s[:, 0:E // 2 * B * D].rearrange("p (g b d) -> p g b d", g=E // 2, b=B)
        yl = region_s[:, E // 2 * B * D:E * B * D].rearrange("p (g b d) -> p g b d", g=E // 2, b=B)
        lg = sb("logits0", [P, T, B, E])
        region_k = sb("region_k", [P, 4, S])
        work, ones32, sel, scan = (region_k[0:B * E, i, :] for i in range(4))
        esl, etl = (region_k[:, i, :].rearrange("p (q n) -> p q n", q=4) for i in (1, 2))
        vv = xh
        rpa = region_k[:, 0, :].rearrange("p (q h d) -> p q h d", q=4, h=2)
        top8 = sb("top8", [B * E, 8])
        pos = sb("slot_of_token", [P, T, B, E])
        region_p = sb("region_p", [P, NT * E * J // 2])
        pick = region_p[:, :].bitcast(F16).rearrange("p (n c) -> p n c", n=NT)
        a1 = region_p[:, 0:B * H * KC].rearrange("p (b c) -> p b c", b=B)
        ntt = region_p[:, B * H * KC:2 * B * H * KC].bitcast(F16).rearrange("p (h n) -> p h n", h=2)
        region_q = sb("region_q", [P, NT * E * J // 2])
        pickt = region_q[:, :].bitcast(F16).rearrange("p (n g c) -> p n g c", n=NT, g=E // 2)
        yk = region_q[:, :].rearrange("p (n w) -> p n w", n=NT)
        region_x = sb("region_x", [P, 2 * E * B * J], F16)
        xg = region_x[:, :].rearrange("p (h e b j) -> p h e b j", h=2, e=E, b=B)
        trg = sb("trig_gathered", [P, E, B, J], F16)
        rpb = sb("rope_b", [P, 4, 2, NROT])
        lsl = sb("exp_neg_logit", [P, 4, 4])
        nms = sb("slot_neg_max", [P, 4])
        zsl = sb("slot_z", [P, 4])
        den = sb("slot_den", [P, 4])
        rzs = sb("slot_rz", [P, 4])

        kbl = region_p[:, B * H * KC:2 * B * H * KC].rearrange("p (b c) -> p b c", b=B)
        vrep = es[:, :, :, :].rearrange("p b t k -> p b (t k)")
        e1 = region_k[:, 0:2, :]
        e1t = region_k[:, 2:4, :]
        xf = region_x[:, :].bitcast(F32)
        xtc = xf[:, 0:2 * P].rearrange("p (r n) -> p r n", r=2)
        on = xf[:, 2 * P:4 * P].rearrange("p (r n) -> p r n", r=2)
        ont = xf[:, 4 * P:6 * P].rearrange("p (r n) -> p r n", r=2)
        nm1 = sb("nm1", [P, 2, H])
        zi = sb("z_inv", [P, 2, H])
        tgw = sb("tanh_gate_ws", [P, 1])
        rmax = sb("r_max", [P, T])
        prob = sb("r_prob", [P, T, E])
        rsum = sb("r_sum", [P, T])
        rtop = sb("r_top", [P, T, 8])
        ridx = sb("r_idx", [P, T, 8], U32)
        gexp = sb("gate_exp", [P, T])
        gden = sb("gate_den", [P, T])
        gate = sb("gates", [P, NT, 2])
        ef = sb("expert_of", [P, T, 2])
        oh = sb("one_hot", [P, T, 2, E])
        msel = sb("routed", [P, NT, E], F16)
        rk = sb("rank_row", [P, T, E])
        ohr = sb("one_hot_row", [P, T, 2, E])
        slotf = sb("slot_f", [P, T, 2])
        slot = sb("slot", [P, NT, 2], I32)
        tsum = sb("tile_sum", [P, E])
        base = sb("routed_before", [P, B + 1, E], F16)
        cnt = sb("count", [P, E])
        cnti = sb("count_i", [P, E], I32)
        ntil = sb("tiles_of", [P, E])
        ncum = sb("tiles_upto", [P, E])
        ge, gn = (xf[:, i * (TILES + 1) * E:(i + 1) * (TILES + 1) * E].rearrange("p (s e) -> p s e", e=E) for i in (2, 3))
        te = sb("tile_expert", [P, TILES + 1])
        tb = sb("tiles_before", [P, TILES + 1])
        trow = sb("tile_row", [P, TILES + 1])
        trow_i = sb("tile_row_i", [P, TILES + 1], I32)
        te_i = sb("tile_expert_i", [P, TILES + 1], I32)
        padr = sb("pad_row_i", [P, E], I32)
        onee = sb("ones_e", [P, E])
        padt = sb("pad_rows", [P, PAY_W])
        hs = region_w[:, 0:4 * CH].rearrange("p (r n) -> p r n", r=4)
        hsp = region_k[:, 0:2, :].bitcast(F16)
        xd = sb("slot_rows", [P, 4, PAY_W])
        dbase = sb("slot_dest_base", [P, 4])
        dst = sb("slot_dest", [P, 4], I32)
        xdt = sb("slot_rows_t", [P, 2, 2 * P], F16)
        sil = region_w[:, 0:2 * FF].rearrange("p (r n) -> p r n", r=2)
        hid = region_w[:, 2 * FF:4 * FF].rearrange("p (r n) -> p r n", r=2)
        hsplit = region_k[:, 0:2, 0:FF].bitcast(F16)
        yv = region_k[:, 2, :].rearrange("p (r n) -> p r n", r=4)

        ld_x = [sem(f"ld_x{b}") for b in range(B)]
        ld_ctx = sem("ld_ctx")
        ld_a = sem("ld_a")
        ld_c = sem("ld_c")
        ld_v = sem("ld_v")
        ld_m = sem("ld_m")
        ld_w = [sem(f"ld_w{i}") for i in range(-(-CHUNKS // WLOAD))]
        stored = sem("stored")
        v_link = sem("v_link")
        g_link = sem("g_link")
        a_link = sem("a_link")
        k_ps = sem("k_ps"); k_sb = sem("k_sb"); v0_sb = sem("v0_sb"); wk_ps = sem("wk_ps"); wk_sb = sem("wk_sb")
        tg_done = sem("tg_done")
        a_mv = sem("a_mv"); a_rs = sem("a_rs"); a_xh = sem("a_xh"); a_xt = sem("a_xt"); a_xte = sem("a_xte")
        a_s = sem("a_s"); a_sub = sem("a_sub"); a_e = sem("a_e"); a_et = sem("a_et"); a_ete = sem("a_ete")
        a_o = sem("a_o"); b_mv = sem("b_mv"); b_rs = sem("b_rs"); b_xh = sem("b_xh"); b_xt = sem("b_xt")
        b_xte = sem("b_xte"); b_hi = sem("b_hi"); b_lo = sem("b_lo"); b_l = sem("b_l"); b_le = sem("b_le")
        w_hi = sem("w_hi"); w_lo = sem("w_lo")
        vw_ps = sem("vw_ps"); vw_hi = sem("vw_hi"); vw_sb = sem("vw_sb")
        l_t = sem("l_t"); p_sb = sem("p_sb"); p_t = sem("p_t")
        pk = sem("pk"); g_ps = sem("g_ps"); g_ev = sem("g_ev"); g_evt = sem("g_evt"); pt_ps = sem("pt_ps"); pt_sb = sem("pt_sb")
        tb_ps = sem("tb_ps"); tb_sb = sem("tb_sb")

        q_ps = sem("q_ps"); q_rope = sem("q_rope"); q_add = sem("q_add"); q_cp = sem("q_cp")
        t_ps = sem("t_ps"); t_sb = sem("t_sb"); s_ps = sem("s_ps"); s_max = sem("s_max"); s_exp = sem("s_exp")
        s_den = sem("s_den"); s_rz = sem("s_rz"); s_scl = sem("s_scl"); et_ps = sem("et_ps"); et_sb = sem("et_sb")
        y_ps = sem("y_ps"); y_hi = sem("y_hi"); y_lo = sem("y_lo")
        k1_ps = sem("k1_ps"); k1_sb = sem("k1_sb"); v1_sb = sem("v1_sb"); vb_sb = sem("vb_sb"); kb_sb = sem("kb_sb")
        a1_ps = sem("a1_ps"); a1_sb = sem("a1_sb"); m_sb = sem("m_sb")
        c_o = sem("c_o"); c_mv = sem("c_mv"); c_rs = sem("c_rs"); c_xh = sem("c_xh"); c_xt = sem("c_xt")
        c_xte = sem("c_xte"); c_s = sem("c_s"); c_sub = sem("c_sub"); c_e = sem("c_e"); c_et = sem("c_et")
        c_ete = sem("c_ete"); c_pv = sem("c_pv"); c_on = sem("c_on"); c_ot = sem("c_ot"); c_ont = sem("c_ont")
        c_w = sem("c_w"); c_x = sem("c_x")
        n_mv = sem("n_mv"); n_rs = sem("n_rs"); n_xh = sem("n_xh"); n_aff = sem("n_aff"); n_hi = sem("n_hi")
        n_lo = sem("n_lo"); n_t = sem("n_t"); n_th = sem("n_th"); n_tl = sem("n_tl"); r_l = sem("r_l")
        r_sub = sem("r_sub"); r_exp = sem("r_exp"); r_d = sem("r_d"); r_ge = sem("r_ge"); r_m = sem("r_m")
        r_rk = sem("r_rk"); r_slot = sem("r_slot"); sent = sem("sent"); r16 = sem("r16")
        cn_ps = sem("cn_ps"); tiles = sem("tiles"); ld_pad = sem("ld_pad"); padded = sem("padded")
        h_ps = sem("h_ps"); h_si = sem("h_si"); h_h = sem("h_h"); h_hi = sem("h_hi"); h_lo = sem("h_lo")
        h_y = sem("h_y"); h_x = sem("h_x")
        d_ld = [sem(f"d_ld{r}") for r in range(4)]
        d_dst = sem("d_dst"); d_base = sem("d_base"); d_xt = sem("d_xt"); d_xe = sem("d_xe"); d_gu = sem("d_gu"); d_si = sem("d_si")
        d_h = sem("d_h"); d_hi = sem("d_hi"); d_lo = sem("d_lo"); d_y = sem("d_y"); d_yv = sem("d_yv")
        d_out = [sem(f"d_out{r}") for r in range(4)]
        ld_y = [sem(f"ld_y{b}") for b in range(B)]
        f_x = sem("f_x")

        def wait(eng, s, v):
            if not isinstance(v, int) or v > 0:
                eng.wait_ge(s, v)

        block = ctx.enter_context(nc.Block())

        @block.sync
        def _(eng):
            eng.dma_start(x[:, 0:T, :], x_v[:, 0:T, :]).then_inc(ld_x[0], 16)
            eng.dma_start(ctxr[:, :, :, :], ctx_in).then_inc(ld_ctx, 16)
            eng.dma_start(wkv0[:, :], wkv0_in).then_inc(ld_ctx, 16)
            for b in range(1, B):
                eng.dma_start(x[:, b * T:(b + 1) * T, :], x_v[:, b * T:(b + 1) * T, :]).then_inc(ld_x[b], 16)
            eng.dma_start(c16[:, :], c16_in).then_inc(ld_c, 16)
            eng.dma_start(cbf[:, :], cbf_in).then_inc(ld_c, 16)
            for i in range(len(ld_w)):
                lo, hi = i * WLOAD * CH, min((i + 1) * WLOAD * CH, W_END)
                at = lo % (WRING * CH)
                if i >= WRING // WLOAD:
                    eng.wait_ge(w_lo, (i + 1) * WLOAD - WRING)
                eng.dma_start(wf[:, at:at + hi - lo], wbig_in[:, lo:hi]).then_inc(ld_w[i], 16)
            eng.dma_start(padt[:, :], pad_in).then_inc(ld_pad, 16)
            eng.wait_ge(ld_pad, 16)
            eng.dma_start(disp[E * REG:E * REG + P, :], padt[:, :]).then_inc(padded, 16)
            eng.wait_ge(tiles, 1)
            for e in range(E):
                row = eng.value_load(padr[0:1, e:e + 1], min_val=0, max_val=E * REG)
                eng.dma_start(disp[ds(row, P), :], padt[:, :]).then_inc(padded, 16)
            eng.wait_ge(padded, 16 * (E + 1))
            eng.wait_ge(sent, 16 * 2 * NT)

            def load_slots(s, r):
                wait(eng, d_xt, s - 3)
                wait(eng, d_dst, s - 3)
                row = eng.value_load(trow_i[0:1, ds(s, 1)], min_val=0, max_val=E * REG)
                eng.dma_start(xd[:, r, :], disp[ds(row, P), :]).then_inc(d_ld[r], 16)

            for r in range(4):
                load_slots(r, r)
            with eng.Fori(1, TILES // 4) as i:
                for r in range(4):
                    load_slots(4 * i + r, r)
            for r in range(4):
                eng.wait_ge(d_out[r], 16 * (TILES // 4))
            for b in range(B):
                eng.dma_start(yk[:, b * T:(b + 1) * T, :], ytok_v[:, b * T:(b + 1) * T, :]).then_inc(ld_y[b], 16)
            for b in range(B):
                eng.wait_ge(f_x, b + 1)
                eng.dma_start(out_v[:, b * T:(b + 1) * T, :], x[:, b * T:(b + 1) * T, :]).then_inc(stored, 16)
            eng.wait_ge(stored, 16 * B)

        @block.scalar
        def _(act):
            act.dma_start(c32[:, :], c32_in).then_inc(ld_a, 16)
            act.dma_start(wq0[:, :], wq0_in).then_inc(ld_a, 16)
            act.dma_start(graw[:, 0:2], gx_in.rearrange("(a n) -> a n", a=1).partition_broadcast(P)).then_inc(ld_a, 16)
            act.dma_start(graw[:, 2:4], gf_in.rearrange("(a n) -> a n", a=1).partition_broadcast(P)).then_inc(ld_a, 16)
            act.dma_start(wr0[:, :], wr0_in).then_inc(ld_a, 16)
            act.dma_start(wv0, wv0_in).then_inc(ld_v, 16)
            act.dma_start(wo0, wo0_in).then_inc(ld_v, 16)
            act.dma_start(wk1[:, :], wk1_in).then_inc(ld_m, 16)
            act.dma_start(wq1[:, :], wq1_in).then_inc(ld_m, 16)
            act.dma_start(wv1[:, :], wv1_in).then_inc(ld_m, 16)
            act.dma_start(wo1[:, :], wo1_in).then_inc(ld_m, 16)
            act.dma_start(gamma[:, :], gamma_in.rearrange("(a n) -> a n", a=1).partition_broadcast(P)).then_inc(ld_m, 16)
            act.dma_start(beta[:, :], beta_in.rearrange("(a n) -> a n", a=1).partition_broadcast(P)).then_inc(ld_m, 16)
            act.dma_start(router[:, :], router_in).then_inc(ld_m, 16)
            act.dma_start(mask8[:, :, :], mask_in).then_inc(ld_m, 16)
            nc.scalar.preload_act_table(ACT.Exp)

            act.wait_ge(k_ps, 1)
            act.activation(k0t[:, :], bank[7][:, 0:B * KC], ACT.Copy).then_inc(k_sb, 1)
            act.wait_ge(wk_ps, 1)
            act.activation(wk0[:, :, :].rearrange("p b k -> p (b k)"), bank[7][:, P:P + B * KC], ACT.Copy).then_inc(wk_sb, 1)
            act.activation(v0[:, :, :].rearrange("p b k -> p (b k)"), bank[6][0:KC, :], ACT.Copy).then_inc(v0_sb, 1)
            act.wait_ge(ld_a, 80)
            act.activation(tg[:, :], graw[:, :], ACT.Tanh).then_inc(tg_done, 1)

            def split_high(i):
                if i % WLOAD == 0:
                    act.wait_ge(ld_w[i // WLOAD], 16)
                n = min(CH, W_END - i * CH)
                r = slice(i % WRING * CH, i % WRING * CH + n)
                act.activation(wf[:, r], wf[:, r], ACT.Copy, scale=WS).then_inc(a_link, 1)
                act.wait_ge(a_link, i + 1)
                act.activation(wh[:, i * CH:i * CH + n], wf[:, r], ACT.Copy).then_inc(w_hi, 1)

            chunk = 0
            for stage, b in skewed(B, 7):
                if stage == 1:
                    act.wait_ge(a_xt, b + 1)
                    act.activation(xt[:, b, :], bank[b % 2][:, :], ACT.Copy).then_inc(a_xte, 1)
                elif stage == 2:
                    act.wait_ge(a_sub, b + 1)
                    act.activation(es[:, b, :, :], es[:, b, :, :], ACT.Exp, scale=D ** -0.5).then_inc(a_e, 1)
                elif stage == 3:
                    act.wait_ge(a_et, b + 1)
                    act.activation(et0[:, b, :], bank[3][0:KC, :], ACT.Copy).then_inc(a_ete, 1)
                elif stage == 5:
                    act.wait_ge(b_xh, b + 1)
                    act.activation(xs[:, 0, b * T:(b + 1) * T, :], xh[:, b * T:(b + 1) * T, :], ACT.Copy).then_inc(b_hi, 1)
                    act.wait_ge(b_xt, b + 1)
                    act.activation(xt[:, b, :], bank[b % 2][:, :], ACT.Copy).then_inc(b_xte, 1)
                if stage in (3, 4) and chunk < 4:
                    split_high(chunk)
                    chunk += 1
            for h in range(2):
                act.wait_ge(vw_ps, h + 1)
                act.activation(vwh[:, 4 * h:4 * h + 4, 0:D], bank[4 + h][:, :].rearrange("p (e d) -> p e d", d=D),
                               ACT.Copy, scale=WS).then_inc(vw_hi, 1)
            act.activation(vwh[:, :, D], wr0[:, :], ACT.Copy, scale=WS).then_inc(vw_hi, 1)
            while chunk < CHUNKS:
                split_high(chunk)
                chunk += 1
            act.wait_ge(k1_ps, 1)
            act.activation(k1t[:, :, :].rearrange("p b k -> p (b k)"), bank[2][:, 0:B * KC], ACT.Copy).then_inc(k1_sb, 1)
            act.activation(vrep[:, :, :].rearrange("p b k -> p (b k)"), bank[3][:, :], ACT.Copy).then_inc(v1_sb, 1)
            for b in range(B):
                for t in range(T):
                    act.wait_ge(pt_ps, b * T + t + 1)
                    act.activation(pickt[:, b * T + t, :, :], bank[6 + t % 2][:, :].rearrange("p (g n) -> p g n", n=P),
                                   ACT.Copy).then_inc(pt_sb, 1)
                act.wait_ge(g_ps, b + 1)
                g = 3 * (b % 2)
                for h in range(2):
                    act.activation(xg[:, h, :, b, :], bank[g + h][:, :].rearrange("p (e j) -> p e j", j=J),
                                   ACT.Copy).then_inc(g_ev, 1)
            for b in range(B):
                act.wait_ge(a1_ps, b + 1)
                act.activation(a1[:, b, :], bank[4 + b % 2][:, :], ACT.Copy).then_inc(a1_sb, 1)

            def rows_out(g):
                for q in range(4):
                    act.wait_ge(q_rope, 4 * g + q + 1)
                    wait(act, t_ps, 2 * (g - 1) + q // 2 + 1)
                    act.activation(qk[:, q, :, NROT:D], bank[q][:, D:2 * D].rearrange("p (h d) -> p h d", h=2),
                                   ACT.Copy, scale=1.0 / WS)
                    act.activation(vv[:, 4 * g + q, :], bank[q][:, 2 * D:3 * D], ACT.Copy, scale=1.0 / WS)
                    act.activation(lsl[:, g, q:q + 1], bank[q][:, 3 * D:3 * D + 1], ACT.Exp, scale=-1.0 / WS).then_inc(q_cp, 1)

            def attend_act(g, more):
                for h in range(2):
                    act.wait_ge(t_ps, 2 * g + h + 1)
                    wait(act, s_ps, g)
                    act.activation(qkt[:, 2 * h:2 * h + 2, :].rearrange("p q n -> p (q n)"), bank[4 + h][:, :],
                                   ACT.Copy, scale=D ** -0.25).then_inc(t_sb, 1)
                act.wait_ge(s_max, g + 1)
                wait(act, et_ps, g)
                for q in range(4):
                    act.activation(esl[:, q, :], bank[6][:, q * P:(q + 1) * P], ACT.Exp, bias=nms[:, q:q + 1],
                                   accum_out=zsl[:, q:q + 1]).then_inc(s_exp, 1)
                if more:
                    rows_out(g + 1)
                act.wait_ge(et_ps, g + 1)
                wait(act, y_ps, g)
                act.activation(etl[:, :, :].rearrange("p q n -> p (q n)"), bank[4][:, :], ACT.Copy).then_inc(et_sb, 1)
                act.wait_ge(y_ps, g + 1)
                act.activation(yh[:, g, :, :].rearrange("p b d -> p (b d)"), bank[7][:, :], ACT.Copy).then_inc(y_hi, 1)

            rows_out(0)
            for g in range(E // 2):
                attend_act(g, g < E // 2 - 1)

            for k in range(NT + 12):
                if 0 <= k - 5 < NT:
                    t = k - 5
                    act.wait_ge(c_ot, t + 1)
                    wait(act, c_w, t - 1)
                    act.activation(ont[:, t % 2, :], bank[4][:, 0:P], ACT.Copy).then_inc(c_ont, 1)
                if 0 <= k - 3 < NT:
                    t = k - 3
                    act.wait_ge(c_et, t + 1)
                    wait(act, c_pv, t - 1)
                    act.activation(e1t[:, t % 2, :], bank[2][:, :], ACT.Copy).then_inc(c_ete, 1)
                if 0 <= k - 2 < NT:
                    t = k - 2
                    act.wait_ge(c_sub, t + 1)
                    act.activation(e1[:, t % 2, :], e1[:, t % 2, :], ACT.Exp, scale=HD ** -0.5).then_inc(c_e, 1)
                if 0 <= k < NT:
                    t = k
                    act.wait_ge(c_xt, t + 1)
                    wait(act, c_s, t - 1)
                    act.activation(xtc[:, t % 2, :], bank[0][:, 0:P], ACT.Copy).then_inc(c_xte, 1)
                b, r = divmod(k, 4)
                if r == 3 and 0 <= b - 2 < B:
                    b -= 2
                    act.wait_ge(n_aff, b + 1)
                    act.activation(pay[:, b * T:(b + 1) * T, 0:D // 2].bitcast(F16), xh[:, b * T:(b + 1) * T, :],
                                   ACT.Copy).then_inc(n_hi, 1)
                elif r == 0 and 0 <= b - 3 < B:
                    b -= 3
                    act.wait_ge(n_t, 2 * b + 1)
                    act.activation(ntt[:, 0, b * S:(b + 1) * S], bank[6][:, :], ACT.Copy).then_inc(n_th, 1)
                elif r == 1 and 0 <= b - 3 < B:
                    b -= 3
                    act.wait_ge(r_sub, b + 1)
                    act.activation(prob[:, :, :], prob[:, :, :], ACT.Exp, scale=1.0 / WS).then_inc(r_exp, 1)
                    act.wait_ge(r_d, b + 1)
                    act.activation(gexp[:, :], gexp[:, :], ACT.Exp).then_inc(r_ge, 1)

            nc.scalar.preload_act_table(ACT.Silu)
            for b in range(B + 1):
                if b >= 1:
                    act.wait_ge(h_h, b)
                    act.activation(hsp[:, (b - 1) % 2, 0:S], hs[:, 2 + (b - 1) % 2, :], ACT.Copy).then_inc(h_hi, 1)
                if b < B:
                    act.wait_ge(h_ps, 2 * b + 1)
                    wait(act, h_h, b - 1)
                    act.activation(hs[:, b % 2, :], bank[2 * (b % 2)][:, :], ACT.Silu, scale=1.0 / WS).then_inc(h_si, 1)

            def step_act(s, u):
                static = isinstance(s, int)
                if not static or 0 <= s + 1 < TILES:
                    act.wait_ge(d_h, s + 2)
                    wait(act, d_y, s)
                    act.activation(hsplit[:, (u + 1) % 2, 0:FF], hid[:, (u + 1) % 2, :], ACT.Copy).then_inc(d_hi, 1)
                if not static or 0 <= s + 3 < TILES:
                    act.wait_ge(d_xt, s + 4)
                    wait(act, d_gu, s + 2)
                    act.activation(xdt[:, (u + 3) % 2, :], bank[4 + (u + 3) % 2][:, 0:2 * P], ACT.Copy).then_inc(d_xe, 1)
                if not static or 0 <= s + 2 < TILES:
                    act.wait_ge(d_gu, s + 3)
                    wait(act, d_h, s + 1)
                    act.activation(sil[:, u % 2, :], bank[u % 2][:, 0:FF], ACT.Silu, scale=1.0 / WS).then_inc(d_si, 1)

            for s in range(-3, 5):
                step_act(s, s % 4)
            with act.Fori(1, TILES // 4 - 1) as i:
                for u in range(1, 5):
                    step_act(4 * i + u, u % 4)
            for s in range(TILES - 3, TILES + 1):
                step_act(s, s % 4)

        @block.gpsimd
        def _(pool):
            links = [0]

            def link(ins):
                links[0] += 1
                ins.then_inc(g_link, 1)
                pool.wait_ge(g_link, links[0])

            def bcp(ap, n):
                p, a = ap.shape
                return ap.rearrange("p (a o) -> p a o", o=1).to_broadcast((p, a, n))

            link(pool.memset(mhalf[:, :], -0.5))

            def rstd_of(b, ready, done):
                n = slice(b * T, (b + 1) * T)
                pool.wait_ge(ready, b + 1)
                link(pool.tensor_scalar(ve[:, n], mv[:, n, 1], LN_EPS, 1.0, ALU.add, ALU.mult))
                pool.tensor_tensor(rstd[:, n], ve[:, n], mhalf[:, n], ALU.pow).then_inc(done, 1)

            def split_low(i):
                pool.wait_ge(w_hi, i + 1)
                n = min(CH, W_END - i * CH)
                r = slice(i % WRING * CH, i % WRING * CH + n)
                c = slice(i * CH, i * CH + n)
                pool.tensor_tensor(wl[:, c], wf[:, r], wh[:, c], ALU.subtract).then_inc(w_lo, 1)

            for stage, b in skewed(B, 7):
                n = slice(b * T, (b + 1) * T)
                if stage == 0:
                    rstd_of(b, a_mv, a_rs)
                elif stage == 4:
                    rstd_of(b, b_mv, b_rs)
                elif stage == 5:
                    pool.wait_ge(b_hi, b + 1)
                    pool.tensor_tensor(xs[:, 1, n, :], xh[:, n, :], xs[:, 0, n, :], ALU.subtract).then_inc(b_lo, 1)
            pool.wait_ge(ld_m, 128)
            link(pool.tensor_copy(maskf[:, :, :], mask8[:, :, :]))
            pool.tensor_scalar(maskbf[:, :, :], maskf[:, :, :], -1.0, 1e9, ALU.add, ALU.mult).then_inc(m_sb, 1)
            for i in range(12):
                split_low(i)
            pool.wait_ge(v1_sb, 1)
            for b in range(B):
                pool.tensor_tensor(vblk[:, b, :, 0:HD], vrep[:, b, :].rearrange("p (h d) -> p h d", d=HD),
                                   bcp(c32[:, C_HR:C_HR + H], HD), ALU.mult)
                pool.tensor_copy(vblk[:, b, :, HD], c32[:, C_HR:C_HR + H]).then_inc(vb_sb, 1)
            pool.wait_ge(g_ps, B)
            pool.wait_ge(pt_ps, NT)
            for b in range(B):
                pool.tensor_tensor(kbl[:, b, :].rearrange("p (h k) -> p h k", k=KC),
                                   k1t[:, b, :].rearrange("p (a k) -> p a k", a=1).to_broadcast((P, H, KC)),
                                   bcp(c32[:, C_HM:C_HM + H], KC), ALU.mult).then_inc(kb_sb, 1)

            def add_rotated(g):
                for q in range(4):
                    pool.wait_ge(q_rope, 4 * g + q + 1)
                    wait(pool, t_ps, 2 * (g - 1) + q // 2 + 1)
                    pool.tensor_tensor(qk[:, q, :, 0:NROT], rpa[:, q, :, :], rpb[:, q, :, :], ALU.add).then_inc(q_add, 1)

            for g in range(E // 2):
                add_rotated(g)
                for i in range(12 + 3 * g, min(15 + 3 * g, CHUNKS)):
                    split_low(i)

            for b in range(B):
                rstd_of(b, c_mv, c_rs)
            for b in range(B + 1):
                if b < B:
                    n = slice(b * T, (b + 1) * T)
                    rstd_of(b, n_mv, n_rs)
                    pool.wait_ge(n_xh, b + 1)
                    link(pool.tensor_tensor(xh[:, n, :], xh[:, n, :],
                                            gamma[:, :].rearrange("p (a d) -> p a d", a=1).to_broadcast((P, T, D)), ALU.mult))
                    pool.tensor_tensor(xh[:, n, :], xh[:, n, :],
                                       beta[:, :].rearrange("p (a d) -> p a d", a=1).to_broadcast((P, T, D)),
                                       ALU.add).then_inc(n_aff, 1)
                if b >= 1:
                    pool.wait_ge(r_slot, b)
                    pool.wait_ge(n_hi, b)
                    pool.wait_ge(n_lo, b)
                    for t in range((b - 1) * T, b * T):
                        for c in range(2):
                            pool.indirect_dma_start(disp, bass.IndirectOffsetOnAxis(slot[:, t, c:c + 1].bitcast(U32), 0),
                                                    pay[:, t, :], None).then_inc(sent, 16)

            due = pool.alloc_register("tiles_due")
            pool.reg_mov(due, 1)
            with pool.Fori(0, TILES // 4):
                for r in range(4):
                    pool.wait_ge(d_yv, due)
                    pool.reg_add(due, due, 1)
                    pool.indirect_dma_start(ytok, bass.IndirectOffsetOnAxis(dst[:, r:r + 1].bitcast(U32), 0),
                                            yv[:, r, :], None).then_inc(d_out[r], 16)

        @block.vector
        def _(dve):
            links = [0]

            def link(ins):
                links[0] += 1
                ins.then_inc(v_link, 1)
                dve.wait_ge(v_link, links[0])

            def norm_stats(b, done):
                for t in range(b * T, (b + 1) * T):
                    last = dve.bn_stats(st[:, t, :], x[:, t, :])
                link(last)
                for t in range(b * T, (b + 1) * T):
                    last = dve.bn_aggr(mv[:, t, :], st[:, t, :])
                last.then_inc(done, 1)

            def normalise(b, done):
                for t in range(b * T, (b + 1) * T):
                    last = dve.tensor_scalar(xh[:, t, :], x[:, t, :], mv[:, t, 0:1], rstd[:, t:t + 1],
                                             ALU.subtract, ALU.mult)
                last.then_inc(done, 1)

            def bc(ap, n):
                p, a = ap.shape
                return ap.rearrange("p (a o) -> p a o", o=1).to_broadcast((p, a, n))

            for stage, b in skewed(B, 7):
                if stage == 0:
                    dve.wait_ge(ld_x[b], 16)
                    norm_stats(b, a_mv)
                elif stage == 1:
                    dve.wait_ge(a_rs, b + 1)
                    dve.wait_ge(a_mv, b + 1)
                    normalise(b, a_xh)
                elif stage == 2:
                    s3 = bank[2][:, 0:T * KC].rearrange("p (t k) -> p t k", k=KC)
                    dve.wait_ge(a_s, b + 1)
                    link(dve.tensor_reduce(nm[:, b, :], s3, AX.X, ALU.max, negate=True))
                    dve.tensor_tensor(es[:, b, :, :], s3, bc(nm[:, b, :], KC), ALU.add).then_inc(a_sub, 1)
                elif stage == 3:
                    dve.wait_ge(a_e, b + 1)
                    link(dve.tensor_reduce(zs[:, b, :], es[:, b, :, :], AX.X, ALU.add))
                    link(dve.reciprocal(rz[:, b, :], zs[:, b, :]))
                    if b == 0:
                        dve.wait_ge(tg_done, 1)
                    link(dve.tensor_scalar(rz[:, b, :], rz[:, b, :], tg[:, 0:1], None, ALU.mult))
                elif stage == 4:
                    dve.wait_ge(a_o, b + 1)
                    for t in range(T):
                        last = dve.scalar_tensor_tensor(x[:, b * T + t, :], bank[4 + b % 2][:, t * D:(t + 1) * D],
                                                        rz[:, b, t:t + 1], x[:, b * T + t, :], ALU.mult, ALU.add)
                    link(last)
                    norm_stats(b, b_mv)
                elif stage == 5:
                    dve.wait_ge(b_rs, b + 1)
                    dve.wait_ge(b_mv, b + 1)
                    dve.wait_ge(a_xt, b + 1)
                    normalise(b, b_xh)
                elif stage == 6:
                    dve.wait_ge(b_l, b + 1)
                    dve.tensor_copy(lg[:, :, b, :], bank[6][:, 0:T * E].rearrange("p (t e) -> p t e", e=E)).then_inc(b_le, 1)

            for h in range(2):
                dve.wait_ge(vw_hi, h + 1)
                dve.scalar_tensor_tensor(vwl[:, 4 * h:4 * h + 4, 0:D], bank[4 + h][:, :].rearrange("p (e d) -> p e d", d=D),
                                         WS, vwh[:, 4 * h:4 * h + 4, 0:D], ALU.mult, ALU.subtract).then_inc(vw_sb, 1)
            dve.wait_ge(vw_hi, 3)
            dve.scalar_tensor_tensor(vwl[:, :, D], wr0[:, :], WS, vwh[:, :, D], ALU.mult, ALU.subtract).then_inc(vw_sb, 1)

            dve.wait_ge(l_t, 1)
            dve.memset(ones32, 1.0)
            link(dve.tensor_copy(work, bank[0][0:B * E, :]))
            for _ in range(J // 8):
                link(dve.max(top8[:, :], work))
                link(dve.match_replace(work, top8[:, :], work, TOPV))
            link(dve.tensor_scalar(sel, work, TOPV, None, ALU.is_equal))
            link(dve.tensor_tensor_scan(scan, ones32, sel, 0.0, ALU.mult, ALU.add))
            dve.tensor_tensor(sel, scan, sel, ALU.mult).then_inc(p_sb, 1)
            dve.wait_ge(p_t, 1)
            link(dve.tensor_copy(pos[:, :, :, :].rearrange("p t b e -> p (t b e)"), bank[1][:, 0:P]))
            iota = c16[:, G_IOTA:G_IOTA + J].rearrange("p (a j) -> p a j", a=1).to_broadcast((P, E, J))
            dve.wait_ge(ld_c, 32)
            for b in range(B):
                for t in range(T):
                    dve.tensor_tensor(pick[:, b * T + t, :].rearrange("p (e j) -> p e j", j=J), iota,
                                      bc(pos[:, t, b, :], J), ALU.is_equal).then_inc(pk, 1)
                if b >= 1:
                    dve.wait_ge(g_ps, b)
                    dve.tensor_copy(trg[:, :, b - 1, :], bank[3 * ((b - 1) % 2) + 2][:, :].rearrange("p (e j) -> p e j", j=J)).then_inc(g_evt, 1)
            dve.wait_ge(g_ps, B)
            dve.tensor_copy(trg[:, :, B - 1, :], bank[5][:, :].rearrange("p (e j) -> p e j", j=J)).then_inc(g_evt, 1)
            dve.wait_ge(ld_m, 128)
            dve.wait_ge(m_sb, 1)
            link(dve.tensor_reduce(anyk[:, :], maskf[:, :, :], AX.X, ALU.max))
            for q in range(4):
                dve.wait_ge(tb_ps, q + 1)
                dve.tensor_scalar(tab[:, 2 * q:2 * q + 2, :, :].rearrange("p e h d -> p (e h d)"), bank[q][:, :], 1.0 / WS, None, ALU.mult).then_inc(tb_sb, 1)

            def rotate(g):
                for q in range(4):
                    e, h = 2 * g + q // 2, q % 2
                    src = bank[q][:, 0:D].rearrange("p (h d) -> p h d", h=2)

                    def table(c0, n):
                        t = tab[:, ds(e, 1), h, c0:c0 + n]
                        return t.to_broadcast((P, 2, n))

                    dve.wait_ge(q_ps, 4 * g + q + 1)
                    wait(dve, q_add, 4 * (g - 1) + q + 1)
                    half = NROT // 2
                    dve.tensor_tensor(rpa[:, q, :, :], src, table(0, NROT), ALU.mult)
                    dve.tensor_tensor(rpb[:, q, :, 0:half], src[:, :, half:NROT], table(NROT, half), ALU.mult)
                    dve.tensor_tensor(rpb[:, q, :, half:NROT], src[:, :, 0:half], table(NROT + half, half),
                                      ALU.mult).then_inc(q_rope, 1)

            def attend_dve(g, more):
                dve.wait_ge(s_ps, g + 1)
                dve.tensor_reduce(nms[:, :], bank[6][:, :].rearrange("p (q n) -> p q n", q=4), AX.X, ALU.max,
                                  negate=True).then_inc(s_max, 1)
                dve.wait_ge(s_exp, 4 * g + 4)
                dve.wait_ge(q_cp, 4 * g + 4)
                dve.scalar_tensor_tensor(den[:, :], lsl[:, g, :], 1.0, zsl[:, :], ALU.add, ALU.mult).then_inc(s_den, 1)
                dve.wait_ge(s_den, g + 1)
                dve.reciprocal(rzs[:, :], den[:, :]).then_inc(s_rz, 1)
                dve.wait_ge(s_rz, g + 1)
                for q in range(4):
                    last = dve.tensor_scalar(esl[:, q, :], esl[:, q, :], rzs[:, q:q + 1], None, ALU.mult)
                last.then_inc(s_scl, 1)
                if more:
                    rotate(g + 1)
                dve.wait_ge(y_hi, g + 1)
                dve.tensor_tensor(yl[:, g, :, :].rearrange("p b d -> p (b d)"), bank[7][:, :],
                                  yh[:, g, :, :].rearrange("p b d -> p (b d)"), ALU.subtract).then_inc(y_lo, 1)

            rotate(0)
            for g in range(E // 2):
                attend_dve(g, g < E // 2 - 1)

            for b in range(B + 1):
                if b < B:
                    n = slice(b * T, (b + 1) * T)
                    dve.wait_ge(c_o, b + 1)
                    xf32 = x[:, n, :].rearrange("p t d -> p (t d)")
                    link(dve.scalar_tensor_tensor(xf32, bank[b % 2][:, :], tg[:, 2:3], xf32, ALU.mult, ALU.add))
                    norm_stats(b, c_mv)
                if b >= 1:
                    dve.wait_ge(c_rs, b)
                    normalise(b - 1, c_xh)

            dve.memset(base[:, 0, :], 0.0)
            dve.memset(onee[:, :], 1.0)
            link(dve.tensor_scalar(tgw[:, :], tg[:, 3:4], 1.0 / WS, None, ALU.mult))
            dve.tensor_scalar(router16[:, 0, :], router[:, :], WS, None, ALU.mult).then_inc(v_link, 1)
            links[0] += 1
            dve.wait_ge(v_link, links[0])
            dve.scalar_tensor_tensor(router16[:, 1, :], router[:, :], WS, router16[:, 0, :], ALU.mult, ALU.subtract).then_inc(r16, 1)
            dve.tensor_copy(pay[:, :, D], c32[:, C_2T:C_2T + NT])
            dve.memset(pay[:, :, D + 2], 0.0)
            for k in range(NT + 12):
                if 0 <= k - 6 < NT:
                    t = k - 6
                    dve.wait_ge(c_w, t + 1)
                    dve.scalar_tensor_tensor(x[:, t, :], bank[5][:, 0:D], tg[:, 1:2], x[:, t, :], ALU.mult, ALU.add).then_inc(c_x, 1)
                    dve.wait_ge(c_x, t + 1)
                    last = dve.bn_stats(st[:, t, :], x[:, t, :])
                    if t % T == T - 1:
                        link(last)
                        for u in range(t - T + 1, t + 1):
                            last = dve.bn_aggr(mv[:, u, :], st[:, u, :])
                        last.then_inc(n_mv, 1)
                if 0 <= k - 4 < NT:
                    t = k - 4
                    o9 = bank[3][:, 0:H * (HD + 1)].rearrange("p (h d) -> p h d", d=HD + 1)
                    z = zi[:, t % 2, :]
                    dve.wait_ge(c_pv, t + 1)
                    link(dve.tensor_scalar(z, o9[:, :, HD], 1e-9, None, ALU.max))
                    link(dve.reciprocal(z, z))
                    wait(dve, c_ot, t - 1)
                    dve.scalar_tensor_tensor(on[:, t % 2, :].rearrange("p (h d) -> p h d", d=HD), o9[:, :, 0:HD],
                                             anyk[:, t % T:t % T + 1], bc(z, HD), ALU.mult, ALU.mult).then_inc(c_on, 1)
                if 0 <= k - 1 < NT:
                    t = k - 1
                    s3 = bank[1][:, :].rearrange("p (h k) -> p h k", k=KC)
                    dve.wait_ge(c_s, t + 1)
                    link(dve.tensor_reduce(nm1[:, t % 2, :], s3, AX.X, ALU.max, negate=True))
                    wait(dve, c_et, t - 1)
                    dve.tensor_tensor(e1[:, t % 2, :].rearrange("p (h k) -> p h k", k=KC), s3, bc(nm1[:, t % 2, :], KC),
                                      ALU.add).then_inc(c_sub, 1)
                b, r = divmod(k, 4)
                if r == 2 and 0 <= b - 2 < B:
                    b -= 2
                    dve.wait_ge(n_rs, b + 1)
                    dve.wait_ge(n_mv, b + 1)
                    normalise(b, n_xh)
                elif r == 3 and 0 <= b - 2 < B:
                    b -= 2
                    n = slice(b * T, (b + 1) * T)
                    dve.wait_ge(n_hi, b + 1)
                    dve.tensor_tensor(pay[:, n, D // 2:D].bitcast(F16), xh[:, n, :], pay[:, n, 0:D // 2].bitcast(F16),
                                      ALU.subtract).then_inc(n_lo, 1)
                elif r == 0 and 0 <= b - 3 < B:
                    b -= 3
                    dve.wait_ge(n_t, 2 * b + 2)
                    dve.tensor_copy(ntt[:, 1, b * S:(b + 1) * S], bank[7][:, :]).then_inc(n_tl, 1)
                elif r == 1 and 0 <= b - 3 < B:
                    b -= 3
                    n = slice(b * T, (b + 1) * T)
                    l3 = bank[6][:, 0:T * E].rearrange("p (t e) -> p t e", e=E)
                    dve.wait_ge(r_l, b + 1)
                    link(dve.tensor_reduce(rmax[:, :], l3, AX.X, ALU.max, negate=True))
                    dve.tensor_tensor(prob[:, :, :], l3, bc(rmax[:, :], E), ALU.add).then_inc(r_sub, 1)
                    dve.wait_ge(r_exp, b + 1)
                    link(dve.tensor_reduce(rsum[:, :], prob[:, :, :], AX.X, ALU.add))
                    link(dve.reciprocal(rsum[:, :], rsum[:, :]))
                    link(dve.tensor_tensor(prob[:, :, :], prob[:, :, :], bc(rsum[:, :], E), ALU.mult))
                    for t in range(T):
                        last = dve.max(rtop[:, t, :], prob[:, t, :])
                    link(last)
                    dve.tensor_tensor(gexp[:, :], rtop[:, :, 1], rtop[:, :, 0], ALU.subtract).then_inc(r_d, 1)
                    for t in range(T):
                        last = dve.max_index(ridx[:, t, :], rtop[:, t, :], prob[:, t, :])
                    link(last)
                    link(dve.tensor_copy(ef[:, :, :], ridx[:, :, 0:2]))
                    link(dve.tensor_tensor(oh[:, :, :, :].rearrange("p t c e -> p (t c) e"),
                                           c32[:, C_I8:C_I8 + E].rearrange("p (a e) -> p a e", a=1).to_broadcast((P, 2 * T, E)),
                                           bc(ef[:, :, :].rearrange("p t c -> p (t c)"), E), ALU.is_equal))
                    link(dve.tensor_tensor(msel[:, n, :], oh[:, :, 0, :], oh[:, :, 1, :], ALU.add))
                    link(dve.tensor_reduce(tsum[:, :], msel[:, n, :].rearrange("p t e -> p e t"), AX.X, ALU.add))
                    dve.tensor_tensor(base[:, b + 1, :], base[:, b, :], tsum[:, :], ALU.add).then_inc(r_m, 1)
                    dve.wait_ge(r_ge, b + 1)
                    link(dve.tensor_scalar(gden[:, :], gexp[:, :], 1.0, None, ALU.add))
                    link(dve.reciprocal(gden[:, :], gden[:, :]))
                    dve.tensor_scalar(gate[:, n, 0], gden[:, :], tg[:, 3:4], None, ALU.mult)
                    dve.scalar_tensor_tensor(gate[:, n, 1], gexp[:, :], tg[:, 3:4], gden[:, :], ALU.mult, ALU.mult)
                    dve.tensor_copy(pay[:, n, D + 1], ef[:, :, 0])
                b, r = divmod(k, 4)
                if r == 3 and 0 <= b - 3 < B:
                    b -= 3
                    n = slice(b * T, (b + 1) * T)
                    dve.wait_ge(r_rk, b + 1)
                    link(dve.tensor_tensor(rk[:, :, :], bank[7][:, 0:T * E].rearrange("p (t e) -> p t e", e=E),
                                           c32[:, C_EREG:C_EREG + E].rearrange("p (a e) -> p a e", a=1).to_broadcast((P, T, E)),
                                           ALU.add))
                    for c in range(2):
                        last = dve.tensor_tensor(ohr[:, :, c, :], oh[:, :, c, :], rk[:, :, :], ALU.mult)
                    link(last)
                    link(dve.tensor_reduce(slotf[:, :, :], ohr[:, :, :, :], AX.X, ALU.add))
                    dve.tensor_copy(slot[:, n, :], slotf[:, :, :]).then_inc(r_slot, 1)

            dve.wait_ge(cn_ps, 1)
            link(dve.tensor_copy(cnt[:, :], bank[6][:, 0:E]))
            link(dve.tensor_scalar(cnti[:, :], cnt[:, :], float(P - 1), None, ALU.add))
            link(dve.tensor_scalar(cnti[:, :], cnti[:, :], 7, None, ALU.logical_shift_right))
            link(dve.tensor_copy(ntil[:, :], cnti[:, :]))
            link(dve.tensor_tensor_scan(ncum[:, :], onee[:, :], ntil[:, :], 0.0, ALU.mult, ALU.add))
            m1 = TILES + 1

            def over_tiles(v):
                return v.rearrange("p (a e) -> p a e", a=1).to_broadcast((P, m1, E))

            link(dve.tensor_tensor(ge[:, :, :], bc(c32[:, C_S:C_S + m1], E), over_tiles(ncum[:, :]), ALU.is_ge))
            link(dve.tensor_reduce(te[:, :], ge[:, :, :], AX.X, ALU.add))
            link(dve.tensor_tensor(gn[:, :, :], ge[:, :, :], over_tiles(ntil[:, :]), ALU.mult))
            link(dve.tensor_reduce(tb[:, :], gn[:, :, :], AX.X, ALU.add))
            link(dve.scalar_tensor_tensor(trow[:, :], tb[:, :], -float(P), c32[:, C_S128:C_S128 + m1], ALU.mult, ALU.add))
            link(dve.scalar_tensor_tensor(trow[:, :], te[:, :], float(REG), trow[:, :], ALU.mult, ALU.add))
            dve.tensor_scalar(trow_i[:, :], trow[:, :], float(E * REG), None, ALU.min)
            dve.tensor_scalar(te_i[:, :], te[:, :], float(E - 1), None, ALU.min)
            dve.tensor_tensor(padr[:, :], cnt[:, :], c32[:, C_EREG:C_EREG + E], ALU.add).then_inc(tiles, 1)

            for b in range(B + 2):
                if 2 <= b:
                    c = b - 2
                    xf32 = x[:, c * T:(c + 1) * T, :].rearrange("p t d -> p (t d)")
                    dve.wait_ge(h_y, c + 1)
                    dve.scalar_tensor_tensor(xf32, bank[4 + c % 2][:, :], tgw[:, :], xf32, ALU.mult, ALU.add).then_inc(h_x, 1)
                if 1 <= b <= B:
                    c = b - 1
                    dve.wait_ge(h_hi, b)
                    dve.tensor_tensor(hsp[:, c % 2, S:2 * S], hs[:, 2 + c % 2, :], hsp[:, c % 2, 0:S], ALU.subtract).then_inc(h_lo, 1)
                if b < B:
                    dve.wait_ge(h_si, b + 1)
                    dve.wait_ge(h_ps, 2 * b + 2)
                    wait(dve, h_lo, b - 1)
                    dve.scalar_tensor_tensor(hs[:, 2 + b % 2, :], bank[2 * (b % 2) + 1][:, :], 1.0 / WS, hs[:, b % 2, :],
                                             ALU.mult, ALU.mult).then_inc(h_h, 1)

            def step_dve(s, u):
                static = isinstance(s, int)
                if not static or 0 <= s - 1 < TILES:
                    r = (u - 1) % 4
                    dve.wait_ge(d_y, s)
                    if not static or s - 1 >= 4:
                        dve.wait_ge(d_out[r], (s - 1 - r) * 4)
                    dve.tensor_scalar(yv[:, r, :], bank[6 + r % 2][:, 0:D], 1.0 / WS, None, ALU.mult).then_inc(d_yv, 1)
                if not static or 0 <= s + 1 < TILES:
                    dve.wait_ge(d_hi, s + 2)
                    dve.tensor_tensor(hsplit[:, (u + 1) % 2, FF:2 * FF], hid[:, (u + 1) % 2, :],
                                      hsplit[:, (u + 1) % 2, 0:FF], ALU.subtract).then_inc(d_lo, 1)
                if not static or 0 <= s + 2 < TILES:
                    dve.wait_ge(d_si, s + 3)
                    dve.scalar_tensor_tensor(hid[:, u % 2, :], bank[2 + u % 2][:, 0:FF], 1.0 / WS, sil[:, u % 2, :],
                                             ALU.mult, ALU.mult).then_inc(d_h, 1)

            def dest_dve(s, r):
                dve.wait_ge(d_ld[r], (s - r) * 4 + 16)
                if not isinstance(s, int) or s >= 4:
                    dve.wait_ge(d_out[r], (s - r) * 4)
                dve.scalar_tensor_tensor(dbase[:, r:r + 1], xd[:, r, D + 2:D + 3], c32[:, ds(C_S128 + s, 1)],
                                         xd[:, r, D:D + 1], ALU.mult, ALU.add).then_inc(d_base, 1)
                dve.wait_ge(d_base, s + 1)
                dve.scalar_tensor_tensor(dst[:, r:r + 1], xd[:, r, D + 1:D + 2], te[:, ds(s, 1)], dbase[:, r:r + 1],
                                         ALU.not_equal, ALU.add).then_inc(d_dst, 1)

            for s in range(-3, 5):
                step_dve(s, s % 4)
                dest_dve(s + 3, (s + 3) % 4)
            with dve.Fori(1, TILES // 4 - 1) as i:
                for u in range(1, 5):
                    step_dve(4 * i + u, u % 4)
                    dest_dve(4 * i + u + 3, (u + 3) % 4)
            for s in range(TILES - 3, TILES + 1):
                step_dve(s, s % 4)
            for b in range(B):
                dve.wait_ge(ld_y[b], 16)
                for c in range(2):
                    for t in range(b * T, (b + 1) * T):
                        last = dve.scalar_tensor_tensor(x[:, t, :], yk[:, t, c * D:(c + 1) * D], gate[:, t, c:c + 1],
                                                        x[:, t, :], ALU.mult, ALU.add)
                    if c == 0:
                        link(last)
                last.then_inc(f_x, 1)

        @block.tensor
        def _(pe):
            def mm(o, l, r, start=True, stop=True):
                return pe.matmul(o, l, r, start=start, stop=stop)

            pe.wait_ge(ld_ctx, 32)
            ctxt = ctxr[:, :, 0, :]
            mm(bank[7][:, 0:B * KC], wkv0[:, 0:D], ctxt).then_inc(k_ps, 1)
            for b in range(B):
                mm(bank[6][0:KC, b * D:(b + 1) * D], ctxr[:, b, 0, :], wkv0[:, D:2 * D])
            pe.wait_ge(k_sb, 1)
            pe.wait_ge(ld_a, 80)
            mm(bank[7][:, P:P + B * KC], wq0[:, :], k0t[:, :]).then_inc(wk_ps, 1)

            for stage, b in skewed(B, 7):
                n0 = b * T
                if stage == 1:
                    pe.wait_ge(a_xh, b + 1)
                    if b >= 2:
                        pe.wait_ge(a_xte, b - 1)
                    for t in range(T):
                        last = pe.transpose(bank[b % 2][:, t * P:(t + 1) * P], xh[:, n0 + t, :], ident)
                    last.then_inc(a_xt, 1)
                elif stage == 2:
                    pe.wait_ge(a_xte, b + 1)
                    pe.wait_ge(wk_sb, 1)
                    if b >= 1:
                        pe.wait_ge(a_sub, b)
                    for t in range(T):
                        last = mm(bank[2][:, t * KC:(t + 1) * KC], xt[:, b, t * P:(t + 1) * P], wk0[:, b, :])
                    last.then_inc(a_s, 1)
                elif stage == 3:
                    pe.wait_ge(a_e, b + 1)
                    if b >= 1:
                        pe.wait_ge(a_ete, b)
                    for t in range(T):
                        last = pe.transpose(bank[3][0:KC, t * P:(t + 1) * P], es[:, b, t, :], ident)
                    last.then_inc(a_et, 1)
                elif stage == 4:
                    pe.wait_ge(a_ete, b + 1)
                    pe.wait_ge(v0_sb, 1)
                    if b >= 2:
                        pe.wait_ge(b_mv, b - 1)
                    for t in range(T):
                        last = mm(bank[4 + b % 2][:, t * D:(t + 1) * D], et0[:, b, t * P:(t + 1) * P], v0[:, b, :])
                    last.then_inc(a_o, 1)
                elif stage == 5:
                    pe.wait_ge(b_xh, b + 1)
                    pe.wait_ge(a_xte, min(b + 4, B))
                    if b >= 2:
                        pe.wait_ge(b_xte, b - 1)
                    for t in range(T):
                        last = pe.transpose(bank[b % 2][:, t * P:(t + 1) * P], xh[:, n0 + t, :], ident)
                    last.then_inc(b_xt, 1)
                elif stage == 6:
                    pe.wait_ge(b_xte, b + 1)
                    if b >= 1:
                        pe.wait_ge(b_le, b)
                    for t in range(T):
                        last = mm(bank[6][:, t * E:(t + 1) * E], xt[:, b, t * P:(t + 1) * P], wr0[:, :])
                    last.then_inc(b_l, 1)

            pe.wait_ge(b_le, B)
            for t in range(T):
                last = pe.transpose(bank[0][0:B * E, t * P:(t + 1) * P], lg[:, t, :, :].rearrange("p b e -> p (b e)"), ident)
            last.then_inc(l_t, 1)
            pe.wait_ge(ld_v, 32)
            for e in range(E):
                last = mm(bank[4 + e // 4][:, (e % 4) * D:(e % 4 + 1) * D], wv0[:, e, :], wo0[:, e, :])
                if e % 4 == 3:
                    last.then_inc(vw_ps, 1)
            pe.wait_ge(ld_m, 128)
            mm(bank[2][:, 0:B * KC], wk1[:, :], ctxt)
            for b in range(B):
                last = mm(bank[3][:, b * D:(b + 1) * D], ctxr[:, b, :, :].rearrange("p r k -> p (r k)"), wv1[:, :])
            last.then_inc(k1_ps, 1)
            pe.wait_ge(p_sb, 1)
            for t in range(T):
                last = pe.transpose(bank[1][:, t * B * E:(t + 1) * B * E], sel[:, t * P:(t + 1) * P], ident[0:B * E, 0:B * E])
            last.then_inc(p_t, 1)
            pe.wait_ge(ld_c, 32)
            pe.wait_ge(b_lo, B)
            pe.wait_ge(vw_sb, 2)
            pe.wait_ge(v1_sb, 1)
            for b in range(B):
                g = 3 * (b % 2)
                for t in range(T):
                    n = b * T + t
                    pe.wait_ge(pk, n + 1)
                    if t == 0 and b >= 2:
                        pe.wait_ge(g_ev, 2 * (b - 1))
                        pe.wait_ge(g_evt, b - 1)
                    for h, lhs in ((0, xs[:, 0, n, :]), (1, xs[:, 1, n, :]), (2, c16[:, G_TRIG + t * D:G_TRIG + (t + 1) * D])):
                        last = mm(bank[g + h][:, :], lhs, pick[:, n, :], start=t == 0, stop=t == T - 1)
                    if t == T - 1:
                        last.then_inc(g_ps, 1)
                    if n >= 2:
                        pe.wait_ge(pt_sb, n - 1)
                    for p in range(E // 2):
                        last = mm(bank[6 + t % 2][:, p * P:(p + 1) * P], pick[:, n, p * P:(p + 1) * P], ident16)
                    last.then_inc(pt_ps, 1)
            pe.wait_ge(g_evt, B)
            pe.wait_ge(g_ev, 2 * B)
            for q in range(4):
                for u in range(4):
                    e, h = 2 * q + u // 2, u % 2
                    last = mm(bank[q][:, u * P:(u + 1) * P], trg[:, e, 2 * h:2 * h + 2, :].rearrange("p b j -> p (b j)"),
                              c16[:, G_COMB:G_COMB + P])
                last.then_inc(tb_ps, 1)

            pe.wait_ge(pt_sb, NT)
            for b in range(B):
                pe.wait_ge(kb_sb, b + 1)
                wait(pe, a1_sb, b - 1)
                mm(bank[4 + b % 2][:, :], wq1[:, :], kbl[:, b, :]).then_inc(a1_ps, 1)

            def project(g):
                for q in range(4):
                    e, h = 2 * g + q // 2, q % 2
                    xa, xb = (xg[:, i, ds(e, 1), 2 * h:2 * h + 2, :].rearrange("p e b j -> p (e b j)") for i in range(2))
                    if isinstance(g, int) and g == 0:
                        pe.wait_ge(tb_sb, q + 1)
                        pe.wait_ge(w_lo, 4)
                        pe.wait_ge(vw_sb, 3)
                    else:
                        pe.wait_ge(q_cp, 4 * (g - 1) + q + 1)
                    for c0, n, wa, wb in (
                            (0, 2 * D, wh[:, ds(W_QK + 2 * D * e, 2 * D)], wl[:, ds(W_QK + 2 * D * e, 2 * D)]),
                            (2 * D, D + 1, vwh[:, ds(e, 1), :].rearrange("p e d -> p (e d)"),
                             vwl[:, ds(e, 1), :].rearrange("p e d -> p (e d)"))):
                        o = bank[q][:, c0:c0 + n]
                        mm(o, xa, wa, True, False)
                        mm(o, xa, wb, False, False)
                        last = mm(o, xb, wa, False, True)
                    last.then_inc(q_ps, 1)

            def attend_pe(g, more):
                wait(pe, et_sb, g)
                for q in range(4):
                    pe.wait_ge(q_add, 4 * g + q + 1)
                    pe.wait_ge(q_cp, 4 * g + q + 1)
                    for h in range(2):
                        c = (q % 2) * 2 * P + h * P
                        last = pe.transpose(bank[4 + q // 2][:, c:c + P], qk[:, q, h, :], ident)
                    if q % 2:
                        last.then_inc(t_ps, 1)
                for q in range(4):
                    if q % 2 == 0:
                        pe.wait_ge(t_sb, 2 * g + q // 2 + 1)
                    if q == 0:
                        wait(pe, s_exp, 4 * g)
                    o = bank[6][:, q * P:(q + 1) * P]
                    mm(o, identbf, causal, True, False)
                    last = mm(o, qkt[:, q, 0:P], qkt[:, q, P:2 * P], False, True)
                last.then_inc(s_ps, 1)
                if more:
                    project(g + 1)
                pe.wait_ge(s_scl, g + 1)
                for q in range(4):
                    last = pe.transpose(bank[4][:, q * P:(q + 1) * P], esl[:, q, :], ident)
                last.then_inc(et_ps, 1)
                pe.wait_ge(et_sb, g + 1)
                wait(pe, y_lo, g)
                for q in range(4):
                    for h in range(2):
                        b = 2 * (q % 2) + h
                        last = mm(bank[7][J * (q // 2):J * (q // 2 + 1), b * D:(b + 1) * D], etl[:, q, h * J:(h + 1) * J],
                                  vv[:, 4 * g + q, :])
                last.then_inc(y_ps, 1)

            pe.wait_ge(a1_sb, B)
            project(0)
            for g in range(E // 2):
                attend_pe(g, g < E // 2 - 1)

            pe.wait_ge(y_lo, E // 2)
            for b in range(B):
                wait(pe, c_mv, b - 1)
                for t in range(T):
                    o = bank[b % 2][:, t * D:(t + 1) * D]
                    for g in range(E // 2):
                        mm(o, pickt[:, b * T + t, g, :], yh[:, g, b, :], g == 0, False)
                        last = mm(o, pickt[:, b * T + t, g, :], yl[:, g, b, :], False, g == E // 2 - 1)
                last.then_inc(c_o, 1)

            pe.wait_ge(c_mv, B)
            pe.wait_ge(m_sb, 1)
            pe.wait_ge(vb_sb, B)
            for k in range(NT + 12):
                if 0 <= k - 6 < NT:
                    t = k - 6
                    pe.wait_ge(c_ont, t + 1)
                    wait(pe, c_x, t)
                    mm(bank[5][:, 0:D], ont[:, t % 2, :], wo1[:, :]).then_inc(c_w, 1)
                if 0 <= k - 5 < NT:
                    t = k - 5
                    pe.wait_ge(c_on, t + 1)
                    wait(pe, c_ont, t)
                    pe.transpose(bank[4][:, 0:P], on[:, t % 2, :], ident).then_inc(c_ot, 1)
                if 0 <= k - 4 < NT:
                    t = k - 4
                    pe.wait_ge(c_ete, t + 1)
                    wait(pe, c_on, t)
                    for c in range(NC):
                        n = HC * (HD + 1)
                        last = mm(bank[3][:, c * n:(c + 1) * n], e1t[:, t % 2, c * P:(c + 1) * P],
                                  vblk[:, t // T, c * HC:(c + 1) * HC, :].rearrange("p h d -> p (h d)"))
                    last.then_inc(c_pv, 1)
                if 0 <= k - 3 < NT:
                    t = k - 3
                    pe.wait_ge(c_e, t + 1)
                    wait(pe, c_ete, t)
                    for c in range(NC):
                        last = pe.transpose(bank[2][:, c * P:(c + 1) * P], e1[:, t % 2, c * P:(c + 1) * P], ident)
                    last.then_inc(c_et, 1)
                if 0 <= k - 1 < NT:
                    t = k - 1
                    pe.wait_ge(c_xte, t + 1)
                    wait(pe, c_sub, t)
                    mm(bank[1][:, :], identbf, maskbf[:, t % T:t % T + 1, :].to_broadcast((P, H, KC)), True, False)
                    mm(bank[1][:, :], xtc[:, t % 2, :], a1[:, t // T, :], False, True).then_inc(c_s, 1)
                if 0 <= k < NT:
                    t = k
                    pe.wait_ge(c_xh, t // T + 1)
                    wait(pe, c_xte, t)
                    pe.transpose(bank[0][:, 0:P], xh[:, t, :], ident).then_inc(c_xt, 1)
                b, r = divmod(k, 4)
                if r == 0 and 0 <= b - 3 < B:
                    b -= 3
                    wait(pe, r_slot, b)
                    wait(pe, r_m, b)
                    for h, s in ((0, n_hi), (1, n_lo)):
                        pe.wait_ge(s, b + 1)
                        for t in range(T):
                            w = pay[:, b * T + t, h * (D // 2):(h + 1) * (D // 2)].bitcast(F16)
                            last = mm(bank[6 + h][:, t * P:(t + 1) * P], w, ident16)
                        last.then_inc(n_t, 1)
                elif r == 1 and 0 <= b - 3 < B:
                    b -= 3
                    pe.wait_ge(n_th, b + 1)
                    pe.wait_ge(n_tl, b + 1)
                    pe.wait_ge(r16, 1)
                    for t in range(T):
                        c = slice(b * S + t * P, b * S + (t + 1) * P)
                        o = bank[6][:, t * E:(t + 1) * E]
                        mm(o, ntt[:, 0, c], router16[:, 0, :], True, False)
                        mm(o, ntt[:, 0, c], router16[:, 1, :], False, False)
                        last = mm(o, ntt[:, 1, c], router16[:, 0, :], False, True)
                    last.then_inc(r_l, 1)
                elif r == 3 and 0 <= b - 3 < B:
                    b -= 3
                    pe.wait_ge(r_m, b + 1)
                    tri, one = c16[:, G_TRI:G_TRI + P], c16[:, G_ONE:G_ONE + P]
                    for t in range(T):
                        o = bank[7][:, t * E:(t + 1) * E]
                        mm(o, tri, msel[:, b * T + t, :], True, False)
                        for u in range(t):
                            mm(o, one, msel[:, b * T + u, :], False, False)
                        last = mm(o, one, base[:, b, :], False, True)
                    last.then_inc(r_rk, 1)
                    if b == B - 1:
                        mm(bank[6][:, 0:E], one, base[:, B, :]).then_inc(cn_ps, 1)

            pe.wait_ge(w_lo, CHUNKS)
            for b in range(B + 1):
                if b < B:
                    wait(pe, h_h, b - 1)
                    for c in range(2):
                        w = slice(W_SG + c * D, W_SG + (c + 1) * D)
                        o, n = bank[2 * (b % 2) + c][:, :], slice(b * S, (b + 1) * S)
                        mm(o, wh[:, w], ntt[:, 0, n], True, False)
                        mm(o, wh[:, w], ntt[:, 1, n], False, False)
                        mm(o, wl[:, w], ntt[:, 0, n], False, True).then_inc(h_ps, 1)
                if b >= 1:
                    c = b - 1
                    pe.wait_ge(h_lo, b)
                    wait(pe, h_x, c - 1)
                    for t in range(T):
                        o = bank[4 + c % 2][:, t * D:(t + 1) * D]
                        hi = hsp[:, c % 2, t * P:(t + 1) * P]
                        lo = hsp[:, c % 2, S + t * P:S + (t + 1) * P]
                        mm(o, hi, wh[:, W_SD:W_SD + D], True, False)
                        mm(o, hi, wl[:, W_SD:W_SD + D], False, False)
                        last = mm(o, lo, wh[:, W_SD:W_SD + D], False, True)
                    last.then_inc(h_y, 1)

            def step_pe(s, u):
                static = isinstance(s, int)
                if not static or 0 <= s + 3 < TILES:
                    r = (u + 3) % 4
                    pe.wait_ge(d_ld[r], (s + 3 - r) * 4 + 16)
                    wait(pe, d_xe, s + 2)
                    for h in range(2):
                        w = xd[:, r, h * (D // 2):(h + 1) * (D // 2)].bitcast(F16)
                        last = mm(bank[4 + r % 2][:, h * P:(h + 1) * P], w, ident16)
                    last.then_inc(d_xt, 1)
                if not static or 0 <= s + 2 < TILES:
                    e = pe.value_load(te_i[0:1, ds(s + 2, 1)], min_val=0, max_val=E - 1)
                    pe.wait_ge(d_xe, s + 3)
                    wait(pe, d_h, s + 1)
                    for i in range(NF):
                        o = bank[2 * (i // FC) + u % 2][:, (i % FC) * P:(i % FC + 1) * P]
                        w = ds(e * (2 * FF) + (W_GU + i * P), P)
                        xa, xb = xdt[:, u % 2, 0:P], xdt[:, u % 2, P:2 * P]
                        mm(o, wh[:, w], xa, True, False)
                        mm(o, wh[:, w], xb, False, False)
                        last = mm(o, wl[:, w], xa, False, True)
                    last.then_inc(d_gu, 1)
                if not static or 0 <= s < TILES:
                    e = pe.value_load(te_i[0:1, ds(s, 1)], min_val=0, max_val=E - 1)
                    pe.wait_ge(d_lo, s + 1)
                    wait(pe, d_yv, s - 1)
                    o = bank[6 + u % 2][:, 0:D]
                    for i in range(FC):
                        w = ds(e * (FC * D) + (W_DN + i * D), D)
                        hi = hsplit[:, u % 2, i * P:(i + 1) * P]
                        lo = hsplit[:, u % 2, FF + i * P:FF + (i + 1) * P]
                        mm(o, hi, wh[:, w], i == 0, False)
                        mm(o, hi, wl[:, w], False, False)
                        last = mm(o, lo, wh[:, w], False, i == FC - 1)
                    last.then_inc(d_y, 1)

            pe.wait_ge(h_x, B)
            for s in range(-3, 5):
                step_pe(s, s % 4)
            with pe.Fori(1, TILES // 4 - 1) as i:
                for u in range(1, 5):
                    step_pe(4 * i + u, u % 4)
            for s in range(TILES - 3, TILES + 1):
                step_pe(s, s % 4)


def constants():
    p = np.arange(P)
    c32 = np.zeros((P, C_END), np.float32)
    c32[:, C_ID:C_ID + P] = np.eye(P)
    c32[:, C_HM:C_HM + H] = p[:, None] // HD == np.arange(H)
    c32[:, C_HR:C_HR + H] = p[:, None] // KC == np.arange(H) % HC
    c32[:, C_S:C_S + TILES + 1] = np.arange(TILES + 1)
    c32[:, C_S128:C_S128 + TILES + 1] = P * np.arange(TILES + 1)
    c32[:, C_EREG:C_EREG + E] = REG * np.arange(E)
    c32[:, C_I8:C_I8 + E] = np.arange(E)
    c32[:, C_2T:C_2T + NT] = 2 * (p[:, None] + P * np.arange(NT))
    half = NROT // 2
    inv = (1.0 / 10000.0 ** (np.arange(half, dtype=np.float32) * np.float32(2.0) / np.float32(NROT))).astype(np.float32)
    ang = np.arange(S, dtype=np.float32)[:, None] * inv
    trig = np.zeros((S, 4 * half), np.float16)
    for i, f in enumerate((np.cos, np.sin)):
        v = f(ang.astype(np.float64)).astype(np.float32)
        hi = v.astype(np.float16)
        trig[:, 2 * i * half:(2 * i + 1) * half] = hi
        trig[:, (2 * i + 1) * half:(2 * i + 2) * half] = v - hi.astype(np.float32)
    c16 = np.zeros((P, G_END), np.float16)
    c16[:, G_ID:G_ID + P] = np.eye(P)
    c16[:, G_IOTA:G_IOTA + J] = 1 + np.arange(J)
    c16[:, G_TRIG:G_TRIG + S] = trig.reshape(T, P, P).transpose(1, 0, 2).reshape(P, S)
    r = p % half
    comb = np.zeros((P, P))
    for c in range(P):
        kind, f = c // half, c % half
        comb[:, c] = (r == f) * (p // (2 * half) == (kind >= 2)) * (-1 if kind == 2 else 1)
    c16[:, G_COMB:G_COMB + P] = comb
    c16[:, G_TRI:G_TRI + P] = p[:, None] < p
    c16[:, G_ONE:G_ONE + P] = 1
    cbf = np.zeros((P, 2 * P), mybir.dt.np(BF16))
    cbf[:, 0:P] = np.eye(P)
    cbf[:, P:2 * P] = np.where((p[:, None] // J == p // J) & (p[:, None] >= p), 0.0, -1e30)
    pad = np.zeros((P, PAY_W), np.float32)
    pad[:, D] = 2 * B * S + p
    pad[:, D + 1] = -1
    pad[:, D + 2] = 1
    return c32, c16, cbf, pad


def laid_out(i):
    a = {k: np.asarray(v) for k, v in i.items()}
    ctxt = a["ctx_1024"].transpose(2, 0, 1)
    wqkv = a["L0_ffn_Wqkv"]
    qkc = np.concatenate([wqkv[:, :, 0:NROT], wqkv[:, :, D:D + NROT], wqkv[:, :, NROT:D], wqkv[:, :, D + NROT:2 * D]], 2)
    big = np.concatenate([
        qkc.transpose(1, 0, 2).reshape(P, -1),
        a["L1_ffn_gate_up_w"].transpose(2, 0, 1).reshape(P, -1),
        a["L1_ffn_down_w"].reshape(E, D, FC, P).transpose(3, 0, 2, 1).reshape(P, -1),
        a["L1_ffn_shared_gate_up_w"].T, a["L1_ffn_shared_down_w"].T], 1)
    c32, c16, cbf, pad = constants()
    return [
        a["x"], np.broadcast_to(ctxt[:, :, None, :], (P, B, HC, KC)),
        a["mask_SxS2_bk0"].reshape(T, P, KC).transpose(1, 0, 2),
        a["g_xattn"], a["g_ffn"], a["L0_xattn_Wq"].T, a["L0_xattn_Wkv"], a["L0_ffn_Wr"].T,
        wqkv[:, :, 2 * D:].transpose(2, 0, 1), a["L0_ffn_Wo"].transpose(1, 0, 2),
        a["L1_xattn_Wk"].T, a["L1_xattn_Wq"], a["L1_xattn_Wv"].T, a["L1_xattn_Wo"].T,
        a["L1_ffn_ln_gamma"], a["L1_ffn_ln_beta"], a["L1_ffn_router_w"].T, big, c32, c16, cbf, pad]


def kernel(**inputs):
    import concourse.bacc as bacc
    from concourse.bass_utils import run_bass_kernel_spmd

    nc = bacc.Bacc("TRN2", target_bir_lowering=False, num_devices=1)
    arrays, args = {}, []
    for n, v in enumerate(laid_out(inputs)):
        v = np.ascontiguousarray(v)
        arrays[f"in{n}"] = v
        args.append(nc.dram_tensor(f"in{n}", v.shape, mybir.dt.from_np(v.dtype), kind="ExternalInput").ap())
    args.append(nc.dram_tensor("out", (B, S, D), F32, kind="ExternalOutput").ap())
    build(nc, *args)
    return run_bass_kernel_spmd(nc, [arrays], core_ids=[0]).results[0]["out"]
```

```python
from contextlib import ExitStack

import numpy as np
import concourse.bass as bass
from concourse import mybir

F32 = mybir.dt.float32
F16 = mybir.dt.float16
BF16 = mybir.dt.bfloat16
I32 = mybir.dt.int32
U32 = mybir.dt.uint32
ALU = mybir.AluOpType
ACT = mybir.ActivationFunctionType
AX = mybir.AxisListType
ds = bass.ds

P = 128
B, S, D = 4, 512, 128
T = S // P
NT = B * T
KC = 32
E = 8
J = S // E
H = 16
HD = D // H
HC = P // KC
NC = H // HC
NROT = 64
FF = 384
FC = FF // P
NF = 2 * FC
WS = 256.0
REG = B * S + P
TILES = 40
TTAB = TILES + 8
PAY_W = D + 3
LN_EPS = 1e-5
TOPV = -3.0e38
NQ = 2 * D + D + 1

W_QK = 0
W_GU = W_QK + E * 2 * D
W_DN = W_GU + E * 2 * FF
W_SG = W_DN + E * FC * D
W_SD = W_SG + 2 * D
W_END = W_SD + D
CH = 512
CHUNKS = -(-W_END // CH)
NX = E * B // 2
X_EVERY = 3
X_PE = {"project": 0, "turn": 6, "scores": 6.5, "et": 11, "mix": 14}
X_ACT = {"rows": 2, "turn_out": 4.5, "exp": 6, "et_out": 10.5, "high": 15}
X_DVE = {"rotate": 0, "max": 6, "scale": 7, "low": 16}
EARLY = 12
A_EVERY = 3
A_PE = {"xt": 3, "scores": 5, "et": 8, "mix": 10, "xt2": 14, "logits": 16}
A_ACT = {"xt_out": 4, "exp": 7, "et_out": 9, "high": 14, "xt2_out": 15}
A_DVE = {"stats": 0, "norm": 2, "shift": 6, "sum": 8, "add": 11, "norm2": 13, "logits_out": 17}
A_POOL = {"rstd": 1, "rstd2": 12, "low": 15}
WLOAD = 4
WRING = 3 * WLOAD

C_ID, C_HM, C_HR, C_S, C_S128, C_EREG, C_I8, C_P8, C_2T = 0, 128, 144, 160, 208, 256, 264, 272, 280
C_END = C_2T + NT
G_ID, G_IOTA, G_TRIG, G_COMB, G_TRI, G_ONE = 0, 128, 192, 704, 832, 960
G_END = 1088


def skewed(n, every, at):
    return [(stage, i) for _, i, stage in sorted((every * i + slot, i, stage) for stage, slot in at.items() for i in range(n))]


def build(nc, x_in, ctx_in, mask_in, gx_in, gf_in, wq0_in, wkv0_in, wr0_in, wv0_in, wo0_in, wk1_in,
          wq1_in, wv1_in, wo1_in, gamma_in, beta_in, router_in, wbig_in, c32_in, c16_in, cbf_in,
          pad_in, out):
    disp = nc.dram_tensor("dispatched_rows", ((E + 1) * REG, PAY_W), F32).ap()
    ytok = nc.dram_tensor("expert_rows", (2 * B * S + TILES * P + 1, D), F32).ap()
    x_v = x_in.rearrange("b (t p) d -> p (b t) d", p=P)
    out_v = out.rearrange("b (t p) d -> p (b t) d", p=P)
    ytok_v = ytok[0:2 * B * S, :].rearrange("(n p k) d -> p n (k d)", p=P, k=2)

    with ExitStack() as ctx:
        def sb(name, shape, dt=F32):
            return ctx.enter_context(nc.sbuf_tensor(name, shape, dt))

        def sem(name):
            return ctx.enter_context(nc.semaphore(name))

        bank = [ctx.enter_context(nc.psum_tensor(f"bank{i}", [P, 512], F32)) for i in range(8)]

        x = sb("x", [P, NT, D])
        tw = sb("tile_window", [P, TILES // 4 + 1, 8])
        tpack = sb("tile_pack", [P, TILES // 4 + 1])
        te_i = sb("tile_expert_i", [P, TILES // 4 + 1], I32)
        c32 = sb("c32", [P, C_END])
        c16 = sb("c16", [P, G_END], F16)
        cbf = sb("cbf", [P, 2 * P], BF16)
        ident = c32[:, C_ID:C_ID + P]
        ident16 = c16[:, G_ID:G_ID + P]
        identbf = cbf[:, 0:P]
        causal = cbf[:, P:2 * P]
        tg = sb("tanh_gates", [P, 4])
        graw = sb("graw", [P, 4])
        st = sb("bn_raw", [P, NT, 6])
        mv = sb("mean_var", [P, NT, 2])
        ve = sb("var_eps", [P, NT])
        rstd = sb("rstd", [P, NT])
        mhalf = sb("minus_half", [P, NT])
        ctxr = sb("ctx_t", [P, B, HC, KC])
        wq0 = sb("wq0", [P, D])
        wkv0 = sb("wkv0", [P, 2 * D])
        wr0 = sb("wr0", [P, E])
        region_w = sb("region_w", [P, 2 * E * D])
        wv0 = region_w[:, 0:E * D].rearrange("p (e d) -> p e d", d=D)
        wo0 = region_w[:, E * D:2 * E * D].rearrange("p (e d) -> p e d", d=D)
        qk = region_w[:, 0:8 * D].rearrange("p (q h d) -> p q h d", q=4, h=2)
        qkt = region_w[:, E * D:E * D + 8 * P].rearrange("p (q n) -> p q n", q=4)
        wk1 = sb("wk1", [P, D])
        wq1 = sb("wq1", [P, D])
        wv1 = sb("wv1", [P, D])
        wo1 = sb("wo1", [P, D])
        gamma = sb("gamma", [P, D])
        beta = sb("beta", [P, D])
        router = sb("router", [P, E])
        router16 = sb("router16", [P, 2, E], F16)
        mask8 = sb("mask8", [P, T, KC], mybir.dt.uint8)
        maskf = sb("maskf", [P, T, KC])
        maskbf = sb("mask_bias", [P, T, KC], BF16)
        anyk = sb("any_key", [P, T])
        k0t = sb("k0t", [P, B * KC])
        k1t = sb("k1t", [P, B, KC])
        wk0 = sb("wq_k0", [P, B, KC])
        v0 = sb("v0", [KC, B, D])
        vblk = sb("v_blocks", [P, B, H, HD + 1])
        wf = sb("w_scaled", [P, WRING * CH])
        wh = sb("w_high", [P, CHUNKS * CH], F16)
        wl = sb("w_low", [P, CHUNKS * CH], F16)
        vwh = sb("vwo_high", [P, E, D + 1], F16)
        vwl = sb("vwo_low", [P, E, D + 1], F16)
        xh = sb("x_hat", [P, NT, D])
        region_t = sb("region_t", [P, NT * PAY_W])
        xt = region_t[:, 0:B * S].rearrange("p (b s) -> p b s", b=B)
        tab = region_t[:, 0:E * 2 * D].rearrange("p (e h d) -> p e h d", e=E, h=2)
        pay = region_t[:, :].rearrange("p (n w) -> p n w", w=PAY_W)
        es = sb("cross_sub", [P, B, T, KC])
        nm = sb("neg_max", [P, B, T])
        zs = sb("z_sum", [P, B, T])
        rz = sb("r_z", [P, B, T])
        et0 = sb("cross_e_t", [KC, B, S])
        region_s = sb("region_s", [P, 2 * NT * D], F16)
        xs = region_s[:, :].rearrange("p (h n d) -> p h n d", h=2, n=NT)
        yh = region_s[:, 0:E // 2 * B * D].rearrange("p (g b d) -> p g b d", g=E // 2, b=B)
        yl = region_s[:, E // 2 * B * D:E * B * D].rearrange("p (g b d) -> p g b d", g=E // 2, b=B)
        lg = sb("logits0", [P, T, B, E])
        region_k = sb("region_k", [P, 4, S])
        work, ones32, sel, scan = (region_k[0:B * E, i, :] for i in range(4))
        esl, etl = (region_k[:, i, :].rearrange("p (q n) -> p q n", q=4) for i in (1, 2))
        vv = xh
        rpa = region_k[:, 0, 0:4 * D].rearrange("p (q h d) -> p q h d", q=4, h=2)
        top8 = sb("top8", [B * E, 8])
        pos = sb("slot_of_token", [P, T, B, E])
        region_p = sb("region_p", [P, NT * E * J // 2])
        pick = region_p[:, :].bitcast(F16).rearrange("p (n c) -> p n c", n=NT)
        a1 = region_p[:, 0:B * H * KC].rearrange("p (b c) -> p b c", b=B)
        ntt = region_p[:, B * H * KC:2 * B * H * KC].bitcast(F16).rearrange("p (h n) -> p h n", h=2)
        region_q = sb("region_q", [P, NT * E * J // 2])
        pickt = region_q[:, :].bitcast(F16).rearrange("p (n g c) -> p n g c", n=NT, g=E // 2)
        vwf = region_q[:, 0:E * (D + 1)].rearrange("p (e d) -> p e d", e=E)
        yk = region_q[:, :].rearrange("p (n w) -> p n w", n=NT)
        region_x = sb("region_x", [P, 2 * E * B * J], F16)
        xg = region_x[:, :].rearrange("p (h e b j) -> p h e b j", h=2, e=E, b=B)
        trg = sb("trig_gathered", [P, E, B, J], F16)
        rpb = sb("rope_b", [P, 4, 2, NROT])
        lsl = sb("exp_neg_logit", [P, 4])
        nms = sb("slot_neg_max", [P, 4])
        zsl = sb("slot_z", [P, 4])
        den = sb("slot_den", [P, 4])
        rzs = sb("slot_rz", [P, 4])

        kbl = region_p[:, B * H * KC:2 * B * H * KC].rearrange("p (b c) -> p b c", b=B)
        vrep = es[:, :, :, :].rearrange("p b t k -> p b (t k)")
        e1 = region_k[:, 0:2, :]
        e1t = region_k[:, 2:4, :]
        xf = region_x[:, :].bitcast(F32)
        xtc = xf[:, 0:2 * P].rearrange("p (r n) -> p r n", r=2)
        on = xf[:, 2 * P:4 * P].rearrange("p (r n) -> p r n", r=2)
        ont = xf[:, 4 * P:6 * P].rearrange("p (r n) -> p r n", r=2)
        nm1 = sb("nm1", [P, 2, H])
        zi = sb("z_inv", [P, 2, H])
        tgw = sb("tanh_gate_ws", [P, 1])
        rmax = sb("r_max", [P, T])
        prob = sb("r_prob", [P, T, E])
        rsum = sb("r_sum", [P, T])
        rtop = sb("r_top", [P, T, 8])
        ridx = sb("r_idx", [P, T, 8], U32)
        gexp = sb("gate_exp", [P, T])
        gden = sb("gate_den", [P, T])
        gate = sb("gates", [P, NT, 2])
        ef = sb("expert_of", [P, T, 2])
        oh = sb("one_hot", [P, T, 2, E])
        msel = sb("routed", [P, NT, E], F16)
        rk = sb("rank_row", [P, T, E])
        ohr = sb("one_hot_row", [P, T, 2, E])
        slotf = sb("slot_f", [P, T, 2])
        slot = sb("slot", [P, NT, 2], I32)
        tsum = sb("tile_sum", [P, E])
        base = sb("routed_before", [P, B + 1, E], F16)
        cnt = sb("count", [P, E])
        cnti = sb("count_i", [P, E], I32)
        ntil = sb("tiles_of", [P, E])
        ncum = sb("tiles_upto", [P, E])
        ge, gn = (xf[:, i * TTAB * E:(i + 1) * TTAB * E].rearrange("p (s e) -> p s e", e=E) for i in (2, 3))
        te = sb("tile_expert", [P, TTAB])
        tb = sb("tiles_before", [P, TTAB])
        trow = sb("tile_row", [P, TTAB])
        trow_i = sb("tile_row_i", [P, TTAB], I32)
        padr = sb("pad_row_i", [P, E], I32)
        onee = sb("ones_e", [P, E])
        padt = sb("pad_rows", [P, PAY_W])
        hs = region_w[:, 0:4 * CH].rearrange("p (r n) -> p r n", r=4)
        hsp = region_k[:, 0:2, :].bitcast(F16)
        xd = sb("slot_rows", [P, 4, PAY_W])
        dbase = sb("slot_dest_base", [P, 1])
        dall = sb("slot_dest_of", [P, TILES])
        dst = sb("slot_dest", [P, 4], I32)
        xdt = sb("slot_rows_t", [P, 2, 2 * P], F16)
        sil = region_w[:, 0:2 * FF].rearrange("p (r n) -> p r n", r=2)
        hid = region_w[:, 2 * FF:4 * FF].rearrange("p (r n) -> p r n", r=2)
        hsplit = region_k[:, 0:2, 0:FF].bitcast(F16)
        yv = region_k[:, 2, :].rearrange("p (r n) -> p r n", r=4)

        ld_x = [sem(f"ld_x{b}") for b in range(B)]
        ld_ctx = sem("ld_ctx")
        ld_id = sem("ld_id")
        ld_g = sem("ld_g")
        ld_c = sem("ld_c")
        ld_v = sem("ld_v")
        ld_m = sem("ld_m")
        ld_w = [sem(f"ld_w{i}") for i in range(-(-CHUNKS // WLOAD))]
        stored = sem("stored")
        v_link = sem("v_link")
        g_link = sem("g_link")
        a_link = sem("a_link")
        k_ps = sem("k_ps"); k_sb = sem("k_sb"); v0_sb = sem("v0_sb"); wk_ps = sem("wk_ps"); wk_sb = sem("wk_sb")
        tg_done = sem("tg_done")
        a_mv = sem("a_mv"); a_rs = sem("a_rs"); a_xh = sem("a_xh"); a_xt = sem("a_xt"); a_xte = sem("a_xte")
        a_s = sem("a_s"); a_sub = sem("a_sub"); a_e = sem("a_e"); a_et = sem("a_et"); a_ete = sem("a_ete")
        a_o = sem("a_o"); b_mv = sem("b_mv"); b_rs = sem("b_rs"); b_xh = sem("b_xh"); b_xt = sem("b_xt")
        b_xte = sem("b_xte"); b_hi = sem("b_hi"); b_lo = sem("b_lo"); b_l = sem("b_l"); b_le = sem("b_le")
        w_hi = sem("w_hi"); w_lo = sem("w_lo")
        vw_ps = sem("vw_ps"); vw_act = sem("vw_act"); vw_sb = sem("vw_sb")
        l_t = sem("l_t"); p_sb = sem("p_sb"); p_t = sem("p_t")
        pk = sem("pk"); g_ps = sem("g_ps"); g_ev = sem("g_ev"); g_evt = sem("g_evt"); pt_ps = sem("pt_ps"); pt_sb = sem("pt_sb")
        tb_ps = sem("tb_ps"); tb_sb = sem("tb_sb")

        q_ps = sem("q_ps"); q_rope = sem("q_rope"); q_add = sem("q_add"); q_cp = sem("q_cp")
        t_ps = sem("t_ps"); t_sb = sem("t_sb"); s_ps = sem("s_ps"); s_max = sem("s_max"); s_exp = sem("s_exp")
        s_scl = sem("s_scl"); et_ps = sem("et_ps"); et_sb = sem("et_sb")
        y_ps = sem("y_ps"); y_hi = sem("y_hi"); y_lo = sem("y_lo")
        k1_ps = sem("k1_ps"); k1_sb = sem("k1_sb"); v1_sb = sem("v1_sb"); vb_sb = sem("vb_sb"); kb_sb = sem("kb_sb")
        a1_ps = sem("a1_ps"); a1_sb = sem("a1_sb"); m_sb = sem("m_sb")
        c_o = sem("c_o"); c_mv = sem("c_mv"); c_rs = sem("c_rs"); c_xh = sem("c_xh"); c_xt = sem("c_xt")
        c_xte = sem("c_xte"); c_s = sem("c_s"); c_sub = sem("c_sub"); c_e = sem("c_e"); c_et = sem("c_et")
        c_ete = sem("c_ete"); c_pv = sem("c_pv"); c_on = sem("c_on"); c_ot = sem("c_ot"); c_ont = sem("c_ont")
        c_w = sem("c_w"); c_x = sem("c_x")
        n_mv = sem("n_mv"); n_rs = sem("n_rs"); n_aff = sem("n_aff"); n_hi = sem("n_hi")
        n_lo = sem("n_lo"); n_t = sem("n_t"); n_th = sem("n_th"); n_tl = sem("n_tl"); r_l = sem("r_l")
        r_sub = sem("r_sub"); r_exp = sem("r_exp"); r_d = sem("r_d"); r_ge = sem("r_ge"); r_m = sem("r_m")
        r_rk = sem("r_rk"); r_slot = sem("r_slot"); sent = sem("sent"); r16 = sem("r16")
        cn_ps = sem("cn_ps"); tiles = sem("tiles"); padded = sem("padded")
        h_ps = sem("h_ps"); h_si = sem("h_si"); h_h = sem("h_h"); h_hi = sem("h_hi"); h_lo = sem("h_lo")
        h_y = sem("h_y"); h_x = sem("h_x")
        d_ld = [sem(f"d_ld{r}") for r in range(4)]
        d_dst = sem("d_dst"); d_base = sem("d_base"); d_xt = sem("d_xt"); d_xe = sem("d_xe"); d_gu = sem("d_gu"); d_si = sem("d_si")
        d_h = sem("d_h"); d_hi = sem("d_hi"); d_lo = sem("d_lo"); d_y = sem("d_y"); d_yv = sem("d_yv")
        d_out = [sem(f"d_out{r}") for r in range(4)]
        ld_y = [sem(f"ld_y{b}") for b in range(B)]
        f_x = sem("f_x")

        def wait(eng, s, v):
            if not isinstance(v, int) or v > 0:
                eng.wait_ge(s, v)

        block = ctx.enter_context(nc.Block())

        @block.sync
        def _(eng):
            eng.dma_start(x[:, 0:T, :], x_v[:, 0:T, :]).then_inc(ld_x[0], 16)
            eng.dma_start(ctxr[:, :, :, :], ctx_in).then_inc(ld_ctx, 16)
            eng.dma_start(wkv0[:, :], wkv0_in).then_inc(ld_ctx, 16)
            eng.dma_start(wq0[:, :], wq0_in).then_inc(ld_ctx, 16)
            for b in range(1, B):
                eng.dma_start(x[:, b * T:(b + 1) * T, :], x_v[:, b * T:(b + 1) * T, :]).then_inc(ld_x[b], 16)
            eng.dma_start(graw[:, 0:2], gx_in.rearrange("(a n) -> a n", a=1).partition_broadcast(P)).then_inc(ld_g, 16)
            eng.dma_start(graw[:, 2:4], gf_in.rearrange("(a n) -> a n", a=1).partition_broadcast(P)).then_inc(ld_g, 16)
            eng.dma_start(wr0[:, :], wr0_in).then_inc(ld_g, 16)
            eng.dma_start(wv0, wv0_in).then_inc(ld_v, 16)
            eng.dma_start(wo0, wo0_in).then_inc(ld_v, 16)
            eng.dma_start(c16[:, :], c16_in).then_inc(ld_c, 16)
            eng.dma_start(cbf[:, :], cbf_in).then_inc(ld_c, 16)
            eng.dma_start(wk1[:, :], wk1_in).then_inc(ld_m, 16)
            eng.dma_start(wq1[:, :], wq1_in).then_inc(ld_m, 16)
            eng.dma_start(wv1[:, :], wv1_in).then_inc(ld_m, 16)
            eng.dma_start(wo1[:, :], wo1_in).then_inc(ld_m, 16)
            eng.dma_start(gamma[:, :], gamma_in.rearrange("(a n) -> a n", a=1).partition_broadcast(P)).then_inc(ld_m, 16)
            eng.dma_start(beta[:, :], beta_in.rearrange("(a n) -> a n", a=1).partition_broadcast(P)).then_inc(ld_m, 16)
            eng.dma_start(router[:, :], router_in).then_inc(ld_m, 16)
            eng.dma_start(mask8[:, :, :], mask_in).then_inc(ld_m, 16)
            for i in range(len(ld_w)):
                lo, hi = i * WLOAD * CH, min((i + 1) * WLOAD * CH, W_END)
                at = lo % (WRING * CH)
                if i >= WRING // WLOAD:
                    eng.wait_ge(w_lo, (i + 1) * WLOAD - WRING)
                eng.dma_start(wf[:, at:at + hi - lo], wbig_in[:, lo:hi]).then_inc(ld_w[i], 16)
            eng.dma_start(padt[:, :], pad_in).then_inc(padded, 16)
            eng.wait_ge(padded, 16)
            eng.dma_start(disp[E * REG:E * REG + P, :], padt[:, :]).then_inc(padded, 16)
            eng.wait_ge(tiles, 1)
            for e in range(E):
                row = eng.value_load(padr[0:1, e:e + 1], min_val=0, max_val=E * REG)
                eng.dma_start(disp[ds(row, P), :], padt[:, :]).then_inc(padded, 16)
            eng.wait_ge(padded, 16 * (E + 2))
            eng.wait_ge(sent, 16 * 2 * NT)

            def load_slots(s, r):
                wait(eng, d_xt, s - 3)
                wait(eng, d_dst, s - 3)
                row = eng.value_load(trow_i[0:1, ds(s, 1)], min_val=0, max_val=E * REG)
                eng.dma_start(xd[:, r, :], disp[ds(row, P), :]).then_inc(d_ld[r], 16)

            for r in range(4):
                load_slots(r, r)
            with eng.Fori(1, TILES // 4) as i:
                for r in range(4):
                    load_slots(4 * i + r, r)
            for r in range(4):
                eng.wait_ge(d_out[r], 16 * (TILES // 4))
            for b in range(B):
                eng.dma_start(yk[:, b * T:(b + 1) * T, :], ytok_v[:, b * T:(b + 1) * T, :]).then_inc(ld_y[b], 16)
            for b in range(B):
                eng.wait_ge(f_x, b + 1)
                eng.dma_start(out_v[:, b * T:(b + 1) * T, :], x[:, b * T:(b + 1) * T, :]).then_inc(stored, 16)
            eng.wait_ge(stored, 16 * B)

        @block.scalar
        def _(act):
            act.dma_start(c32[:, :], c32_in).then_inc(ld_id, 16)
            nc.scalar.preload_act_table(ACT.Exp)

            act.wait_ge(k_ps, 1)
            act.activation(k0t[:, :], bank[7][:, 0:B * KC], ACT.Copy).then_inc(k_sb, 1)
            act.wait_ge(wk_ps, 1)
            act.activation(wk0[:, :, :].rearrange("p b k -> p (b k)"), bank[7][:, P:P + B * KC], ACT.Copy).then_inc(wk_sb, 1)
            act.activation(v0[:, :, :].rearrange("p b k -> p (b k)"), bank[6][0:KC, :], ACT.Copy).then_inc(v0_sb, 1)
            act.wait_ge(ld_g, 48)
            act.activation(tg[:, :], graw[:, :], ACT.Tanh).then_inc(tg_done, 1)

            def split_high(i):
                if i % WLOAD == 0:
                    act.wait_ge(ld_w[i // WLOAD], 16)
                n = min(CH, W_END - i * CH)
                r = slice(i % WRING * CH, i % WRING * CH + n)
                act.activation(wf[:, r], wf[:, r], ACT.Copy, scale=WS).then_inc(a_link, 1)
                act.wait_ge(a_link, i + 1)
                act.activation(wh[:, i * CH:i * CH + n], wf[:, r], ACT.Copy).then_inc(w_hi, 1)

            for stage, b in skewed(B, A_EVERY, A_ACT):
                if stage == "xt_out":
                    act.wait_ge(a_xt, b + 1)
                    act.activation(xt[:, b, :], bank[b % 2][:, :], ACT.Copy).then_inc(a_xte, 1)
                elif stage == "exp":
                    act.wait_ge(a_sub, b + 1)
                    act.activation(es[:, b, :, :], es[:, b, :, :], ACT.Exp, scale=D ** -0.5).then_inc(a_e, 1)
                elif stage == "et_out":
                    act.wait_ge(a_et, b + 1)
                    act.activation(et0[:, b, :], bank[3][0:KC, :], ACT.Copy).then_inc(a_ete, 1)
                elif stage == "high":
                    act.wait_ge(b_xh, b + 1)
                    act.activation(xs[:, 0, b * T:(b + 1) * T, :], xh[:, b * T:(b + 1) * T, :], ACT.Copy).then_inc(b_hi, 1)
                elif stage == "xt2_out":
                    act.wait_ge(b_xt, b + 1)
                    act.activation(xt[:, b, :], bank[b % 2][:, :], ACT.Copy).then_inc(b_xte, 1)
            for h in range(2):
                act.wait_ge(vw_ps, h + 1)
                act.activation(vwf[:, 4 * h:4 * h + 4, 0:D], bank[4 + h][:, :].rearrange("p (e d) -> p e d", d=D),
                               ACT.Copy, scale=WS).then_inc(vw_act, 1)
            act.activation(vwf[:, :, D], wr0[:, :], ACT.Copy, scale=WS).then_inc(vw_act, 1)
            act.wait_ge(vw_act, 3)
            act.activation(vwh[:, :, :], vwf[:, :, :], ACT.Copy).then_inc(vw_act, 1)
            act.wait_ge(k1_ps, 1)
            act.activation(k1t[:, :, :].rearrange("p b k -> p (b k)"), bank[2][:, 0:B * KC], ACT.Copy).then_inc(k1_sb, 1)
            act.activation(vrep[:, :, :].rearrange("p b k -> p (b k)"), bank[3][:, :], ACT.Copy).then_inc(v1_sb, 1)
            for i in range(EARLY):
                split_high(i)
            act.wait_ge(vw_sb, 1)
            for b in range(B):
                for t in range(T):
                    act.wait_ge(pt_ps, b * T + t + 1)
                    act.activation(pickt[:, b * T + t, :, :], bank[6 + t % 2][:, :].rearrange("p (g n) -> p g n", n=P),
                                   ACT.Copy).then_inc(pt_sb, 1)
                act.wait_ge(g_ps, b + 1)
                g = 3 * (b % 2)
                for h in range(2):
                    act.activation(xg[:, h, :, b, :], bank[g + h][:, :].rearrange("p (e j) -> p e j", j=J),
                                   ACT.Copy).then_inc(g_ev, 1)
            for stage, n in skewed(NX, X_EVERY, X_ACT):
                q = n % 4
                if stage == "rows":
                    act.wait_ge(q_rope, n + 1)
                    wait(act, t_ps, n - 3)
                    wait(act, y_ps, n - 3)
                    act.activation(qk[:, q, :, NROT:D], bank[n % 2][:, D:2 * D].rearrange("p (h d) -> p h d", h=2),
                                   ACT.Copy, scale=1.0 / WS)
                    act.activation(vv[:, q, :], bank[n % 2][:, 2 * D:3 * D], ACT.Copy, scale=1.0 / WS)
                    act.activation(lsl[:, q:q + 1], bank[n % 2][:, 3 * D:3 * D + 1], ACT.Exp, scale=-1.0 / WS).then_inc(q_cp, 1)
                elif stage == "turn_out":
                    act.wait_ge(t_ps, n + 1)
                    wait(act, s_ps, n - 3)
                    act.activation(qkt[:, q, :], bank[2 + n % 2][:, 0:2 * P], ACT.Copy, scale=D ** -0.25).then_inc(t_sb, 1)
                elif stage == "exp":
                    act.wait_ge(s_max, n + 1)
                    wait(act, et_ps, n - 3)
                    act.activation(esl[:, q, :], bank[4 + n % 2][:, 0:P], ACT.Exp, bias=nms[:, q:q + 1],
                                   accum_out=zsl[:, q:q + 1]).then_inc(s_exp, 1)
                elif stage == "et_out":
                    act.wait_ge(et_ps, n + 1)
                    wait(act, y_ps, n - 3)
                    act.activation(etl[:, q, :], bank[4 + n % 2][:, P:2 * P], ACT.Copy).then_inc(et_sb, 1)
                elif stage == "high" and q == 3:
                    g = n // 4
                    act.wait_ge(y_ps, n + 1)
                    act.activation(yh[:, g, :, :].rearrange("p b d -> p (b d)"), bank[6 + g % 2][:, :], ACT.Copy).then_inc(y_hi, 1)
            for b in range(B):
                act.wait_ge(a1_ps, b + 1)
                act.activation(a1[:, b, :], bank[4 + b % 2][:, :], ACT.Copy).then_inc(a1_sb, 1)

            for k in range(NT + 12):
                for i in range(EARLY + 2 * k, min(EARLY + 2 * k + 2, CHUNKS)):
                    split_high(i)
                if 0 <= k - 5 < NT:
                    t = k - 5
                    act.wait_ge(c_ot, t + 1)
                    wait(act, c_w, t - 1)
                    act.activation(ont[:, t % 2, :], bank[4][:, 0:P], ACT.Copy).then_inc(c_ont, 1)
                if 0 <= k - 3 < NT:
                    t = k - 3
                    act.wait_ge(c_et, t + 1)
                    wait(act, c_pv, t - 1)
                    act.activation(e1t[:, t % 2, :], bank[2][:, :], ACT.Copy).then_inc(c_ete, 1)
                if 0 <= k - 2 < NT:
                    t = k - 2
                    act.wait_ge(c_sub, t + 1)
                    act.activation(e1[:, t % 2, :], e1[:, t % 2, :], ACT.Exp, scale=HD ** -0.5).then_inc(c_e, 1)
                if 0 <= k < NT:
                    t = k
                    act.wait_ge(c_xt, t + 1)
                    wait(act, c_s, t - 1)
                    act.activation(xtc[:, t % 2, :], bank[0][:, 0:P], ACT.Copy).then_inc(c_xte, 1)
                b, r = divmod(k, 4)
                if r == 3 and 0 <= b - 2 < B:
                    b -= 2
                    act.wait_ge(n_aff, b + 1)
                    act.activation(pay[:, b * T:(b + 1) * T, 0:D // 2].bitcast(F16), xh[:, b * T:(b + 1) * T, :],
                                   ACT.Copy).then_inc(n_hi, 1)
                elif r == 0 and 0 <= b - 3 < B:
                    b -= 3
                    act.wait_ge(n_t, 2 * b + 1)
                    act.activation(ntt[:, 0, b * S:(b + 1) * S], bank[6][:, :], ACT.Copy).then_inc(n_th, 1)
                elif r == 1 and 0 <= b - 3 < B:
                    b -= 3
                    act.wait_ge(r_sub, b + 1)
                    act.activation(prob[:, :, :], prob[:, :, :], ACT.Exp, scale=1.0 / WS).then_inc(r_exp, 1)
                    act.wait_ge(r_d, b + 1)
                    act.activation(gexp[:, :], gexp[:, :], ACT.Exp).then_inc(r_ge, 1)

            nc.scalar.preload_act_table(ACT.Silu)
            for b in range(B + 1):
                if b >= 1:
                    act.wait_ge(h_h, b)
                    act.activation(hsp[:, (b - 1) % 2, 0:S], hs[:, 2 + (b - 1) % 2, :], ACT.Copy).then_inc(h_hi, 1)
                if b < B:
                    act.wait_ge(h_ps, 2 * b + 1)
                    wait(act, h_h, b - 1)
                    act.activation(hs[:, b % 2, :], bank[2 * (b % 2)][:, :], ACT.Silu, scale=1.0 / WS).then_inc(h_si, 1)

            def step_act(s, u):
                static = isinstance(s, int)
                if not static or 0 <= s + 1 < TILES:
                    act.wait_ge(d_h, s + 2)
                    wait(act, d_y, s)
                    act.activation(hsplit[:, (u + 1) % 2, 0:FF], hid[:, (u + 1) % 2, :], ACT.Copy).then_inc(d_hi, 1)
                if not static or 0 <= s + 3 < TILES:
                    act.wait_ge(d_xt, s + 4)
                    wait(act, d_gu, s + 2)
                    act.activation(xdt[:, (u + 3) % 2, :], bank[4 + (u + 3) % 2][:, 0:2 * P], ACT.Copy).then_inc(d_xe, 1)
                if not static or 0 <= s + 2 < TILES:
                    act.wait_ge(d_gu, s + 3)
                    wait(act, d_h, s + 1)
                    act.activation(sil[:, u % 2, :], bank[u % 2][:, 0:FF], ACT.Silu, scale=1.0 / WS).then_inc(d_si, 1)

            for s in range(-3, 5):
                step_act(s, s % 4)
            with act.Fori(1, TILES // 4 - 1) as i:
                for u in range(1, 5):
                    step_act(4 * i + u, u % 4)
            for s in range(TILES - 3, TILES + 1):
                step_act(s, s % 4)

        @block.gpsimd
        def _(pool):
            links = [0]

            def link(ins):
                links[0] += 1
                ins.then_inc(g_link, 1)
                pool.wait_ge(g_link, links[0])

            def bcp(ap, n):
                p, a = ap.shape
                return ap.rearrange("p (a o) -> p a o", o=1).to_broadcast((p, a, n))

            link(pool.memset(mhalf[:, :], -0.5))

            def rstd_of(b, ready, done):
                n = slice(b * T, (b + 1) * T)
                pool.wait_ge(ready, b + 1)
                link(pool.tensor_scalar(ve[:, n], mv[:, n, 1], LN_EPS, 1.0, ALU.add, ALU.mult))
                pool.tensor_tensor(rstd[:, n], ve[:, n], mhalf[:, n], ALU.pow).then_inc(done, 1)

            def split_low(i):
                pool.wait_ge(w_hi, i + 1)
                n = min(CH, W_END - i * CH)
                r = slice(i % WRING * CH, i % WRING * CH + n)
                c = slice(i * CH, i * CH + n)
                pool.tensor_tensor(wl[:, c], wf[:, r], wh[:, c], ALU.subtract).then_inc(w_lo, 1)

            for stage, b in skewed(B, A_EVERY, A_POOL):
                n = slice(b * T, (b + 1) * T)
                if stage == "rstd":
                    rstd_of(b, a_mv, a_rs)
                elif stage == "rstd2":
                    rstd_of(b, b_mv, b_rs)
                elif stage == "low":
                    pool.wait_ge(b_hi, b + 1)
                    pool.tensor_tensor(xs[:, 1, n, :], xh[:, n, :], xs[:, 0, n, :], ALU.subtract).then_inc(b_lo, 1)
            pool.wait_ge(ld_m, 128)
            link(pool.tensor_copy(maskf[:, :, :], mask8[:, :, :]))
            pool.tensor_scalar(maskbf[:, :, :], maskf[:, :, :], -1.0, 1e9, ALU.add, ALU.mult).then_inc(m_sb, 1)
            pool.wait_ge(vw_act, 4)
            pool.tensor_tensor(vwl[:, :, :], vwf[:, :, :], vwh[:, :, :], ALU.subtract).then_inc(vw_sb, 1)
            for i in range(EARLY):
                split_low(i)
            pool.wait_ge(v1_sb, 1)
            for b in range(B):
                pool.tensor_tensor(vblk[:, b, :, 0:HD], vrep[:, b, :].rearrange("p (h d) -> p h d", d=HD),
                                   bcp(c32[:, C_HR:C_HR + H], HD), ALU.mult)
                pool.tensor_copy(vblk[:, b, :, HD], c32[:, C_HR:C_HR + H]).then_inc(vb_sb, 1)
            for n in range(NX):
                q = n % 4
                pool.wait_ge(q_rope, n + 1)
                wait(pool, t_ps, n - 3)
                pool.tensor_tensor(qk[:, q, :, 0:NROT], rpa[:, q, :, :], rpb[:, q, :, :], ALU.add).then_inc(q_add, 1)
            pool.wait_ge(g_ps, B)
            pool.wait_ge(pt_ps, NT)
            pool.wait_ge(k1_sb, 1)
            for b in range(B):
                pool.tensor_tensor(kbl[:, b, :].rearrange("p (h k) -> p h k", k=KC),
                                   k1t[:, b, :].rearrange("p (a k) -> p a k", a=1).to_broadcast((P, H, KC)),
                                   bcp(c32[:, C_HM:C_HM + H], KC), ALU.mult).then_inc(kb_sb, 1)

            for b in range(B):
                rstd_of(b, c_mv, c_rs)
            for i in range(EARLY, CHUNKS):
                split_low(i)
            def send_rows(b, tiles_of_b):
                for t in tiles_of_b:
                    for c in range(2):
                        pool.indirect_dma_start(disp, bass.IndirectOffsetOnAxis(slot[:, b * T + t, c:c + 1].bitcast(U32), 0),
                                                pay[:, b * T + t, :], None).then_inc(sent, 16)

            for b in range(B + 2):
                if b >= 2:
                    pool.wait_ge(r_slot, b - 1)
                    pool.wait_ge(n_hi, b - 1)
                    pool.wait_ge(n_lo, b - 1)
                    send_rows(b - 2, range(T // 2))
                if b < B:
                    rstd_of(b, n_mv, n_rs)
                if b >= 2:
                    send_rows(b - 2, range(T // 2, T))

            due = pool.alloc_register("tiles_due")
            pool.reg_mov(due, 1)
            with pool.Fori(0, TILES // 4):
                for r in range(4):
                    pool.wait_ge(d_yv, due)
                    pool.reg_add(due, due, 1)
                    pool.indirect_dma_start(ytok, bass.IndirectOffsetOnAxis(dst[:, r:r + 1].bitcast(U32), 0),
                                            yv[:, r, :], None).then_inc(d_out[r], 16)

        @block.vector
        def _(dve):
            links = [0]

            def link(ins):
                links[0] += 1
                ins.then_inc(v_link, 1)
                dve.wait_ge(v_link, links[0])

            def norm_stats(b, done):
                for t in range(b * T, (b + 1) * T):
                    last = dve.bn_stats(st[:, t, :], x[:, t, :])
                link(last)
                for t in range(b * T, (b + 1) * T):
                    last = dve.bn_aggr(mv[:, t, :], st[:, t, :])
                last.then_inc(done, 1)

            def normalise(b, done):
                for t in range(b * T, (b + 1) * T):
                    last = dve.tensor_scalar(xh[:, t, :], x[:, t, :], mv[:, t, 0:1], rstd[:, t:t + 1],
                                             ALU.subtract, ALU.mult)
                last.then_inc(done, 1)

            def bc(ap, n):
                p, a = ap.shape
                return ap.rearrange("p (a o) -> p a o", o=1).to_broadcast((p, a, n))

            for stage, b in skewed(B, A_EVERY, A_DVE):
                if stage == "stats":
                    dve.wait_ge(ld_x[b], 16)
                    norm_stats(b, a_mv)
                elif stage == "norm":
                    dve.wait_ge(a_rs, b + 1)
                    dve.wait_ge(a_mv, b + 1)
                    normalise(b, a_xh)
                elif stage == "shift":
                    s3 = bank[2][:, 0:T * KC].rearrange("p (t k) -> p t k", k=KC)
                    dve.wait_ge(a_s, b + 1)
                    link(dve.tensor_reduce(nm[:, b, :], s3, AX.X, ALU.max, negate=True))
                    dve.tensor_tensor(es[:, b, :, :], s3, bc(nm[:, b, :], KC), ALU.add).then_inc(a_sub, 1)
                elif stage == "sum":
                    dve.wait_ge(a_e, b + 1)
                    link(dve.tensor_reduce(zs[:, b, :], es[:, b, :, :], AX.X, ALU.add))
                    link(dve.reciprocal(rz[:, b, :], zs[:, b, :]))
                    if b == 0:
                        dve.wait_ge(tg_done, 1)
                    link(dve.tensor_scalar(rz[:, b, :], rz[:, b, :], tg[:, 0:1], None, ALU.mult))
                elif stage == "add":
                    dve.wait_ge(a_o, b + 1)
                    for t in range(T):
                        last = dve.scalar_tensor_tensor(x[:, b * T + t, :], bank[4 + b % 2][:, t * D:(t + 1) * D],
                                                        rz[:, b, t:t + 1], x[:, b * T + t, :], ALU.mult, ALU.add)
                    link(last)
                    norm_stats(b, b_mv)
                elif stage == "norm2":
                    dve.wait_ge(b_rs, b + 1)
                    dve.wait_ge(b_mv, b + 1)
                    dve.wait_ge(a_xt, b + 1)
                    normalise(b, b_xh)
                elif stage == "logits_out":
                    dve.wait_ge(b_l, b + 1)
                    dve.tensor_copy(lg[:, :, b, :], bank[6][:, 0:T * E].rearrange("p (t e) -> p t e", e=E)).then_inc(b_le, 1)

            dve.memset(ones32, 1.0)
            dve.wait_ge(l_t, 1)
            link(dve.tensor_copy(work, bank[0][0:B * E, :]))
            for _ in range(J // 8):
                link(dve.max(top8[:, :], work))
                link(dve.match_replace(work, top8[:, :], work, TOPV))
            link(dve.tensor_scalar(sel, work, TOPV, None, ALU.is_equal))
            link(dve.tensor_tensor_scan(scan, ones32, sel, 0.0, ALU.mult, ALU.add))
            dve.tensor_tensor(sel, scan, sel, ALU.mult).then_inc(p_sb, 1)
            dve.wait_ge(p_t, 1)
            link(dve.tensor_copy(pos[:, :, :, :].rearrange("p t b e -> p (t b e)"), bank[1][:, 0:P]))
            iota = c16[:, G_IOTA:G_IOTA + J].rearrange("p (a j) -> p a j", a=1).to_broadcast((P, E, J))
            dve.wait_ge(ld_c, 32)
            for b in range(B):
                for t in range(T):
                    dve.tensor_tensor(pick[:, b * T + t, :].rearrange("p (e j) -> p e j", j=J), iota,
                                      bc(pos[:, t, b, :], J), ALU.is_equal).then_inc(pk, 1)
                if b >= 1:
                    dve.wait_ge(g_ps, b)
                    dve.tensor_copy(trg[:, :, b - 1, :], bank[3 * ((b - 1) % 2) + 2][:, :].rearrange("p (e j) -> p e j", j=J)).then_inc(g_evt, 1)
            dve.wait_ge(g_ps, B)
            dve.tensor_copy(trg[:, :, B - 1, :], bank[5][:, :].rearrange("p (e j) -> p e j", j=J)).then_inc(g_evt, 1)
            dve.wait_ge(ld_m, 128)
            dve.wait_ge(m_sb, 1)
            link(dve.tensor_reduce(anyk[:, :], maskf[:, :, :], AX.X, ALU.max))
            for q in range(4):
                dve.wait_ge(tb_ps, q + 1)
                dve.tensor_scalar(tab[:, 2 * q:2 * q + 2, :, :].rearrange("p e h d -> p (e h d)"), bank[q][:, :], 1.0 / WS, None, ALU.mult).then_inc(tb_sb, 1)

            half = NROT // 2
            for stage, n in skewed(NX, X_EVERY, X_DVE):
                q = n % 4
                if stage == "rotate":
                    e, h = n // 2, n % 2
                    src = bank[n % 2][:, 0:D].rearrange("p (h d) -> p h d", h=2)

                    def table(c0, w):
                        return tab[:, e:e + 1, h, c0:c0 + w].to_broadcast((P, 2, w))

                    dve.wait_ge(q_ps, n + 1)
                    wait(dve, q_add, n - 3)
                    dve.tensor_tensor(rpa[:, q, :, :], src, table(0, NROT), ALU.mult)
                    dve.tensor_tensor(rpb[:, q, :, 0:half], src[:, :, half:NROT], table(NROT, half), ALU.mult)
                    dve.tensor_tensor(rpb[:, q, :, half:NROT], src[:, :, 0:half], table(NROT + half, half),
                                      ALU.mult).then_inc(q_rope, 1)
                elif stage == "max":
                    dve.wait_ge(s_ps, n + 1)
                    wait(dve, s_exp, n - 3)
                    dve.tensor_reduce(nms[:, q:q + 1], bank[4 + n % 2][:, 0:P], AX.X, ALU.max, negate=True).then_inc(s_max, 1)
                elif stage == "scale":
                    dve.wait_ge(s_exp, n + 1)
                    dve.wait_ge(q_cp, n + 1)
                    link(dve.scalar_tensor_tensor(den[:, q:q + 1], lsl[:, q:q + 1], 1.0, zsl[:, q:q + 1], ALU.add, ALU.mult))
                    link(dve.reciprocal(rzs[:, q:q + 1], den[:, q:q + 1]))
                    dve.tensor_scalar(esl[:, q, :], esl[:, q, :], rzs[:, q:q + 1], None, ALU.mult).then_inc(s_scl, 1)
                elif stage == "low" and q == 3:
                    g = n // 4
                    dve.wait_ge(y_hi, g + 1)
                    dve.tensor_tensor(yl[:, g, :, :].rearrange("p b d -> p (b d)"), bank[6 + g % 2][:, :],
                                      yh[:, g, :, :].rearrange("p b d -> p (b d)"), ALU.subtract).then_inc(y_lo, 1)

            for b in range(B + 1):
                if b < B:
                    n = slice(b * T, (b + 1) * T)
                    dve.wait_ge(c_o, b + 1)
                    xf32 = x[:, n, :].rearrange("p t d -> p (t d)")
                    link(dve.scalar_tensor_tensor(xf32, bank[b % 2][:, :], tg[:, 2:3], xf32, ALU.mult, ALU.add))
                    norm_stats(b, c_mv)
                if b >= 1:
                    dve.wait_ge(c_rs, b)
                    normalise(b - 1, c_xh)

            dve.memset(base[:, 0, :], 0.0)
            dve.memset(onee[:, :], 1.0)
            link(dve.tensor_scalar(tgw[:, :], tg[:, 3:4], 1.0 / WS, None, ALU.mult))
            dve.tensor_scalar(router16[:, 0, :], router[:, :], WS, None, ALU.mult).then_inc(v_link, 1)
            links[0] += 1
            dve.wait_ge(v_link, links[0])
            dve.scalar_tensor_tensor(router16[:, 1, :], router[:, :], WS, router16[:, 0, :], ALU.mult, ALU.subtract).then_inc(r16, 1)
            dve.tensor_copy(pay[:, :, D], c32[:, C_2T:C_2T + NT])
            dve.memset(pay[:, :, D + 2], 0.0)
            for k in range(NT + 12):
                if 0 <= k - 6 < NT:
                    t = k - 6
                    dve.wait_ge(c_w, t + 1)
                    dve.scalar_tensor_tensor(x[:, t, :], bank[5][:, 0:D], tg[:, 1:2], x[:, t, :], ALU.mult, ALU.add).then_inc(c_x, 1)
                    dve.wait_ge(c_x, t + 1)
                    last = dve.bn_stats(st[:, t, :], x[:, t, :])
                    if t % T == T - 1:
                        link(last)
                        for u in range(t - T + 1, t + 1):
                            last = dve.bn_aggr(mv[:, u, :], st[:, u, :])
                        last.then_inc(n_mv, 1)
                if 0 <= k - 4 < NT:
                    t = k - 4
                    o9 = bank[3][:, 0:H * (HD + 1)].rearrange("p (h d) -> p h d", d=HD + 1)
                    z = zi[:, t % 2, :]
                    dve.wait_ge(c_pv, t + 1)
                    link(dve.reciprocal(z, o9[:, :, HD]))
                    wait(dve, c_ot, t - 1)
                    dve.scalar_tensor_tensor(on[:, t % 2, :].rearrange("p (h d) -> p h d", d=HD), o9[:, :, 0:HD],
                                             anyk[:, t % T:t % T + 1], bc(z, HD), ALU.mult, ALU.mult).then_inc(c_on, 1)
                if 0 <= k - 1 < NT:
                    t = k - 1
                    s3 = bank[1][:, :].rearrange("p (h k) -> p h k", k=KC)
                    dve.wait_ge(c_s, t + 1)
                    link(dve.tensor_reduce(nm1[:, t % 2, :], s3, AX.X, ALU.max, negate=True))
                    wait(dve, c_et, t - 1)
                    dve.tensor_tensor(e1[:, t % 2, :].rearrange("p (h k) -> p h k", k=KC), s3, bc(nm1[:, t % 2, :], KC),
                                      ALU.add).then_inc(c_sub, 1)
                b, r = divmod(k, 4)
                if r == 2 and 0 <= b - 2 < B:
                    b -= 2
                    dve.wait_ge(n_rs, b + 1)
                    dve.wait_ge(n_mv, b + 1)
                    for t in range(b * T, (b + 1) * T):
                        last = dve.scalar_tensor_tensor(xh[:, t, :], x[:, t, :], mv[:, t, 0:1], gamma[:, :],
                                                        ALU.subtract, ALU.mult)
                    link(last)
                    for t in range(b * T, (b + 1) * T):
                        last = dve.scalar_tensor_tensor(xh[:, t, :], xh[:, t, :], rstd[:, t:t + 1], beta[:, :],
                                                        ALU.mult, ALU.add)
                    last.then_inc(n_aff, 1)
                elif r == 3 and 0 <= b - 2 < B:
                    b -= 2
                    n = slice(b * T, (b + 1) * T)
                    dve.wait_ge(n_hi, b + 1)
                    dve.tensor_tensor(pay[:, n, D // 2:D].bitcast(F16), xh[:, n, :], pay[:, n, 0:D // 2].bitcast(F16),
                                      ALU.subtract).then_inc(n_lo, 1)
                elif r == 0 and 0 <= b - 3 < B:
                    b -= 3
                    dve.wait_ge(n_t, 2 * b + 2)
                    dve.tensor_copy(ntt[:, 1, b * S:(b + 1) * S], bank[7][:, :]).then_inc(n_tl, 1)
                elif r == 1 and 0 <= b - 3 < B:
                    b -= 3
                    n = slice(b * T, (b + 1) * T)
                    l3 = bank[6][:, 0:T * E].rearrange("p (t e) -> p t e", e=E)
                    dve.wait_ge(r_l, b + 1)
                    link(dve.tensor_reduce(rmax[:, :], l3, AX.X, ALU.max, negate=True))
                    dve.tensor_tensor(prob[:, :, :], l3, bc(rmax[:, :], E), ALU.add).then_inc(r_sub, 1)
                    dve.wait_ge(r_exp, b + 1)
                    link(dve.tensor_reduce(rsum[:, :], prob[:, :, :], AX.X, ALU.add))
                    link(dve.reciprocal(rsum[:, :], rsum[:, :]))
                    link(dve.tensor_tensor(prob[:, :, :], prob[:, :, :], bc(rsum[:, :], E), ALU.mult))
                    for t in range(T):
                        last = dve.max(rtop[:, t, :], prob[:, t, :])
                    link(last)
                    dve.tensor_tensor(gexp[:, :], rtop[:, :, 1], rtop[:, :, 0], ALU.subtract).then_inc(r_d, 1)
                    for t in range(T):
                        last = dve.max_index(ridx[:, t, :], rtop[:, t, :], prob[:, t, :])
                    link(last)
                    link(dve.tensor_copy(ef[:, :, :], ridx[:, :, 0:2]))
                    link(dve.tensor_tensor(oh[:, :, :, :].rearrange("p t c e -> p (t c) e"),
                                           c32[:, C_I8:C_I8 + E].rearrange("p (a e) -> p a e", a=1).to_broadcast((P, 2 * T, E)),
                                           bc(ef[:, :, :].rearrange("p t c -> p (t c)"), E), ALU.is_equal))
                    link(dve.tensor_tensor(msel[:, n, :], oh[:, :, 0, :], oh[:, :, 1, :], ALU.add))
                    link(dve.tensor_reduce(tsum[:, :], msel[:, n, :].rearrange("p t e -> p e t"), AX.X, ALU.add))
                    dve.tensor_tensor(base[:, b + 1, :], base[:, b, :], tsum[:, :], ALU.add).then_inc(r_m, 1)
                    dve.wait_ge(r_ge, b + 1)
                    link(dve.tensor_scalar(gden[:, :], gexp[:, :], 1.0, None, ALU.add))
                    link(dve.reciprocal(gden[:, :], gden[:, :]))
                    dve.tensor_scalar(gate[:, n, 0], gden[:, :], tg[:, 3:4], None, ALU.mult)
                    dve.scalar_tensor_tensor(gate[:, n, 1], gexp[:, :], tg[:, 3:4], gden[:, :], ALU.mult, ALU.mult)
                    dve.tensor_copy(pay[:, n, D + 1], ef[:, :, 0])
                b, r = divmod(k, 4)
                if r == 3 and 0 <= b - 3 < B:
                    b -= 3
                    n = slice(b * T, (b + 1) * T)
                    dve.wait_ge(r_rk, b + 1)
                    link(dve.tensor_tensor(rk[:, :, :], bank[7][:, 0:T * E].rearrange("p (t e) -> p t e", e=E),
                                           c32[:, C_EREG:C_EREG + E].rearrange("p (a e) -> p a e", a=1).to_broadcast((P, T, E)),
                                           ALU.add))
                    for c in range(2):
                        last = dve.tensor_tensor(ohr[:, :, c, :], oh[:, :, c, :], rk[:, :, :], ALU.mult)
                    link(last)
                    link(dve.tensor_reduce(slotf[:, :, :], ohr[:, :, :, :], AX.X, ALU.add))
                    dve.tensor_copy(slot[:, n, :], slotf[:, :, :]).then_inc(r_slot, 1)

            dve.wait_ge(cn_ps, 1)
            link(dve.tensor_copy(cnt[:, :], bank[6][:, 0:E]))
            link(dve.tensor_scalar(cnti[:, :], cnt[:, :], float(P - 1), None, ALU.add))
            link(dve.tensor_scalar(cnti[:, :], cnti[:, :], 7, None, ALU.logical_shift_right))
            link(dve.tensor_copy(ntil[:, :], cnti[:, :]))
            link(dve.tensor_tensor_scan(ncum[:, :], onee[:, :], ntil[:, :], 0.0, ALU.mult, ALU.add))
            m1 = TTAB

            def over_tiles(v):
                return v.rearrange("p (a e) -> p a e", a=1).to_broadcast((P, m1, E))

            link(dve.tensor_tensor(ge[:, :, :], bc(c32[:, C_S:C_S + m1], E), over_tiles(ncum[:, :]), ALU.is_ge))
            link(dve.tensor_reduce(te[:, :], ge[:, :, :], AX.X, ALU.add))
            link(dve.tensor_tensor(gn[:, :, :], ge[:, :, :], over_tiles(ntil[:, :]), ALU.mult))
            link(dve.tensor_reduce(tb[:, :], gn[:, :, :], AX.X, ALU.add))
            link(dve.scalar_tensor_tensor(trow[:, :], tb[:, :], -float(P), c32[:, C_S128:C_S128 + m1], ALU.mult, ALU.add))
            link(dve.scalar_tensor_tensor(trow[:, :], te[:, :], float(REG), trow[:, :], ALU.mult, ALU.add))
            dve.tensor_scalar(trow_i[:, :], trow[:, :], float(E * REG), None, ALU.min)
            dve.tensor_tensor(padr[:, :], cnt[:, :], c32[:, C_EREG:C_EREG + E], ALU.add).then_inc(tiles, 1)
            w = TILES // 4
            for h in range(2):
                dve.tensor_scalar(tw[:, 0:w, 4 * h:4 * h + 4],
                                  te[:, 1 + 4 * h:1 + 4 * h + TILES].rearrange("p (i j) -> p i j", j=4),
                                  float(E - 1), None, ALU.min)
            link(dve.tensor_scalar(tw[:, w, :], te[:, 0:8], float(E - 1), None, ALU.min))
            link(dve.tensor_tensor(tw[:, :, :], tw[:, :, :],
                                   c32[:, C_P8:C_P8 + 8].rearrange("p (a j) -> p a j", a=1).to_broadcast((P, w + 1, 8)),
                                   ALU.mult))
            link(dve.tensor_reduce(tpack[:, :], tw[:, :, :], AX.X, ALU.add))
            dve.tensor_copy(te_i[:, :], tpack[:, :]).then_inc(tiles, 1)

            for b in range(B + 2):
                if 2 <= b:
                    c = b - 2
                    xf32 = x[:, c * T:(c + 1) * T, :].rearrange("p t d -> p (t d)")
                    dve.wait_ge(h_y, c + 1)
                    dve.scalar_tensor_tensor(xf32, bank[4 + c % 2][:, :], tgw[:, :], xf32, ALU.mult, ALU.add).then_inc(h_x, 1)
                if 1 <= b <= B:
                    c = b - 1
                    dve.wait_ge(h_hi, b)
                    dve.tensor_tensor(hsp[:, c % 2, S:2 * S], hs[:, 2 + c % 2, :], hsp[:, c % 2, 0:S], ALU.subtract).then_inc(h_lo, 1)
                if b < B:
                    dve.wait_ge(h_si, b + 1)
                    dve.wait_ge(h_ps, 2 * b + 2)
                    wait(dve, h_lo, b - 1)
                    dve.scalar_tensor_tensor(hs[:, 2 + b % 2, :], bank[2 * (b % 2) + 1][:, :], 1.0 / WS, hs[:, b % 2, :],
                                             ALU.mult, ALU.mult).then_inc(h_h, 1)

            def step_dve(s, u):
                static = isinstance(s, int)
                if not static or 0 <= s + 3 < TILES:
                    r = (u + 3) % 4
                    dve.wait_ge(d_ld[r], (s + 3 - r) * 4 + 16)
                    wait(dve, d_dst, s + 3)
                    dve.scalar_tensor_tensor(dbase[:, :], xd[:, r, D + 2:D + 3], c32[:, ds(C_S128 + s + 3, 1)],
                                             xd[:, r, D:D + 1], ALU.mult, ALU.add).then_inc(d_base, 1)
                if not static or 0 <= s - 1 < TILES:
                    r = (u - 1) % 4
                    dve.wait_ge(d_y, s)
                    if not static or s - 1 >= 4:
                        dve.wait_ge(d_out[r], (s - 1 - r) * 4)
                    dve.tensor_scalar(yv[:, r, :], bank[6 + r % 2][:, 0:D], 1.0 / WS, None, ALU.mult)
                    dve.wait_ge(d_dst, s)
                    dve.tensor_copy(dst[:, r:r + 1], dall[:, ds(s - 1, 1)]).then_inc(d_yv, 1)
                if not static or 0 <= s + 1 < TILES:
                    dve.wait_ge(d_hi, s + 2)
                    dve.tensor_tensor(hsplit[:, (u + 1) % 2, FF:2 * FF], hid[:, (u + 1) % 2, :],
                                      hsplit[:, (u + 1) % 2, 0:FF], ALU.subtract).then_inc(d_lo, 1)
                if not static or 0 <= s + 3 < TILES:
                    dve.wait_ge(d_base, s + 4)
                    dve.scalar_tensor_tensor(dall[:, ds(s + 3, 1)], xd[:, (u + 3) % 4, D + 1:D + 2], te[:, ds(s + 3, 1)],
                                             dbase[:, :], ALU.not_equal, ALU.add).then_inc(d_dst, 1)
                if not static or 0 <= s + 2 < TILES:
                    dve.wait_ge(d_si, s + 3)
                    dve.scalar_tensor_tensor(hid[:, u % 2, :], bank[2 + u % 2][:, 0:FF], 1.0 / WS, sil[:, u % 2, :],
                                             ALU.mult, ALU.mult).then_inc(d_h, 1)

            for s in range(-3, 5):
                step_dve(s, s % 4)
            with dve.Fori(1, TILES // 4 - 1) as i:
                for u in range(1, 5):
                    step_dve(4 * i + u, u % 4)
            for s in range(TILES - 3, TILES + 1):
                step_dve(s, s % 4)
            for b in range(B):
                dve.wait_ge(ld_y[b], 16)
                for c in range(2):
                    for t in range(b * T, (b + 1) * T):
                        last = dve.scalar_tensor_tensor(x[:, t, :], yk[:, t, c * D:(c + 1) * D], gate[:, t, c:c + 1],
                                                        x[:, t, :], ALU.mult, ALU.add)
                    if c == 0:
                        link(last)
                last.then_inc(f_x, 1)

        @block.tensor
        def _(pe):
            def mm(o, l, r, start=True, stop=True):
                return pe.matmul(o, l, r, start=start, stop=stop)

            pe.wait_ge(ld_ctx, 48)
            ctxt = ctxr[:, :, 0, :]
            mm(bank[7][:, 0:B * KC], wkv0[:, 0:D], ctxt).then_inc(k_ps, 1)
            for b in range(B):
                mm(bank[6][0:KC, b * D:(b + 1) * D], ctxr[:, b, 0, :], wkv0[:, D:2 * D])
            pe.wait_ge(k_sb, 1)
            mm(bank[7][:, P:P + B * KC], wq0[:, :], k0t[:, :]).then_inc(wk_ps, 1)

            for stage, b in skewed(B, A_EVERY, A_PE):
                n0 = b * T
                if stage == "xt":
                    pe.wait_ge(a_xh, b + 1)
                    pe.wait_ge(ld_id, 16)
                    if b >= 2:
                        pe.wait_ge(a_xte, b - 1)
                    for t in range(T):
                        last = pe.transpose(bank[b % 2][:, t * P:(t + 1) * P], xh[:, n0 + t, :], ident)
                    last.then_inc(a_xt, 1)
                elif stage == "scores":
                    pe.wait_ge(a_xte, b + 1)
                    pe.wait_ge(wk_sb, 1)
                    if b >= 1:
                        pe.wait_ge(a_sub, b)
                    for t in range(T):
                        last = mm(bank[2][:, t * KC:(t + 1) * KC], xt[:, b, t * P:(t + 1) * P], wk0[:, b, :])
                    last.then_inc(a_s, 1)
                elif stage == "et":
                    pe.wait_ge(a_e, b + 1)
                    if b >= 1:
                        pe.wait_ge(a_ete, b)
                    for t in range(T):
                        last = pe.transpose(bank[3][0:KC, t * P:(t + 1) * P], es[:, b, t, :], ident)
                    last.then_inc(a_et, 1)
                elif stage == "mix":
                    pe.wait_ge(a_ete, b + 1)
                    pe.wait_ge(v0_sb, 1)
                    if b >= 2:
                        pe.wait_ge(b_mv, b - 1)
                    for t in range(T):
                        last = mm(bank[4 + b % 2][:, t * D:(t + 1) * D], et0[:, b, t * P:(t + 1) * P], v0[:, b, :])
                    last.then_inc(a_o, 1)
                elif stage == "xt2":
                    pe.wait_ge(b_xh, b + 1)
                    pe.wait_ge(a_xte, min(b + 3, B))
                    if b >= 2:
                        pe.wait_ge(b_xte, b - 1)
                    for t in range(T):
                        last = pe.transpose(bank[b % 2][:, t * P:(t + 1) * P], xh[:, n0 + t, :], ident)
                    last.then_inc(b_xt, 1)
                elif stage == "logits":
                    pe.wait_ge(b_xte, b + 1)
                    pe.wait_ge(ld_g, 48)
                    if b >= 1:
                        pe.wait_ge(b_le, b)
                    for t in range(T):
                        last = mm(bank[6][:, t * E:(t + 1) * E], xt[:, b, t * P:(t + 1) * P], wr0[:, :])
                    last.then_inc(b_l, 1)

            pe.wait_ge(b_le, B)
            for t in range(T):
                last = pe.transpose(bank[0][0:B * E, t * P:(t + 1) * P], lg[:, t, :, :].rearrange("p b e -> p (b e)"), ident)
            last.then_inc(l_t, 1)
            pe.wait_ge(ld_v, 32)
            for e in range(E):
                last = mm(bank[4 + e // 4][:, (e % 4) * D:(e % 4 + 1) * D], wv0[:, e, :], wo0[:, e, :])
                if e % 4 == 3:
                    last.then_inc(vw_ps, 1)
            pe.wait_ge(ld_m, 128)
            mm(bank[2][:, 0:B * KC], wk1[:, :], ctxt)
            for b in range(B):
                last = mm(bank[3][:, b * D:(b + 1) * D], ctxr[:, b, :, :].rearrange("p r k -> p (r k)"), wv1[:, :])
            last.then_inc(k1_ps, 1)
            pe.wait_ge(p_sb, 1)
            for t in range(T):
                last = pe.transpose(bank[1][:, t * B * E:(t + 1) * B * E], sel[:, t * P:(t + 1) * P], ident[0:B * E, 0:B * E])
            last.then_inc(p_t, 1)
            pe.wait_ge(ld_c, 32)
            pe.wait_ge(b_lo, B)
            pe.wait_ge(vw_act, 3)
            pe.wait_ge(v1_sb, 1)
            for b in range(B):
                g = 3 * (b % 2)
                for t in range(T):
                    n = b * T + t
                    pe.wait_ge(pk, n + 1)
                    if t == 0 and b >= 2:
                        pe.wait_ge(g_ev, 2 * (b - 1))
                        pe.wait_ge(g_evt, b - 1)
                    for h, lhs in ((0, xs[:, 0, n, :]), (1, xs[:, 1, n, :]), (2, c16[:, G_TRIG + t * D:G_TRIG + (t + 1) * D])):
                        last = mm(bank[g + h][:, :], lhs, pick[:, n, :], start=t == 0, stop=t == T - 1)
                    if t == T - 1:
                        last.then_inc(g_ps, 1)
                    if n >= 2:
                        pe.wait_ge(pt_sb, n - 1)
                    for p in range(E // 2):
                        last = mm(bank[6 + t % 2][:, p * P:(p + 1) * P], pick[:, n, p * P:(p + 1) * P], ident16)
                    last.then_inc(pt_ps, 1)
            pe.wait_ge(g_evt, B)
            pe.wait_ge(g_ev, 2 * B)
            for q in range(4):
                for u in range(4):
                    e, h = 2 * q + u // 2, u % 2
                    last = mm(bank[q][:, u * P:(u + 1) * P], trg[:, e, 2 * h:2 * h + 2, :].rearrange("p b j -> p (b j)"),
                              c16[:, G_COMB:G_COMB + P])
                last.then_inc(tb_ps, 1)

            pe.wait_ge(pt_sb, NT)
            pe.wait_ge(w_lo, 4)
            pe.wait_ge(vw_sb, 1)
            for stage, n in skewed(NX, X_EVERY, X_PE):
                q, e, h = n % 4, n // 2, n % 2
                if stage == "project":
                    if n < 2:
                        pe.wait_ge(tb_sb, 4)
                    wait(pe, q_cp, n - 1)
                    xa, xb = (xg[:, i, e, 2 * h:2 * h + 2, :].rearrange("p b j -> p (b j)") for i in range(2))
                    c = slice(W_QK + 2 * D * e, W_QK + 2 * D * (e + 1))
                    for c0, w, wa, wb in ((0, 2 * D, wh[:, c], wl[:, c]), (2 * D, D + 1, vwh[:, e, :], vwl[:, e, :])):
                        o = bank[n % 2][:, c0:c0 + w]
                        mm(o, xa, wa, True, False)
                        mm(o, xa, wb, False, False)
                        last = mm(o, xb, wa, False, True)
                    last.then_inc(q_ps, 1)
                elif stage == "turn":
                    pe.wait_ge(q_add, n + 1)
                    pe.wait_ge(q_cp, n + 1)
                    wait(pe, t_sb, n - 1)
                    for i in range(2):
                        last = pe.transpose(bank[2 + n % 2][:, i * P:(i + 1) * P], qk[:, q, i, :], ident)
                    last.then_inc(t_ps, 1)
                elif stage == "scores":
                    pe.wait_ge(t_sb, n + 1)
                    wait(pe, et_sb, n - 1)
                    o = bank[4 + n % 2][:, 0:P]
                    mm(o, identbf, causal, True, False)
                    mm(o, qkt[:, q, 0:P], qkt[:, q, P:2 * P], False, True).then_inc(s_ps, 1)
                elif stage == "et":
                    pe.wait_ge(s_scl, n + 1)
                    pe.transpose(bank[4 + n % 2][:, P:2 * P], esl[:, q, :], ident).then_inc(et_ps, 1)
                elif stage == "mix":
                    g = n // 4
                    pe.wait_ge(et_sb, n + 1)
                    if q == 0:
                        wait(pe, y_lo, g - 1)
                    for i in range(2):
                        b = 2 * h + i
                        last = mm(bank[6 + g % 2][J * (e % 2):J * (e % 2 + 1), b * D:(b + 1) * D],
                                  etl[:, q, i * J:(i + 1) * J], vv[:, q, :])
                    last.then_inc(y_ps, 1)

            pe.wait_ge(y_lo, E // 2)
            for b in range(B):
                wait(pe, c_mv, b - 1)
                for t in range(T):
                    o = bank[b % 2][:, t * D:(t + 1) * D]
                    for g in range(E // 2):
                        mm(o, pickt[:, b * T + t, g, :], yh[:, g, b, :], g == 0, False)
                        last = mm(o, pickt[:, b * T + t, g, :], yl[:, g, b, :], False, g == E // 2 - 1)
                last.then_inc(c_o, 1)
                pe.wait_ge(kb_sb, b + 1)
                wait(pe, a1_sb, b - 1)
                mm(bank[4 + b % 2][:, :], wq1[:, :], kbl[:, b, :]).then_inc(a1_ps, 1)

            pe.wait_ge(c_mv, B)
            pe.wait_ge(a1_sb, B)
            pe.wait_ge(m_sb, 1)
            pe.wait_ge(vb_sb, B)
            for k in range(NT + 12):
                if 0 <= k - 6 < NT:
                    t = k - 6
                    pe.wait_ge(c_ont, t + 1)
                    wait(pe, c_x, t)
                    mm(bank[5][:, 0:D], ont[:, t % 2, :], wo1[:, :]).then_inc(c_w, 1)
                if 0 <= k - 5 < NT:
                    t = k - 5
                    pe.wait_ge(c_on, t + 1)
                    wait(pe, c_ont, t)
                    pe.transpose(bank[4][:, 0:P], on[:, t % 2, :], ident).then_inc(c_ot, 1)
                if 0 <= k - 4 < NT:
                    t = k - 4
                    pe.wait_ge(c_ete, t + 1)
                    wait(pe, c_on, t)
                    for c in range(NC):
                        n = HC * (HD + 1)
                        last = mm(bank[3][:, c * n:(c + 1) * n], e1t[:, t % 2, c * P:(c + 1) * P],
                                  vblk[:, t // T, c * HC:(c + 1) * HC, :].rearrange("p h d -> p (h d)"))
                    last.then_inc(c_pv, 1)
                if 0 <= k - 3 < NT:
                    t = k - 3
                    pe.wait_ge(c_e, t + 1)
                    wait(pe, c_ete, t)
                    for c in range(NC):
                        last = pe.transpose(bank[2][:, c * P:(c + 1) * P], e1[:, t % 2, c * P:(c + 1) * P], ident)
                    last.then_inc(c_et, 1)
                if 0 <= k - 1 < NT:
                    t = k - 1
                    pe.wait_ge(c_xte, t + 1)
                    wait(pe, c_sub, t)
                    mm(bank[1][:, :], identbf, maskbf[:, t % T:t % T + 1, :].to_broadcast((P, H, KC)), True, False)
                    mm(bank[1][:, :], xtc[:, t % 2, :], a1[:, t // T, :], False, True).then_inc(c_s, 1)
                if 0 <= k < NT:
                    t = k
                    pe.wait_ge(c_xh, t // T + 1)
                    wait(pe, c_xte, t)
                    pe.transpose(bank[0][:, 0:P], xh[:, t, :], ident).then_inc(c_xt, 1)
                b, r = divmod(k, 4)
                if r == 0 and 0 <= b - 3 < B:
                    b -= 3
                    wait(pe, r_slot, b)
                    wait(pe, r_m, b)
                    for h, s in ((0, n_hi), (1, n_lo)):
                        pe.wait_ge(s, b + 1)
                        for t in range(T):
                            w = pay[:, b * T + t, h * (D // 2):(h + 1) * (D // 2)].bitcast(F16)
                            last = mm(bank[6 + h][:, t * P:(t + 1) * P], w, ident16)
                        last.then_inc(n_t, 1)
                elif r == 1 and 0 <= b - 3 < B:
                    b -= 3
                    pe.wait_ge(n_th, b + 1)
                    pe.wait_ge(n_tl, b + 1)
                    pe.wait_ge(r16, 1)
                    for t in range(T):
                        c = slice(b * S + t * P, b * S + (t + 1) * P)
                        o = bank[6][:, t * E:(t + 1) * E]
                        mm(o, ntt[:, 0, c], router16[:, 0, :], True, False)
                        mm(o, ntt[:, 0, c], router16[:, 1, :], False, False)
                        last = mm(o, ntt[:, 1, c], router16[:, 0, :], False, True)
                    last.then_inc(r_l, 1)
                elif r == 3 and 0 <= b - 3 < B:
                    b -= 3
                    pe.wait_ge(r_m, b + 1)
                    tri, one = c16[:, G_TRI:G_TRI + P], c16[:, G_ONE:G_ONE + P]
                    for t in range(T):
                        o = bank[7][:, t * E:(t + 1) * E]
                        mm(o, tri, msel[:, b * T + t, :], True, False)
                        for u in range(t):
                            mm(o, one, msel[:, b * T + u, :], False, False)
                        last = mm(o, one, base[:, b, :], False, True)
                    last.then_inc(r_rk, 1)
                    if b == B - 1:
                        mm(bank[6][:, 0:E], one, base[:, B, :]).then_inc(cn_ps, 1)

            pe.wait_ge(w_lo, CHUNKS)
            for b in range(B + 1):
                if b < B:
                    wait(pe, h_h, b - 1)
                    for c in range(2):
                        w = slice(W_SG + c * D, W_SG + (c + 1) * D)
                        o, n = bank[2 * (b % 2) + c][:, :], slice(b * S, (b + 1) * S)
                        mm(o, wh[:, w], ntt[:, 0, n], True, False)
                        mm(o, wh[:, w], ntt[:, 1, n], False, False)
                        mm(o, wl[:, w], ntt[:, 0, n], False, True).then_inc(h_ps, 1)
                if b >= 1:
                    c = b - 1
                    pe.wait_ge(h_lo, b)
                    wait(pe, h_x, c - 1)
                    for t in range(T):
                        o = bank[4 + c % 2][:, t * D:(t + 1) * D]
                        hi = hsp[:, c % 2, t * P:(t + 1) * P]
                        lo = hsp[:, c % 2, S + t * P:S + (t + 1) * P]
                        mm(o, hi, wh[:, W_SD:W_SD + D], True, False)
                        mm(o, hi, wl[:, W_SD:W_SD + D], False, False)
                        last = mm(o, lo, wh[:, W_SD:W_SD + D], False, True)
                    last.then_inc(h_y, 1)

            def experts(i):
                word = pe.value_load(te_i[0:1, ds(i, 1)], min_val=0, max_val=8 ** 8 - 1)
                return [(word >> (3 * j)) & (E - 1) for j in range(8)]

            def step_pe(s, u, expert, expert2):
                static = isinstance(s, int)
                if not static or 0 <= s + 3 < TILES:
                    r = (u + 3) % 4
                    pe.wait_ge(d_ld[r], (s + 3 - r) * 4 + 16)
                    wait(pe, d_xe, s + 2)
                    for h in range(2):
                        w = xd[:, r, h * (D // 2):(h + 1) * (D // 2)].bitcast(F16)
                        last = mm(bank[4 + r % 2][:, h * P:(h + 1) * P], w, ident16)
                    last.then_inc(d_xt, 1)
                if not static or 0 <= s + 2 < TILES:
                    pe.wait_ge(d_xe, s + 3)
                    wait(pe, d_h, s + 1)
                    for i in range(NF):
                        o = bank[2 * (i // FC) + u % 2][:, (i % FC) * P:(i % FC + 1) * P]
                        w = ds(expert2 * (2 * FF) + (W_GU + i * P), P)
                        xa, xb = xdt[:, u % 2, 0:P], xdt[:, u % 2, P:2 * P]
                        mm(o, wh[:, w], xa, True, False)
                        mm(o, wh[:, w], xb, False, False)
                        last = mm(o, wl[:, w], xa, False, True)
                    last.then_inc(d_gu, 1)
                if not static or 0 <= s < TILES:
                    pe.wait_ge(d_lo, s + 1)
                    wait(pe, d_yv, s - 1)
                    o = bank[6 + u % 2][:, 0:D]
                    for i in range(FC):
                        w = ds(expert * (FC * D) + (W_DN + i * D), D)
                        hi = hsplit[:, u % 2, i * P:(i + 1) * P]
                        lo = hsplit[:, u % 2, FF + i * P:FF + (i + 1) * P]
                        mm(o, hi, wh[:, w], i == 0, False)
                        mm(o, hi, wl[:, w], False, False)
                        last = mm(o, lo, wh[:, w], False, i == FC - 1)
                    last.then_inc(d_y, 1)

            pe.wait_ge(h_x, B)
            pe.wait_ge(tiles, 2)
            first = experts(TILES // 4)
            for s in range(-3, 5):
                step_pe(s, s % 4, first[max(s, 0)], first[max(s + 2, 0)])
            with pe.Fori(1, TILES // 4 - 1) as i:
                e = experts(i)
                for u in range(1, 5):
                    step_pe(4 * i + u, u % 4, e[u - 1], e[u + 1])
            last = experts(TILES // 4 - 1)
            for s in range(TILES - 3, TILES + 1):
                u = s - (TILES - 3)
                step_pe(s, s % 4, last[u], last[u + 2])


def constants():
    p = np.arange(P)
    c32 = np.zeros((P, C_END), np.float32)
    c32[:, C_ID:C_ID + P] = np.eye(P)
    c32[:, C_HM:C_HM + H] = p[:, None] // HD == np.arange(H)
    c32[:, C_HR:C_HR + H] = p[:, None] // KC == np.arange(H) % HC
    c32[:, C_S:C_S + TTAB] = np.arange(TTAB)
    c32[:, C_S128:C_S128 + TTAB] = P * np.arange(TTAB)
    c32[:, C_EREG:C_EREG + E] = REG * np.arange(E)
    c32[:, C_I8:C_I8 + E] = np.arange(E)
    c32[:, C_2T:C_2T + NT] = 2 * (p[:, None] + P * np.arange(NT))
    c32[:, C_P8:C_P8 + 8] = 8.0 ** np.arange(8)
    half = NROT // 2
    inv = (1.0 / 10000.0 ** (np.arange(half, dtype=np.float32) * np.float32(2.0) / np.float32(NROT))).astype(np.float32)
    ang = np.arange(S, dtype=np.float32)[:, None] * inv
    trig = np.zeros((S, 4 * half), np.float16)
    for i, f in enumerate((np.cos, np.sin)):
        v = f(ang.astype(np.float64)).astype(np.float32)
        hi = v.astype(np.float16)
        trig[:, 2 * i * half:(2 * i + 1) * half] = hi
        trig[:, (2 * i + 1) * half:(2 * i + 2) * half] = v - hi.astype(np.float32)
    c16 = np.zeros((P, G_END), np.float16)
    c16[:, G_ID:G_ID + P] = np.eye(P)
    c16[:, G_IOTA:G_IOTA + J] = 1 + np.arange(J)
    c16[:, G_TRIG:G_TRIG + S] = trig.reshape(T, P, P).transpose(1, 0, 2).reshape(P, S)
    r = p % half
    comb = np.zeros((P, P))
    for c in range(P):
        kind, f = c // half, c % half
        comb[:, c] = (r == f) * (p // (2 * half) == (kind >= 2)) * (-1 if kind == 2 else 1)
    c16[:, G_COMB:G_COMB + P] = comb
    c16[:, G_TRI:G_TRI + P] = p[:, None] < p
    c16[:, G_ONE:G_ONE + P] = 1
    cbf = np.zeros((P, 2 * P), mybir.dt.np(BF16))
    cbf[:, 0:P] = np.eye(P)
    cbf[:, P:2 * P] = np.where((p[:, None] // J == p // J) & (p[:, None] >= p), 0.0, -1e30)
    pad = np.zeros((P, PAY_W), np.float32)
    pad[:, D] = 2 * B * S + p
    pad[:, D + 1] = -1
    pad[:, D + 2] = 1
    return c32, c16, cbf, pad


def laid_out(i):
    a = {k: np.asarray(v) for k, v in i.items()}
    ctxt = a["ctx_1024"].transpose(2, 0, 1)
    wqkv = a["L0_ffn_Wqkv"]
    qkc = np.concatenate([wqkv[:, :, 0:NROT], wqkv[:, :, D:D + NROT], wqkv[:, :, NROT:D], wqkv[:, :, D + NROT:2 * D]], 2)
    big = np.concatenate([
        qkc.transpose(1, 0, 2).reshape(P, -1),
        a["L1_ffn_gate_up_w"].transpose(2, 0, 1).reshape(P, -1),
        a["L1_ffn_down_w"].reshape(E, D, FC, P).transpose(3, 0, 2, 1).reshape(P, -1),
        a["L1_ffn_shared_gate_up_w"].T, a["L1_ffn_shared_down_w"].T], 1)
    c32, c16, cbf, pad = constants()
    return [
        a["x"], np.broadcast_to(ctxt[:, :, None, :], (P, B, HC, KC)),
        a["mask_SxS2_bk0"].reshape(T, P, KC).transpose(1, 0, 2),
        a["g_xattn"], a["g_ffn"], a["L0_xattn_Wq"].T, a["L0_xattn_Wkv"], a["L0_ffn_Wr"].T,
        wqkv[:, :, 2 * D:].transpose(2, 0, 1), a["L0_ffn_Wo"].transpose(1, 0, 2),
        a["L1_xattn_Wk"].T, a["L1_xattn_Wq"], a["L1_xattn_Wv"].T, a["L1_xattn_Wo"].T,
        a["L1_ffn_ln_gamma"], a["L1_ffn_ln_beta"], a["L1_ffn_router_w"].T, big, c32, c16, cbf, pad]


def kernel(**inputs):
    import concourse.bacc as bacc
    from concourse.bass_utils import run_bass_kernel_spmd

    nc = bacc.Bacc("TRN2", target_bir_lowering=False, num_devices=1)
    arrays, args = {}, []
    for n, v in enumerate(laid_out(inputs)):
        v = np.ascontiguousarray(v)
        arrays[f"in{n}"] = v
        args.append(nc.dram_tensor(f"in{n}", v.shape, mybir.dt.from_np(v.dtype), kind="ExternalInput").ap())
    args.append(nc.dram_tensor("out", (B, S, D), F32, kind="ExternalOutput").ap())
    build(nc, *args)
    return run_bass_kernel_spmd(nc, [arrays], core_ids=[0]).results[0]["out"]
```

```python
from contextlib import ExitStack

import numpy as np
import concourse.bass as bass
from concourse import mybir

F32 = mybir.dt.float32
F16 = mybir.dt.float16
BF16 = mybir.dt.bfloat16
I32 = mybir.dt.int32
U32 = mybir.dt.uint32
ALU = mybir.AluOpType
ACT = mybir.ActivationFunctionType
AX = mybir.AxisListType
ds = bass.ds

P = 128
B, S, D = 4, 512, 128
T = S // P
NT = B * T
KC = 32
E = 8
J = S // E
H = 16
HD = D // H
HC = P // KC
NC = H // HC
NROT = 64
FF = 384
FC = FF // P
NF = 2 * FC
WS = 256.0
REG = B * S + P
TILES = 40
TTAB = TILES + 8
PAY_W = D + 3
LN_EPS = 1e-5
TOPV = -3.0e38
NQ = 2 * D + D + 1

W_QK = 0
W_GU = W_QK + E * 2 * D
W_DN = W_GU + E * 2 * FF
W_SG = W_DN + E * FC * D
W_SD = W_SG + 2 * D
W_END = W_SD + D
CH = 512
CHUNKS = -(-W_END // CH)
SH = 2
EARLY = 12
WLOAD = 4
WRING = 3 * WLOAD

NX = E * B // 2

A_EVERY = 3
A_PE = {"xt": 6, "scores": 8, "et": 10, "mix": 12, "xt2": 21, "logits": 22}
A_ACT = {"norm": 2, "xt_out": 3, "exp": 6, "et_out": 7, "norm2": 15, "xt2_out": 18, "high": 61}
A_DVE = {"stats": -23, "shift": 13, "sum": 13, "add": 18, "logits_out": 41}
A_POOL = {"rstd": -44, "rstd2": 11, "low": 28}
X_EVERY = 3
X_PE = {"project": 0, "turn": 6, "scores": 6.5, "et": 11, "mix": 14}
X_ACT = {"rows": 2, "turn_out": 4.5, "exp": 6, "et_out": 10.5, "high": 15}
X_DVE = {"rotate": 0, "max": 6, "scale": 7, "low": 16}
C_EVERY = 1
C_PE = {"scatter": -5.2, "keys": -5.1, "xt": 0.5, "scores": 1.6, "et": 3, "pv": 4, "ot": 5.5, "w": 6, "turn": 9.1,
        "logits": 10.5, "rank": 11.4}
C_ACT = {"chunk": -4.9, "norm": 1.1, "keys_out": 1.2, "xt_out": 1.8, "exp": 3.2, "e1t": 4.5, "ont": 6.5, "norm2": 8,
         "high": 8.6, "turn_out": 10.8, "exp_logits": 11.4}
C_DVE = {"residual": -4.8, "shift": 1.9, "over_sum": 4.4, "add": 6.3, "affine": 7.6, "low": 8.9,
         "shift_logits": 10.4, "route": 10.9, "slots": 12}
C_POOL = {"rstd": -9.7, "low": -5.3, "rstd2": -4.2, "send": 1.8, "send2": 5.4}

C_ID, C_HM, C_HR, C_S, C_S128, C_EREG, C_I8, C_P8, C_2T = 0, 128, 144, 160, 208, 256, 264, 272, 280
C_END = C_2T + NT
G_ID, G_IOTA, G_TRIG, G_COMB, G_TRI, G_ONE = 0, 128, 192, 704, 832, 960
G_END = 1088


def skewed(n, every, at):
    return [(stage, i) for _, i, stage in sorted((every * i + slot, i, stage) for stage, slot in at.items() for i in range(n))]


def build(nc, x_in, ctx_in, mask_in, gx_in, gf_in, wq0_in, wkv0_in, wr0_in, wv0_in, wo0_in, wk1_in,
          wq1_in, wv1_in, wo1_in, gamma_in, beta_in, router_in, wbig_in, c32_in, c16_in, cbf_in,
          pad_in, out):
    disp = nc.dram_tensor("dispatched_rows", ((E + 1) * REG, PAY_W), F32).ap()
    ytok = nc.dram_tensor("expert_rows", (2 * B * S + TILES * P + 1, D), F32).ap()
    x_v = x_in.rearrange("b (t p) d -> p (b t) d", p=P)
    out_v = out.rearrange("b (t p) d -> p (b t) d", p=P)
    ytok_v = ytok[0:2 * B * S, :].rearrange("(n p k) d -> p n (k d)", p=P, k=2)

    with ExitStack() as ctx:
        def sb(name, shape, dt=F32):
            return ctx.enter_context(nc.sbuf_tensor(name, shape, dt))

        def sem(name):
            return ctx.enter_context(nc.semaphore(name))

        bank = [ctx.enter_context(nc.psum_tensor(f"bank{i}", [P, 512], F32)) for i in range(8)]

        x = sb("x", [P, NT, D])
        c32 = sb("c32", [P, C_END])
        c16 = sb("c16", [P, G_END], F16)
        cbf = sb("cbf", [P, 2 * P], BF16)
        ident = c32[:, C_ID:C_ID + P]
        ident16 = c16[:, G_ID:G_ID + P]
        identbf = cbf[:, 0:P]
        causal = cbf[:, P:2 * P]
        tg = sb("tanh_gates", [P, 4])
        graw = sb("graw", [P, 4])
        st = sb("bn_raw", [P, NT, 6])
        mv = sb("mean_var", [P, NT, 2])
        ve = sb("var_eps", [P, NT])
        rstd = sb("rstd", [P, NT])
        nmr = sb("minus_mean_rstd", [P, NT])
        mhalf = sb("minus_half", [P, NT])
        ctxr = sb("ctx_t", [P, B, HC, KC])
        wq0 = sb("wq0", [P, D])
        wkv0 = sb("wkv0", [P, 2 * D])
        wr0 = sb("wr0", [P, E])
        region_w = sb("region_w", [P, 2 * E * D])
        wv0 = region_w[:, 0:E * D].rearrange("p (e d) -> p e d", d=D)
        wo0 = region_w[:, E * D:2 * E * D].rearrange("p (e d) -> p e d", d=D)
        qk = region_w[:, 0:8 * D].rearrange("p (q h d) -> p q h d", q=4, h=2)
        qkt = region_w[:, E * D:E * D + 8 * P].rearrange("p (q n) -> p q n", q=4)
        wk1 = sb("wk1", [P, D])
        wq1 = sb("wq1", [P, D])
        wv1 = sb("wv1", [P, D])
        wo1 = sb("wo1", [P, D])
        gamma = sb("gamma", [P, D])
        beta = sb("beta", [P, D])
        router = sb("router", [P, E])
        router16 = sb("router16", [P, 2, E], F16)
        mask8 = sb("mask8", [P, T, KC], mybir.dt.uint8)
        maskf = sb("maskf", [P, T, KC])
        maskbf = sb("mask_bias", [P, T, KC], BF16)
        anyk = sb("any_key", [P, T])
        k0t = sb("k0t", [P, B * KC])
        k1t = sb("k1t", [P, B, KC])
        wk0 = sb("wq_k0", [P, B, KC])
        v0 = sb("v0", [KC, B, D])
        vblk = sb("v_blocks", [P, B, H, HD + 1])
        wf = sb("w_scaled", [P, WRING * CH])
        wh = sb("w_high", [P, CHUNKS * CH], F16)
        wl = sb("w_low", [P, CHUNKS * CH], F16)
        vwh = sb("vwo_high", [P, E, D + 1], F16)
        vwl = sb("vwo_low", [P, E, D + 1], F16)
        xh = sb("x_hat", [P, NT, D])
        region_t = sb("region_t", [P, NT * PAY_W])
        xt = region_t[:, 0:B * S].rearrange("p (b s) -> p b s", b=B)
        tab = region_t[:, 0:E * 2 * D].rearrange("p (e h d) -> p e h d", e=E, h=2)
        pay = region_t[:, :].rearrange("p (n w) -> p n w", w=PAY_W)
        es = sb("cross_sub", [P, B, T, KC])
        nm = sb("neg_max", [P, B, T])
        zs = sb("z_sum", [P, B, T])
        rz = sb("r_z", [P, B, T])
        et0 = sb("cross_e_t", [KC, B, S])
        region_s = sb("region_s", [P, 2 * NT * D], F16)
        xs = region_s[:, :].rearrange("p (h n d) -> p h n d", h=2, n=NT)
        yh = region_s[:, 0:E // 2 * B * D].rearrange("p (g b d) -> p g b d", g=E // 2, b=B)
        yl = region_s[:, E // 2 * B * D:E * B * D].rearrange("p (g b d) -> p g b d", g=E // 2, b=B)
        lg = sb("logits0", [P, T, B, E])
        region_k = sb("region_k", [P, 4, S])
        work, ones32, sel, scan = (region_k[0:B * E, i, :] for i in range(4))
        esl, etl = (region_k[:, i, :].rearrange("p (q n) -> p q n", q=4) for i in (1, 2))
        vv = xh
        rpa = region_k[:, 0, 0:4 * D].rearrange("p (q h d) -> p q h d", q=4, h=2)
        top8 = sb("top8", [B * E, 8])
        pos = sb("slot_of_token", [P, T, B, E])
        region_p = sb("region_p", [P, NT * E * J // 2])
        pick = region_p[:, :].bitcast(F16).rearrange("p (n c) -> p n c", n=NT)
        a1 = region_p[:, 0:B * H * KC].rearrange("p (b c) -> p b c", b=B)
        ntt = region_p[:, B * H * KC:2 * B * H * KC].bitcast(F16).rearrange("p (h n) -> p h n", h=2)
        region_q = sb("region_q", [P, NT * E * J // 2])
        pickt = region_q[:, :].bitcast(F16).rearrange("p (n g c) -> p n g c", n=NT, g=E // 2)
        vwf = region_q[:, 0:E * (D + 1)].rearrange("p (e d) -> p e d", e=E)
        yk = region_q[:, :].rearrange("p (n w) -> p n w", n=NT)
        region_x = sb("region_x", [P, 2 * E * B * J], F16)
        xg = region_x[:, :].rearrange("p (h e b j) -> p h e b j", h=2, e=E, b=B)
        trg = sb("trig_gathered", [P, E, B, J], F16)
        rpb = sb("rope_b", [P, 4, 2, NROT])
        lsl = sb("exp_neg_logit", [P, 4])
        nms = sb("slot_neg_max", [P, 4])
        zsl = sb("slot_z", [P, 4])
        den = sb("slot_den", [P, 4])
        rzs = sb("slot_rz", [P, 4])

        kbl = region_p[:, B * H * KC:2 * B * H * KC].rearrange("p (b c) -> p b c", b=B)
        vrep = es[:, :, :, :].rearrange("p b t k -> p b (t k)")
        e1 = region_k[:, 0:2, :]
        e1t = region_k[:, 2:4, :]
        xf = region_x[:, :].bitcast(F32)
        xtc = xf[:, 0:2 * P].rearrange("p (r n) -> p r n", r=2)
        on = xf[:, 2 * P:4 * P].rearrange("p (r n) -> p r n", r=2)
        ont = xf[:, 4 * P:6 * P].rearrange("p (r n) -> p r n", r=2)
        nm1 = sb("nm1", [P, 2, H])
        zi = sb("z_inv", [P, 2, H])
        tgw = sb("tanh_gate_ws", [P, 1])
        rmax = sb("r_max", [P, T])
        prob = sb("r_prob", [P, NT, E])
        rsum = sb("r_sum", [P, NT])
        ptop = sb("r_ptop", [P, NT, 2])
        rtop = sb("r_top", [P, NT, 8])
        ridx = sb("r_idx", [P, T, 8], U32)
        gexp = sb("gate_exp", [P, NT])
        gden = sb("gate_den", [P, NT])
        gate = sb("gates", [P, NT, 2])
        ef = sb("expert_of", [P, T, 2])
        oh = sb("one_hot", [P, T, 2, E])
        msel = sb("routed", [P, NT, E], F16)
        rk = sb("rank_row", [P, T, E])
        ohr = sb("one_hot_row", [P, T, 2, E])
        slotf = sb("slot_f", [P, T, 2])
        slot = sb("slot", [P, NT, 2], I32)
        tsum = sb("tile_sum", [P, E])
        base = sb("routed_before", [P, B + 1, E], F16)
        cnt = sb("count", [P, E])
        cnti = sb("count_i", [P, E], I32)
        ntil = sb("tiles_of", [P, E])
        ncum = sb("tiles_upto", [P, E])
        ge, gn = (xf[:, i * TTAB * E:(i + 1) * TTAB * E].rearrange("p (s e) -> p s e", e=E) for i in (2, 3))
        te = sb("tile_expert", [P, TTAB])
        tb = sb("tiles_before", [P, TTAB])
        trow = sb("tile_row", [P, TTAB])
        trow_i = sb("tile_row_i", [P, TTAB], I32)
        tw = sb("tile_window", [P, TILES // 4, 8])
        tpack = sb("tile_pack", [P, TILES // 4])
        te_i = sb("tile_pack_i", [P, TILES // 4], I32)
        padr = sb("pad_row_i", [P, E], I32)
        onee = sb("ones_e", [P, E])
        padt = sb("pad_rows", [P, PAY_W])
        hs = region_w[:, 0:4 * CH].rearrange("p (r n) -> p r n", r=4)
        hsp = region_k[:, 0:2, :].bitcast(F16)
        xd = sb("slot_rows", [P, 4, PAY_W])
        dbase = sb("slot_dest_base", [P, 1])
        dall = sb("slot_dest_of", [P, TILES])
        dst = sb("slot_dest", [P, 4], I32)
        xdt = sb("slot_rows_t", [P, 2, 2 * P], F16)
        sil = region_w[:, 0:2 * FF].rearrange("p (r n) -> p r n", r=2)
        hid = region_w[:, 2 * FF:4 * FF].rearrange("p (r n) -> p r n", r=2)
        hsplit = region_k[:, 0:2, 0:FF].bitcast(F16)
        hidt = xf[:, 0:2 * FF].bitcast(F16).rearrange("p (r n) -> p r n", r=2)
        xt_ps = bank[4][:, 0:P].bitcast(F16)
        ht_ps = bank[5][:, 0:FF].bitcast(F16)
        yv = region_k[:, 2, :].rearrange("p (r n) -> p r n", r=4)

        x_loaded = [sem(f"x_loaded{b}") for b in range(B)]
        ctx_loaded = sem("ctx_loaded")
        c32_loaded = sem("c32_loaded")
        gates_loaded = sem("gates_loaded")
        c16_loaded = sem("c16_loaded")
        vo0_loaded = sem("vo0_loaded")
        layer1_loaded = sem("layer1_loaded")
        w_loaded = [sem(f"w_loaded{i}") for i in range(-(-CHUNKS // WLOAD))]
        stored = sem("stored")
        v_link = sem("v_link")
        g_link = sem("g_link")
        a_link = sem("a_link")
        k0_made = sem("k0_made")
        k0_out = sem("k0_out")
        v0_out = sem("v0_out")
        wqk0_made = sem("wqk0_made")
        wqk0_out = sem("wqk0_out")
        tanh_done = sem("tanh_done")
        pre0_stats = sem("pre0_stats")
        pre0_rstd = sem("pre0_rstd")
        pre0_normed = sem("pre0_normed")
        pre0_turned = sem("pre0_turned")
        pre0_turned_out = sem("pre0_turned_out")
        cross0_scores = sem("cross0_scores")
        cross0_shifted = sem("cross0_shifted")
        cross0_exp = sem("cross0_exp")
        cross0_exp_turned = sem("cross0_exp_turned")
        cross0_exp_out = sem("cross0_exp_out")
        cross0_mixed = sem("cross0_mixed")
        sel_stats = sem("sel_stats")
        sel_rstd = sem("sel_rstd")
        sel_normed = sem("sel_normed")
        sel_turned = sem("sel_turned")
        sel_turned_out = sem("sel_turned_out")
        sel_high = sem("sel_high")
        sel_low = sem("sel_low")
        sel_logits = sem("sel_logits")
        sel_logits_out = sem("sel_logits_out")
        w_high_done = sem("w_high_done")
        w_low_done = sem("w_low_done")
        vwo_made = sem("vwo_made")
        vwo_scaled = sem("vwo_scaled")
        vwo_split = sem("vwo_split")
        logit_rows = sem("logit_rows")
        slot_rows_made = sem("slot_rows_made")
        slot_rows_turned = sem("slot_rows_turned")
        one_hot_made = sem("one_hot_made")
        gathered = sem("gathered")
        gathered_out = sem("gathered_out")
        trig_out = sem("trig_out")
        one_hot_turned = sem("one_hot_turned")
        one_hot_turned_out = sem("one_hot_turned_out")
        tables_made = sem("tables_made")
        tables_out = sem("tables_out")

        qkv_made = sem("qkv_made")
        rope_products = sem("rope_products")
        rope_done = sem("rope_done")
        rows_out = sem("rows_out")
        qk_turned = sem("qk_turned")
        qk_turned_out = sem("qk_turned_out")
        slot_scores = sem("slot_scores")
        slot_max = sem("slot_max")
        slot_exp = sem("slot_exp")
        slot_scaled = sem("slot_scaled")
        slot_exp_turned = sem("slot_exp_turned")
        slot_exp_out = sem("slot_exp_out")
        slot_mixed = sem("slot_mixed")
        mixed_high = sem("mixed_high")
        mixed_low = sem("mixed_low")
        kv1_made = sem("kv1_made")
        k1_out = sem("k1_out")
        v1_out = sem("v1_out")
        v_blocks_done = sem("v_blocks_done")
        k_blocks_done = sem("k_blocks_done")
        wqk1_made = sem("wqk1_made")
        wqk1_out = sem("wqk1_out")
        mask_done = sem("mask_done")
        scattered = sem("scattered")
        pre1_stats = sem("pre1_stats")
        pre1_rstd = sem("pre1_rstd")
        pre1_normed = sem("pre1_normed")
        pre1_turned = sem("pre1_turned")
        pre1_turned_out = sem("pre1_turned_out")
        cross1_scores = sem("cross1_scores")
        cross1_shifted = sem("cross1_shifted")
        cross1_exp = sem("cross1_exp")
        cross1_exp_turned = sem("cross1_exp_turned")
        cross1_exp_out = sem("cross1_exp_out")
        cross1_mixed = sem("cross1_mixed")
        cross1_over_sum = sem("cross1_over_sum")
        cross1_turned = sem("cross1_turned")
        cross1_turned_out = sem("cross1_turned_out")
        cross1_projected = sem("cross1_projected")
        cross1_added = sem("cross1_added")
        ffn_stats = sem("ffn_stats")
        ffn_normed = sem("ffn_normed")
        ffn_rstd = sem("ffn_rstd")
        ffn_affine = sem("ffn_affine")
        ffn_high = sem("ffn_high")
        ffn_low = sem("ffn_low")
        ffn_turned = sem("ffn_turned")
        ffn_turned_out = sem("ffn_turned_out")
        route_logits = sem("route_logits")
        route_shifted = sem("route_shifted")
        route_exp = sem("route_exp")
        top2_difference = sem("top2_difference")
        top2_exp = sem("top2_exp")
        routed_marked = sem("routed_marked")
        route_ranks = sem("route_ranks")
        slots_ready = sem("slots_ready")
        sent = sem("sent")
        router_split = sem("router_split")
        counts_made = sem("counts_made")
        tiles = sem("tiles")
        padded = sem("padded")
        sh_gate_up = sem("sh_gate_up")
        sh_silu = sem("sh_silu")
        sh_hidden = sem("sh_hidden")
        sh_high = sem("sh_high")
        sh_low = sem("sh_low")
        sh_down = sem("sh_down")
        sh_added = sem("sh_added")
        rows_loaded = [sem(f"rows_loaded{r}") for r in range(4)]
        dest_ready = sem("dest_ready")
        dest_base = sem("dest_base")
        rows_turned = sem("rows_turned")
        rows_turned_out = sem("rows_turned_out")
        gate_up_made = sem("gate_up_made")
        silu_done = sem("silu_done")
        hidden_done = sem("hidden_done")
        hidden_high = sem("hidden_high")
        hidden_turned = sem("hidden_turned")
        hidden_turned_out = sem("hidden_turned_out")
        hidden_low = sem("hidden_low")
        down_made = sem("down_made")
        rows_ready = sem("rows_ready")
        rows_sent = [sem(f"rows_sent{r}") for r in range(4)]
        sum_done = sem("sum_done")
        last_gated = sem("last_gated")
        gates_done = sem("gates_done")
        last_added = sem("last_added")

        def wait(eng, s, v):
            if not isinstance(v, int) or v > 0:
                eng.wait_ge(s, v)

        block = ctx.enter_context(nc.Block())

        @block.sync
        def _(eng):
            eng.dma_start(x[:, 0:T, :], x_v[:, 0:T, :]).then_inc(x_loaded[0], 16)
            eng.dma_start(ctxr[:, :, :, :], ctx_in).then_inc(ctx_loaded, 16)
            eng.dma_start(wkv0[:, :], wkv0_in).then_inc(ctx_loaded, 16)
            eng.dma_start(wq0[:, :], wq0_in).then_inc(ctx_loaded, 16)
            for b in range(1, B):
                eng.dma_start(x[:, b * T:(b + 1) * T, :], x_v[:, b * T:(b + 1) * T, :]).then_inc(x_loaded[b], 16)
            eng.dma_start(graw[:, 0:2], gx_in.rearrange("(a n) -> a n", a=1).partition_broadcast(P)).then_inc(gates_loaded, 16)
            eng.dma_start(graw[:, 2:4], gf_in.rearrange("(a n) -> a n", a=1).partition_broadcast(P)).then_inc(gates_loaded, 16)
            eng.dma_start(wr0[:, :], wr0_in).then_inc(gates_loaded, 16)
            eng.dma_start(wv0, wv0_in).then_inc(vo0_loaded, 16)
            eng.dma_start(wo0, wo0_in).then_inc(vo0_loaded, 16)
            eng.dma_start(c16[:, :], c16_in).then_inc(c16_loaded, 16)
            eng.dma_start(cbf[:, :], cbf_in).then_inc(c16_loaded, 16)
            eng.dma_start(wk1[:, :], wk1_in).then_inc(layer1_loaded, 16)
            eng.dma_start(wq1[:, :], wq1_in).then_inc(layer1_loaded, 16)
            eng.dma_start(wv1[:, :], wv1_in).then_inc(layer1_loaded, 16)
            eng.dma_start(wo1[:, :], wo1_in).then_inc(layer1_loaded, 16)
            eng.dma_start(gamma[:, :], gamma_in.rearrange("(a n) -> a n", a=1).partition_broadcast(P)).then_inc(layer1_loaded, 16)
            eng.dma_start(beta[:, :], beta_in.rearrange("(a n) -> a n", a=1).partition_broadcast(P)).then_inc(layer1_loaded, 16)
            eng.dma_start(router[:, :], router_in).then_inc(layer1_loaded, 16)
            eng.dma_start(mask8[:, :, :], mask_in).then_inc(layer1_loaded, 16)
            for i in range(len(w_loaded)):
                lo, hi = i * WLOAD * CH, min((i + 1) * WLOAD * CH, W_END)
                at = lo % (WRING * CH)
                if i >= WRING // WLOAD:
                    eng.wait_ge(w_low_done, (i + 1) * WLOAD - WRING)
                eng.dma_start(wf[:, at:at + hi - lo], wbig_in[:, lo:hi]).then_inc(w_loaded[i], 16)
            eng.dma_start(padt[:, :], pad_in).then_inc(padded, 16)
            eng.wait_ge(padded, 16)
            eng.dma_start(disp[E * REG:E * REG + P, :], padt[:, :]).then_inc(padded, 16)
            eng.wait_ge(tiles, 1)
            for e in range(E):
                row = eng.value_load(padr[0:1, e:e + 1], min_val=0, max_val=E * REG)
                eng.dma_start(disp[ds(row, P), :], padt[:, :]).then_inc(padded, 16)
            eng.wait_ge(padded, 16 * (E + 2))
            eng.wait_ge(sent, 16 * 2 * NT)
            eng.wait_ge(tiles, 2)

            def load_slots(s, r):
                wait(eng, rows_turned, s - 3)
                wait(eng, dest_ready, s - 3)
                row = eng.value_load(trow_i[0:1, ds(s, 1)], min_val=0, max_val=E * REG)
                eng.dma_start(xd[:, r, :], disp[ds(row, P), :]).then_inc(rows_loaded[r], 16)

            for r in range(4):
                load_slots(r, r)
            with eng.Fori(1, TILES // 4) as i:
                for r in range(4):
                    load_slots(4 * i + r, r)
            for r in range(4):
                eng.wait_ge(rows_sent[r], 16 * (TILES // 4))
            for b in (0, B - 1, *range(1, B - 1)):
                eng.dma_start(yk[:, b * T:(b + 1) * T, :], ytok_v[:, b * T:(b + 1) * T, :]).then_inc(x_loaded[b], 16)
            for b in range(B):
                if b < B - 1:
                    eng.wait_ge(sum_done, b + 1)
                else:
                    eng.wait_ge(last_added, 2)
                eng.dma_start(out_v[:, b * T:(b + 1) * T, :], x[:, b * T:(b + 1) * T, :]).then_inc(stored, 16)
            eng.wait_ge(stored, 16 * B)

        @block.scalar
        def _(act):
            act.dma_start(c32[:, :], c32_in).then_inc(c32_loaded, 16)
            nc.scalar.preload_act_table(ACT.Exp)

            act.wait_ge(k0_made, 1)
            act.activation(k0t[:, :], bank[7][:, 0:B * KC], ACT.Copy).then_inc(k0_out, 1)
            act.wait_ge(wqk0_made, 1)
            act.activation(wk0[:, :, :].rearrange("p b k -> p (b k)"), bank[7][:, P:P + B * KC], ACT.Copy).then_inc(wqk0_out, 1)
            act.activation(v0[:, :, :].rearrange("p b k -> p (b k)"), bank[6][0:KC, :], ACT.Copy).then_inc(v0_out, 1)
            act.wait_ge(gates_loaded, 48)
            act.activation(tg[:, :], graw[:, :], ACT.Tanh).then_inc(tanh_done, 1)

            def normalise(b, ready, done):
                act.wait_ge(ready, b + 1)
                for t in range(b * T, (b + 1) * T):
                    last = act.activation(xh[:, t, :], x[:, t, :], ACT.Identity, bias=nmr[:, t:t + 1],
                                          scale=rstd[:, t:t + 1])
                last.then_inc(done, 1)

            def split_high(i):
                if i % WLOAD == 0:
                    act.wait_ge(w_loaded[i // WLOAD], 16)
                n = min(CH, W_END - i * CH)
                r = slice(i % WRING * CH, i % WRING * CH + n)
                act.activation(wf[:, r], wf[:, r], ACT.Copy, scale=WS).then_inc(a_link, 1)
                act.wait_ge(a_link, i + 1)
                act.activation(wh[:, i * CH:i * CH + n], wf[:, r], ACT.Copy).then_inc(w_high_done, 1)

            for stage, b in skewed(B, A_EVERY, A_ACT):
                if stage == "norm":
                    act.wait_ge(x_loaded[b], 16)
                    normalise(b, pre0_rstd, pre0_normed)
                elif stage == "norm2":
                    act.wait_ge(pre0_turned, b + 1)
                    normalise(b, sel_rstd, sel_normed)
                elif stage == "xt_out":
                    act.wait_ge(pre0_turned, b + 1)
                    act.activation(xt[:, b, :], bank[b % 2][:, :], ACT.Copy).then_inc(pre0_turned_out, 1)
                elif stage == "exp":
                    act.wait_ge(cross0_shifted, b + 1)
                    act.activation(es[:, b, :, :], es[:, b, :, :], ACT.Exp, scale=D ** -0.5).then_inc(cross0_exp, 1)
                elif stage == "et_out":
                    act.wait_ge(cross0_exp_turned, b + 1)
                    act.activation(et0[:, b, :], bank[3][0:KC, :], ACT.Copy).then_inc(cross0_exp_out, 1)
                elif stage == "high":
                    act.wait_ge(sel_normed, b + 1)
                    act.activation(xs[:, 0, b * T:(b + 1) * T, :], xh[:, b * T:(b + 1) * T, :], ACT.Copy).then_inc(sel_high, 1)
                elif stage == "xt2_out":
                    act.wait_ge(sel_turned, b + 1)
                    act.activation(xt[:, b, :], bank[b % 2][:, :], ACT.Copy).then_inc(sel_turned_out, 1)
            for h in range(2):
                act.wait_ge(vwo_made, h + 1)
                act.activation(vwf[:, 4 * h:4 * h + 4, 0:D], bank[4 + h][:, :].rearrange("p (e d) -> p e d", d=D),
                               ACT.Copy, scale=WS).then_inc(vwo_scaled, 1)
            act.activation(vwf[:, :, D], wr0[:, :], ACT.Copy, scale=WS).then_inc(vwo_scaled, 1)
            act.wait_ge(vwo_scaled, 3)
            act.activation(vwh[:, :, :], vwf[:, :, :], ACT.Copy).then_inc(vwo_scaled, 1)
            act.wait_ge(kv1_made, 1)
            act.activation(k1t[:, :, :].rearrange("p b k -> p (b k)"), bank[2][:, 0:B * KC], ACT.Copy).then_inc(k1_out, 1)
            act.activation(vrep[:, :, :].rearrange("p b k -> p (b k)"), bank[3][:, :], ACT.Copy).then_inc(v1_out, 1)
            for i in range(EARLY):
                split_high(i)
            act.wait_ge(vwo_split, 1)
            for b in range(B):
                for t in range(T):
                    act.wait_ge(one_hot_turned, b * T + t + 1)
                    act.activation(pickt[:, b * T + t, :, :], bank[6 + t % 2][:, :].rearrange("p (g n) -> p g n", n=P),
                                   ACT.Copy).then_inc(one_hot_turned_out, 1)
                act.wait_ge(gathered, b + 1)
                g = 3 * (b % 2)
                for h in range(2):
                    act.activation(xg[:, h, :, b, :], bank[g + h][:, :].rearrange("p (e j) -> p e j", j=J),
                                   ACT.Copy).then_inc(gathered_out, 1)
            for stage, n in skewed(NX, X_EVERY, X_ACT):
                q = n % 4
                if stage == "rows":
                    act.wait_ge(rope_products, n + 1)
                    wait(act, qk_turned, n - 3)
                    wait(act, slot_mixed, n - 3)
                    act.activation(qk[:, q, :, NROT:D], bank[n % 2][:, D:2 * D].rearrange("p (h d) -> p h d", h=2),
                                   ACT.Copy, scale=1.0 / WS)
                    act.activation(vv[:, q, :], bank[n % 2][:, 2 * D:3 * D], ACT.Copy, scale=1.0 / WS)
                    act.activation(lsl[:, q:q + 1], bank[n % 2][:, 3 * D:3 * D + 1], ACT.Exp, scale=-1.0 / WS).then_inc(rows_out, 1)
                elif stage == "turn_out":
                    act.wait_ge(qk_turned, n + 1)
                    wait(act, slot_scores, n - 3)
                    act.activation(qkt[:, q, :], bank[2 + n % 2][:, 0:2 * P], ACT.Copy, scale=D ** -0.25).then_inc(qk_turned_out, 1)
                elif stage == "exp":
                    act.wait_ge(slot_max, n + 1)
                    wait(act, slot_exp_turned, n - 3)
                    act.activation(esl[:, q, :], bank[4 + n % 2][:, 0:P], ACT.Exp, bias=nms[:, q:q + 1],
                                   accum_out=zsl[:, q:q + 1]).then_inc(slot_exp, 1)
                elif stage == "et_out":
                    act.wait_ge(slot_exp_turned, n + 1)
                    wait(act, slot_mixed, n - 3)
                    act.activation(etl[:, q, :], bank[4 + n % 2][:, P:2 * P], ACT.Copy).then_inc(slot_exp_out, 1)
                elif stage == "high" and q == 3:
                    g = n // 4
                    act.wait_ge(slot_mixed, n + 1)
                    act.activation(yh[:, g, :, :].rearrange("p b d -> p (b d)"), bank[6 + g % 2][:, :], ACT.Copy).then_inc(mixed_high, 1)
            for stage, t in skewed(NT, C_EVERY, C_ACT):
                b = t // T
                if stage == "chunk" and EARLY + t < CHUNKS:
                    split_high(EARLY + t)
                elif stage == "keys_out" and t == 0:
                    for c in range(B):
                        act.wait_ge(wqk1_made, c + 1)
                        act.activation(a1[:, c, :], bank[4 + c % 2][:, :], ACT.Copy).then_inc(wqk1_out, 1)
                elif stage == "norm" and t % T == 0:
                    normalise(b, pre1_rstd, pre1_normed)
                elif stage == "norm2" and t % T == T - 1:
                    normalise(b, ffn_rstd, ffn_normed)
                elif stage == "ont":
                    act.wait_ge(cross1_turned, t + 1)
                    wait(act, cross1_projected, t - 1)
                    act.activation(ont[:, t % 2, :], bank[4][:, 0:P], ACT.Copy).then_inc(cross1_turned_out, 1)
                elif stage == "e1t":
                    act.wait_ge(cross1_exp_turned, t + 1)
                    wait(act, cross1_mixed, t - 1)
                    act.activation(e1t[:, t % 2, :], bank[2][:, :], ACT.Copy).then_inc(cross1_exp_out, 1)
                elif stage == "exp":
                    act.wait_ge(cross1_shifted, t + 1)
                    act.activation(e1[:, t % 2, :], e1[:, t % 2, :], ACT.Exp, scale=HD ** -0.5).then_inc(cross1_exp, 1)
                elif stage == "xt_out":
                    act.wait_ge(pre1_turned, t + 1)
                    wait(act, cross1_scores, t - 1)
                    act.activation(xtc[:, t % 2, :], bank[0][:, 0:P], ACT.Copy).then_inc(pre1_turned_out, 1)
                elif stage == "high" and t % T == T - 1:
                    act.wait_ge(ffn_affine, b + 1)
                    act.activation(pay[:, b * T:(b + 1) * T, 0:D // 2].bitcast(F16), xh[:, b * T:(b + 1) * T, :],
                                   ACT.Copy).then_inc(ffn_high, 1)
                elif stage == "turn_out" and t % T == T - 1:
                    for h in range(2):
                        act.wait_ge(ffn_turned, 2 * b + h + 1)
                        act.activation(ntt[:, h, b * S:(b + 1) * S], bank[6 + h][:, :], ACT.Copy).then_inc(ffn_turned_out, 1)
                elif stage == "exp_logits" and t % T == T - 1:
                    act.wait_ge(route_shifted, b + 1)
                    act.activation(prob[:, b * T:(b + 1) * T, :], prob[:, b * T:(b + 1) * T, :], ACT.Exp,
                                   scale=1.0 / WS).then_inc(route_exp, 1)
            act.wait_ge(top2_difference, 1)
            act.activation(gexp[:, :], gexp[:, :], ACT.Exp).then_inc(top2_exp, 1)

            nc.scalar.preload_act_table(ACT.Silu)

            def shared_act(b0, b1):
                for b in range(b0, b1 + 1):
                    if b > b0:
                        act.wait_ge(sh_hidden, b)
                        act.activation(hsp[:, (b - 1) % 2, 0:S], hs[:, 2 + (b - 1) % 2, :], ACT.Copy).then_inc(sh_high, 1)
                    if b < b1:
                        act.wait_ge(sh_gate_up, 2 * b + 1)
                        wait(act, sh_hidden, b - 1)
                        act.activation(hs[:, b % 2, :], bank[2 * (b % 2)][:, :], ACT.Silu, scale=1.0 / WS).then_inc(sh_silu, 1)

            shared_act(0, SH)
            def step_act(s, u):
                static = isinstance(s, int)
                if not static or 0 <= s + 2 < TILES:
                    act.wait_ge(hidden_done, s + 3)
                    wait(act, hidden_turned, s + 1)
                    act.activation(hsplit[:, u % 2, 0:FF], hid[:, u % 2, :], ACT.Copy).then_inc(hidden_high, 1)
                if not static or 0 <= s + 3 < TILES:
                    act.wait_ge(gate_up_made, s + 4)
                    wait(act, hidden_done, s + 2)
                    v = (u + 3) % 2
                    act.activation(sil[:, v, :], bank[2 * v][:, 0:FF], ACT.Silu, scale=1.0 / WS).then_inc(silu_done, 1)
                if not static or 0 <= s + 1 < TILES:
                    act.wait_ge(hidden_turned, s + 2)
                    wait(act, down_made, s)
                    act.activation(hidt[:, (u + 1) % 2, :], ht_ps, ACT.Copy).then_inc(hidden_turned_out, 1)

            for s in range(-4, 8):
                step_act(s, s % 4)
            with act.Fori(2, TILES // 4 - 1) as i:
                for u in range(4):
                    step_act(4 * i + u, u)
            for s in range(TILES - 4, TILES + 1):
                step_act(s, s % 4)
            act.wait_ge(hidden_low, TILES)
            act.wait_ge(down_made, TILES)
            shared_act(SH, B)
            act.wait_ge(gates_done, 1)
            act.wait_ge(x_loaded[B - 1], 32)
            for c in range(2):
                for t in range((B - 1) * T, NT):
                    last = act.activation(yk[:, t, c * D:(c + 1) * D], yk[:, t, c * D:(c + 1) * D], ACT.Copy,
                                          scale=gate[:, t, c:c + 1])
                last.then_inc(last_gated, 1)

        @block.gpsimd
        def _(pool):
            links = [0]

            def link(ins):
                links[0] += 1
                ins.then_inc(g_link, 1)
                pool.wait_ge(g_link, links[0])

            def bcp(ap, n):
                p, a = ap.shape
                return ap.rearrange("p (a o) -> p a o", o=1).to_broadcast((p, a, n))

            link(pool.memset(mhalf[:, :], -0.5))

            def rstd_of(b, ready, done):
                n = slice(b * T, (b + 1) * T)
                pool.wait_ge(ready, b + 1)
                pool.tensor_scalar(nmr[:, n], mv[:, n, 0], -1.0, 0.0, ALU.mult, ALU.add)
                link(pool.tensor_scalar(ve[:, n], mv[:, n, 1], LN_EPS, 1.0, ALU.add, ALU.mult))
                link(pool.tensor_tensor(rstd[:, n], ve[:, n], mhalf[:, n], ALU.pow))
                pool.tensor_tensor(nmr[:, n], nmr[:, n], rstd[:, n], ALU.mult).then_inc(done, 1)

            def split_low(i):
                pool.wait_ge(w_high_done, i + 1)
                n = min(CH, W_END - i * CH)
                r = slice(i % WRING * CH, i % WRING * CH + n)
                c = slice(i * CH, i * CH + n)
                pool.tensor_tensor(wl[:, c], wf[:, r], wh[:, c], ALU.subtract).then_inc(w_low_done, 1)

            for stage, b in skewed(B, A_EVERY, A_POOL):
                n = slice(b * T, (b + 1) * T)
                if stage == "rstd":
                    rstd_of(b, pre0_stats, pre0_rstd)
                elif stage == "rstd2":
                    rstd_of(b, sel_stats, sel_rstd)
                elif stage == "low":
                    pool.wait_ge(sel_high, b + 1)
                    pool.tensor_tensor(xs[:, 1, n, :], xh[:, n, :], xs[:, 0, n, :], ALU.subtract).then_inc(sel_low, 1)
            pool.wait_ge(layer1_loaded, 128)
            link(pool.tensor_copy(maskf[:, :, :], mask8[:, :, :]))
            pool.tensor_scalar(maskbf[:, :, :], maskf[:, :, :], -1.0, 1e9, ALU.add, ALU.mult).then_inc(mask_done, 1)
            pool.wait_ge(vwo_scaled, 4)
            pool.tensor_tensor(vwl[:, :, :], vwf[:, :, :], vwh[:, :, :], ALU.subtract).then_inc(vwo_split, 1)
            for i in range(EARLY):
                split_low(i)
            pool.wait_ge(v1_out, 1)
            for b in range(B):
                pool.tensor_tensor(vblk[:, b, :, 0:HD], vrep[:, b, :].rearrange("p (h d) -> p h d", d=HD),
                                   bcp(c32[:, C_HR:C_HR + H], HD), ALU.mult)
                pool.tensor_copy(vblk[:, b, :, HD], c32[:, C_HR:C_HR + H]).then_inc(v_blocks_done, 1)
            for n in range(NX):
                q = n % 4
                pool.wait_ge(rope_products, n + 1)
                wait(pool, qk_turned, n - 3)
                pool.tensor_tensor(qk[:, q, :, 0:NROT], rpa[:, q, :, :], rpb[:, q, :, :], ALU.add).then_inc(rope_done, 1)
            pool.wait_ge(gathered, B)
            pool.wait_ge(one_hot_turned, NT)
            pool.wait_ge(k1_out, 1)
            for b in range(B):
                pool.tensor_tensor(kbl[:, b, :].rearrange("p (h k) -> p h k", k=KC),
                                   k1t[:, b, :].rearrange("p (a k) -> p a k", a=1).to_broadcast((P, H, KC)),
                                   bcp(c32[:, C_HM:C_HM + H], KC), ALU.mult).then_inc(k_blocks_done, 1)

            def send_rows(b, tiles_of_b):
                for t in tiles_of_b:
                    for c in range(2):
                        pool.indirect_dma_start(disp, bass.IndirectOffsetOnAxis(slot[:, b * T + t, c:c + 1].bitcast(U32), 0),
                                                pay[:, b * T + t, :], None).then_inc(sent, 16)

            for stage, t in skewed(NT, C_EVERY, C_POOL):
                b = t // T
                if stage == "rstd" and t % T == 0:
                    rstd_of(b, pre1_stats, pre1_rstd)
                elif stage == "low" and EARLY + t < CHUNKS:
                    split_low(EARLY + t)
                elif stage == "rstd2" and t % T == T - 1:
                    rstd_of(b, ffn_stats, ffn_rstd)
                elif stage == "send" and t % T == T - 1:
                    pool.wait_ge(slots_ready, b + 1)
                    pool.wait_ge(ffn_high, b + 1)
                    pool.wait_ge(ffn_low, b + 1)
                    send_rows(b, range(T // 2))
                elif stage == "send2" and t % T == T - 1:
                    send_rows(b, range(T // 2, T))

            due = pool.alloc_register("tiles_due")
            pool.reg_mov(due, 1)
            with pool.Fori(0, TILES // 4):
                for r in range(4):
                    pool.wait_ge(rows_ready, due)
                    pool.reg_add(due, due, 1)
                    pool.indirect_dma_start(ytok, bass.IndirectOffsetOnAxis(dst[:, r:r + 1].bitcast(U32), 0),
                                            yv[:, r, :], None).then_inc(rows_sent[r], 16)
            pool.wait_ge(sh_added, B)
            n = slice((B - 1) * T, NT)
            for c in range(2):
                pool.wait_ge(last_gated, c + 1)
                if c == 1:
                    pool.wait_ge(last_added, 1)
                pool.tensor_tensor(x[:, n, :], x[:, n, :], yk[:, n, c * D:(c + 1) * D], ALU.add).then_inc(last_added, 1)

        @block.vector
        def _(dve):
            links = [0]

            def link(ins):
                links[0] += 1
                ins.then_inc(v_link, 1)
                dve.wait_ge(v_link, links[0])

            def norm_stats(b, done):
                for t in range(b * T, (b + 1) * T):
                    last = dve.bn_stats(st[:, t, :], x[:, t, :])
                link(last)
                for t in range(b * T, (b + 1) * T):
                    last = dve.bn_aggr(mv[:, t, :], st[:, t, :])
                last.then_inc(done, 1)

            def bc(ap, n):
                p, a = ap.shape
                return ap.rearrange("p (a o) -> p a o", o=1).to_broadcast((p, a, n))

            for stage, b in skewed(B, A_EVERY, A_DVE):
                if stage == "stats":
                    dve.wait_ge(x_loaded[b], 16)
                    norm_stats(b, pre0_stats)
                elif stage == "shift":
                    s3 = bank[2][:, 0:T * KC].rearrange("p (t k) -> p t k", k=KC)
                    dve.wait_ge(cross0_scores, b + 1)
                    link(dve.tensor_reduce(nm[:, b, :], s3, AX.X, ALU.max, negate=True))
                    dve.tensor_tensor(es[:, b, :, :], s3, bc(nm[:, b, :], KC), ALU.add).then_inc(cross0_shifted, 1)
                elif stage == "sum":
                    dve.wait_ge(cross0_exp, b + 1)
                    link(dve.tensor_reduce(zs[:, b, :], es[:, b, :, :], AX.X, ALU.add))
                    link(dve.reciprocal(rz[:, b, :], zs[:, b, :]))
                    if b == 0:
                        dve.wait_ge(tanh_done, 1)
                    link(dve.tensor_scalar(rz[:, b, :], rz[:, b, :], tg[:, 0:1], None, ALU.mult))
                elif stage == "add":
                    dve.wait_ge(cross0_mixed, b + 1)
                    for t in range(T):
                        last = dve.scalar_tensor_tensor(x[:, b * T + t, :], bank[4 + b % 2][:, t * D:(t + 1) * D],
                                                        rz[:, b, t:t + 1], x[:, b * T + t, :], ALU.mult, ALU.add)
                    link(last)
                    norm_stats(b, sel_stats)
                elif stage == "logits_out":
                    dve.wait_ge(sel_logits, b + 1)
                    dve.tensor_copy(lg[:, :, b, :], bank[6][:, 0:T * E].rearrange("p (t e) -> p t e", e=E)).then_inc(sel_logits_out, 1)

            dve.memset(ones32, 1.0)
            dve.wait_ge(logit_rows, 1)
            link(dve.tensor_copy(work, bank[0][0:B * E, :]))
            for _ in range(J // 8):
                link(dve.max(top8[:, :], work))
                link(dve.match_replace(work, top8[:, :], work, TOPV))
            link(dve.tensor_scalar(sel, work, TOPV, None, ALU.is_equal))
            link(dve.tensor_tensor_scan(scan, ones32, sel, 0.0, ALU.mult, ALU.add))
            dve.tensor_tensor(sel, scan, sel, ALU.mult).then_inc(slot_rows_made, 1)
            dve.wait_ge(slot_rows_turned, 1)
            link(dve.tensor_copy(pos[:, :, :, :].rearrange("p t b e -> p (t b e)"), bank[1][:, 0:P]))
            iota = c16[:, G_IOTA:G_IOTA + J].rearrange("p (a j) -> p a j", a=1).to_broadcast((P, E, J))
            dve.wait_ge(c16_loaded, 32)
            for b in range(B):
                for t in range(T):
                    dve.tensor_tensor(pick[:, b * T + t, :].rearrange("p (e j) -> p e j", j=J), iota,
                                      bc(pos[:, t, b, :], J), ALU.is_equal).then_inc(one_hot_made, 1)
                if b >= 1:
                    dve.wait_ge(gathered, b)
                    dve.tensor_copy(trg[:, :, b - 1, :], bank[3 * ((b - 1) % 2) + 2][:, :].rearrange("p (e j) -> p e j", j=J)
                                    ).then_inc(trig_out, 1)
            dve.wait_ge(gathered, B)
            dve.tensor_copy(trg[:, :, B - 1, :], bank[5][:, :].rearrange("p (e j) -> p e j", j=J)).then_inc(trig_out, 1)
            dve.wait_ge(layer1_loaded, 128)
            dve.wait_ge(mask_done, 1)
            link(dve.tensor_reduce(anyk[:, :], maskf[:, :, :], AX.X, ALU.max))
            for q in range(4):
                dve.wait_ge(tables_made, q + 1)
                dve.tensor_scalar(tab[:, 2 * q:2 * q + 2, :, :].rearrange("p e h d -> p (e h d)"), bank[q][:, :],
                                  1.0 / WS, None, ALU.mult).then_inc(tables_out, 1)

            half = NROT // 2
            for stage, n in skewed(NX, X_EVERY, X_DVE):
                q = n % 4
                if stage == "rotate":
                    e, h = n // 2, n % 2
                    src = bank[n % 2][:, 0:D].rearrange("p (h d) -> p h d", h=2)

                    def table(c0, w):
                        return tab[:, e:e + 1, h, c0:c0 + w].to_broadcast((P, 2, w))

                    dve.wait_ge(qkv_made, n + 1)
                    wait(dve, rope_done, n - 3)
                    dve.tensor_tensor(rpa[:, q, :, :], src, table(0, NROT), ALU.mult)
                    dve.tensor_tensor(rpb[:, q, :, 0:half], src[:, :, half:NROT], table(NROT, half), ALU.mult)
                    dve.tensor_tensor(rpb[:, q, :, half:NROT], src[:, :, 0:half], table(NROT + half, half),
                                      ALU.mult).then_inc(rope_products, 1)
                elif stage == "max":
                    dve.wait_ge(slot_scores, n + 1)
                    wait(dve, slot_exp, n - 3)
                    dve.tensor_reduce(nms[:, q:q + 1], bank[4 + n % 2][:, 0:P], AX.X, ALU.max, negate=True).then_inc(slot_max, 1)
                elif stage == "scale":
                    dve.wait_ge(slot_exp, n + 1)
                    dve.wait_ge(rows_out, n + 1)
                    link(dve.scalar_tensor_tensor(den[:, q:q + 1], lsl[:, q:q + 1], 1.0, zsl[:, q:q + 1], ALU.add, ALU.mult))
                    link(dve.reciprocal(rzs[:, q:q + 1], den[:, q:q + 1]))
                    dve.tensor_scalar(esl[:, q, :], esl[:, q, :], rzs[:, q:q + 1], None, ALU.mult).then_inc(slot_scaled, 1)
                elif stage == "low" and q == 3:
                    g = n // 4
                    dve.wait_ge(mixed_high, g + 1)
                    dve.tensor_tensor(yl[:, g, :, :].rearrange("p b d -> p (b d)"), bank[6 + g % 2][:, :],
                                      yh[:, g, :, :].rearrange("p b d -> p (b d)"), ALU.subtract).then_inc(mixed_low, 1)

            dve.memset(base[:, 0, :], 0.0)
            dve.memset(onee[:, :], 1.0)
            link(dve.tensor_scalar(tgw[:, :], tg[:, 3:4], 1.0 / WS, None, ALU.mult))
            link(dve.tensor_scalar(router16[:, 0, :], router[:, :], WS, None, ALU.mult))
            dve.scalar_tensor_tensor(router16[:, 1, :], router[:, :], WS, router16[:, 0, :], ALU.mult,
                                     ALU.subtract).then_inc(router_split, 1)
            dve.tensor_copy(pay[:, :, D], c32[:, C_2T:C_2T + NT])
            dve.memset(pay[:, :, D + 2], 0.0)
            for stage, t in skewed(NT, C_EVERY, C_DVE):
                b = t // T
                n = slice(b * T, (b + 1) * T)
                if stage == "residual" and t % T == 0:
                    dve.wait_ge(scattered, b + 1)
                    xf32 = x[:, n, :].rearrange("p t d -> p (t d)")
                    link(dve.scalar_tensor_tensor(xf32, bank[6 + b % 2][:, :], tg[:, 2:3], xf32, ALU.mult, ALU.add))
                    norm_stats(b, pre1_stats)
                elif stage == "shift":
                    s3 = bank[1][:, :].rearrange("p (h k) -> p h k", k=KC)
                    dve.wait_ge(cross1_scores, t + 1)
                    link(dve.tensor_reduce(nm1[:, t % 2, :], s3, AX.X, ALU.max, negate=True))
                    wait(dve, cross1_exp_turned, t - 1)
                    dve.tensor_tensor(e1[:, t % 2, :].rearrange("p (h k) -> p h k", k=KC), s3, bc(nm1[:, t % 2, :], KC),
                                      ALU.add).then_inc(cross1_shifted, 1)
                elif stage == "over_sum":
                    o9 = bank[3][:, 0:H * (HD + 1)].rearrange("p (h d) -> p h d", d=HD + 1)
                    z = zi[:, t % 2, :]
                    dve.wait_ge(cross1_mixed, t + 1)
                    link(dve.reciprocal(z, o9[:, :, HD]))
                    wait(dve, cross1_turned, t - 1)
                    dve.scalar_tensor_tensor(on[:, t % 2, :].rearrange("p (h d) -> p h d", d=HD), o9[:, :, 0:HD],
                                             anyk[:, t % T:t % T + 1], bc(z, HD), ALU.mult, ALU.mult).then_inc(cross1_over_sum, 1)
                elif stage == "add":
                    dve.wait_ge(cross1_projected, t + 1)
                    dve.scalar_tensor_tensor(x[:, t, :], bank[5][:, 0:D], tg[:, 1:2], x[:, t, :], ALU.mult,
                                             ALU.add).then_inc(cross1_added, 1)
                    dve.wait_ge(cross1_added, t + 1)
                    last = dve.bn_stats(st[:, t, :], x[:, t, :])
                    if t % T == T - 1:
                        link(last)
                        for u in range(t - T + 1, t + 1):
                            last = dve.bn_aggr(mv[:, u, :], st[:, u, :])
                        last.then_inc(ffn_stats, 1)
                elif stage == "affine" and t % T == T - 1:
                    dve.wait_ge(ffn_normed, b + 1)
                    link(dve.tensor_tensor(xh[:, n, :], xh[:, n, :],
                                           gamma[:, :].rearrange("p (a d) -> p a d", a=1).to_broadcast((P, T, D)), ALU.mult))
                    dve.tensor_tensor(xh[:, n, :], xh[:, n, :],
                                      beta[:, :].rearrange("p (a d) -> p a d", a=1).to_broadcast((P, T, D)),
                                      ALU.add).then_inc(ffn_affine, 1)
                elif stage == "low" and t % T == T - 1:
                    dve.wait_ge(ffn_high, b + 1)
                    dve.tensor_tensor(pay[:, n, D // 2:D].bitcast(F16), xh[:, n, :], pay[:, n, 0:D // 2].bitcast(F16),
                                      ALU.subtract).then_inc(ffn_low, 1)
                elif stage == "shift_logits" and t % T == T - 1:
                    l3 = bank[6][:, 0:T * E].rearrange("p (t e) -> p t e", e=E)
                    dve.wait_ge(route_logits, b + 1)
                    link(dve.tensor_reduce(rmax[:, :], l3, AX.X, ALU.max, negate=True))
                    dve.tensor_tensor(prob[:, n, :], l3, bc(rmax[:, :], E), ALU.add).then_inc(route_shifted, 1)
                elif stage == "route" and t % T == T - 1:
                    dve.wait_ge(route_exp, b + 1)
                    for u in range(b * T, (b + 1) * T):
                        last = dve.max(rtop[:, u, :], prob[:, u, :])
                    link(last)
                    for u in range(T):
                        last = dve.max_index(ridx[:, u, :], rtop[:, b * T + u, :], prob[:, b * T + u, :])
                    link(last)
                    link(dve.tensor_copy(ef[:, :, :], ridx[:, :, 0:2]))
                    dve.tensor_copy(pay[:, n, D + 1], ef[:, :, 0])
                    link(dve.tensor_tensor(oh[:, :, :, :].rearrange("p t c e -> p (t c) e"),
                                           c32[:, C_I8:C_I8 + E].rearrange("p (a e) -> p a e", a=1).to_broadcast((P, 2 * T, E)),
                                           bc(ef[:, :, :].rearrange("p t c -> p (t c)"), E), ALU.is_equal))
                    link(dve.tensor_tensor(msel[:, n, :], oh[:, :, 0, :], oh[:, :, 1, :], ALU.add))
                    link(dve.tensor_reduce(tsum[:, :], msel[:, n, :].rearrange("p t e -> p e t"), AX.X, ALU.add))
                    dve.tensor_tensor(base[:, b + 1, :], base[:, b, :], tsum[:, :], ALU.add).then_inc(routed_marked, 1)
                elif stage == "slots" and t % T == T - 1:
                    if b == B - 1:
                        link(dve.tensor_reduce(rsum[:, :], prob[:, :, :], AX.X, ALU.add))
                        link(dve.reciprocal(rsum[:, :], rsum[:, :]))
                        link(dve.tensor_tensor(ptop[:, :, :], rtop[:, :, 0:2], bc(rsum[:, :], 2), ALU.mult))
                        dve.tensor_tensor(gexp[:, :], ptop[:, :, 1], ptop[:, :, 0], ALU.subtract).then_inc(top2_difference, 1)
                    dve.wait_ge(route_ranks, b + 1)
                    link(dve.tensor_tensor(rk[:, :, :], bank[7][:, 0:T * E].rearrange("p (t e) -> p t e", e=E),
                                           c32[:, C_EREG:C_EREG + E].rearrange("p (a e) -> p a e", a=1).to_broadcast((P, T, E)),
                                           ALU.add))
                    for c in range(2):
                        last = dve.tensor_tensor(ohr[:, :, c, :], oh[:, :, c, :], rk[:, :, :], ALU.mult)
                    link(last)
                    link(dve.tensor_reduce(slotf[:, :, :], ohr[:, :, :, :], AX.X, ALU.add))
                    dve.tensor_copy(slot[:, n, :], slotf[:, :, :]).then_inc(slots_ready, 1)

            dve.wait_ge(counts_made, 1)
            link(dve.tensor_copy(cnt[:, :], bank[6][:, 0:E]))
            dve.tensor_tensor(padr[:, :], cnt[:, :], c32[:, C_EREG:C_EREG + E], ALU.add).then_inc(tiles, 1)
            link(dve.tensor_scalar(cnti[:, :], cnt[:, :], float(P - 1), None, ALU.add))
            link(dve.tensor_scalar(cnti[:, :], cnti[:, :], 7, None, ALU.logical_shift_right))
            link(dve.tensor_copy(ntil[:, :], cnti[:, :]))
            link(dve.tensor_tensor_scan(ncum[:, :], onee[:, :], ntil[:, :], 0.0, ALU.mult, ALU.add))

            def over_tiles(v):
                return v.rearrange("p (a e) -> p a e", a=1).to_broadcast((P, TTAB, E))

            link(dve.tensor_tensor(ge[:, :, :], bc(c32[:, C_S:C_S + TTAB], E), over_tiles(ncum[:, :]), ALU.is_ge))
            link(dve.tensor_reduce(te[:, :], ge[:, :, :], AX.X, ALU.add))
            link(dve.tensor_tensor(gn[:, :, :], ge[:, :, :], over_tiles(ntil[:, :]), ALU.mult))
            link(dve.tensor_reduce(tb[:, :], gn[:, :, :], AX.X, ALU.add))
            link(dve.scalar_tensor_tensor(trow[:, :], tb[:, :], -float(P), c32[:, C_S128:C_S128 + TTAB], ALU.mult, ALU.add))
            link(dve.scalar_tensor_tensor(trow[:, :], te[:, :], float(REG), trow[:, :], ALU.mult, ALU.add))
            dve.tensor_scalar(trow_i[:, :], trow[:, :], float(E * REG), None, ALU.min).then_inc(tiles, 1)
            for h in range(2):
                last = dve.tensor_scalar(tw[:, :, 4 * h:4 * h + 4],
                                         te[:, 4 * h:4 * h + TILES].rearrange("p (i j) -> p i j", j=4),
                                         float(E - 1), None, ALU.min)
            link(last)
            link(dve.tensor_tensor(tw[:, :, :], tw[:, :, :],
                                   c32[:, C_P8:C_P8 + 8].rearrange("p (a j) -> p a j", a=1).to_broadcast((P, TILES // 4, 8)),
                                   ALU.mult))
            link(dve.tensor_reduce(tpack[:, :], tw[:, :, :], AX.X, ALU.add))
            dve.tensor_copy(te_i[:, :], tpack[:, :]).then_inc(tiles, 1)

            def shared_dve(b0, b1):
                for b in range(b0, b1 + 2):
                    if b0 + 2 <= b:
                        c = b - 2
                        xf32 = x[:, c * T:(c + 1) * T, :].rearrange("p t d -> p (t d)")
                        dve.wait_ge(sh_down, c + 1)
                        dve.scalar_tensor_tensor(xf32, bank[4 + c % 2][:, :], tgw[:, :], xf32, ALU.mult, ALU.add).then_inc(sh_added, 1)
                    if b0 + 1 <= b <= b1:
                        c = b - 1
                        dve.wait_ge(sh_high, b)
                        dve.tensor_tensor(hsp[:, c % 2, S:2 * S], hs[:, 2 + c % 2, :], hsp[:, c % 2, 0:S], ALU.subtract).then_inc(sh_low, 1)
                    if b < b1:
                        dve.wait_ge(sh_silu, b + 1)
                        dve.wait_ge(sh_gate_up, 2 * b + 2)
                        wait(dve, sh_low, b - 1)
                        dve.scalar_tensor_tensor(hs[:, 2 + b % 2, :], bank[2 * (b % 2) + 1][:, :], 1.0 / WS, hs[:, b % 2, :],
                                                 ALU.mult, ALU.mult).then_inc(sh_hidden, 1)

            shared_dve(0, SH)
            def step_dve(s, u):
                static = isinstance(s, int)
                if not static or 0 <= s + 4 < TILES:
                    dve.wait_ge(rows_loaded[u], (s + 4 - u) * 4 + 16)
                    wait(dve, dest_ready, s + 4)
                    dve.scalar_tensor_tensor(dbase[:, :], xd[:, u, D + 2:D + 3], c32[:, ds(C_S128 + s + 4, 1)],
                                             xd[:, u, D:D + 1], ALU.mult, ALU.add).then_inc(dest_base, 1)
                if not static or 0 <= s - 1 < TILES:
                    r = (u - 1) % 4
                    dve.wait_ge(down_made, s)
                    if not static or s - 1 >= 4:
                        dve.wait_ge(rows_sent[r], (s - 1 - r) * 4)
                    dve.tensor_scalar(yv[:, r, :], bank[6 + r % 2][:, 0:D], 1.0 / WS, None, ALU.mult)
                    dve.wait_ge(dest_ready, s)
                    dve.tensor_copy(dst[:, r:r + 1], dall[:, ds(s - 1, 1)]).then_inc(rows_ready, 1)
                if not static or 0 <= s + 4 < TILES:
                    dve.wait_ge(rows_turned, s + 5)
                    wait(dve, gate_up_made, s + 3)
                    dve.tensor_copy(xdt[:, u % 2, :], xt_ps).then_inc(rows_turned_out, 1)
                if not static or 0 <= s + 2 < TILES:
                    dve.wait_ge(hidden_high, s + 3)
                    dve.tensor_tensor(hsplit[:, u % 2, FF:2 * FF], hid[:, u % 2, :], hsplit[:, u % 2, 0:FF],
                                      ALU.subtract).then_inc(hidden_low, 1)
                if not static or 0 <= s + 4 < TILES:
                    dve.wait_ge(dest_base, s + 5)
                    dve.scalar_tensor_tensor(dall[:, ds(s + 4, 1)], xd[:, u, D + 1:D + 2], te[:, ds(s + 4, 1)],
                                             dbase[:, :], ALU.not_equal, ALU.add).then_inc(dest_ready, 1)
                if not static or 0 <= s + 3 < TILES:
                    v = (u + 3) % 2
                    dve.wait_ge(silu_done, s + 4)
                    dve.scalar_tensor_tensor(hid[:, v, :], bank[2 * v + 1][:, 0:FF], 1.0 / WS, sil[:, v, :],
                                             ALU.mult, ALU.mult).then_inc(hidden_done, 1)

            for s in range(-4, 8):
                step_dve(s, s % 4)
            with dve.Fori(2, TILES // 4 - 1) as i:
                for u in range(4):
                    step_dve(4 * i + u, u)
            for s in range(TILES - 4, TILES + 1):
                step_dve(s, s % 4)
            dve.wait_ge(top2_exp, 1)
            link(dve.tensor_scalar(gden[:, :], gexp[:, :], 1.0, None, ALU.add))
            link(dve.reciprocal(gden[:, :], gden[:, :]))
            dve.tensor_scalar(gate[:, :, 0], gden[:, :], tg[:, 3:4], None, ALU.mult)
            dve.scalar_tensor_tensor(gate[:, :, 1], gexp[:, :], tg[:, 3:4], gden[:, :], ALU.mult, ALU.mult).then_inc(gates_done, 1)
            dve.wait_ge(gates_done, 1)
            shared_dve(SH, B)
            for b in range(B - 1):
                dve.wait_ge(x_loaded[b], 32)
                for c in range(2):
                    for t in range(b * T, (b + 1) * T):
                        last = dve.scalar_tensor_tensor(x[:, t, :], yk[:, t, c * D:(c + 1) * D], gate[:, t, c:c + 1],
                                                        x[:, t, :], ALU.mult, ALU.add)
                    if c == 0:
                        link(last)
                last.then_inc(sum_done, 1)

        @block.tensor
        def _(pe):
            def mm(o, l, r, start=True, stop=True):
                return pe.matmul(o, l, r, start=start, stop=stop)

            pe.wait_ge(ctx_loaded, 48)
            ctxt = ctxr[:, :, 0, :]
            mm(bank[7][:, 0:B * KC], wkv0[:, 0:D], ctxt).then_inc(k0_made, 1)
            for b in range(B):
                mm(bank[6][0:KC, b * D:(b + 1) * D], ctxr[:, b, 0, :], wkv0[:, D:2 * D])
            pe.wait_ge(k0_out, 1)
            mm(bank[7][:, P:P + B * KC], wq0[:, :], k0t[:, :]).then_inc(wqk0_made, 1)

            for stage, b in skewed(B, A_EVERY, A_PE):
                n0 = b * T
                if stage == "xt":
                    pe.wait_ge(pre0_normed, b + 1)
                    pe.wait_ge(c32_loaded, 16)
                    if b >= 2:
                        pe.wait_ge(pre0_turned_out, b - 1)
                    for t in range(T):
                        last = pe.transpose(bank[b % 2][:, t * P:(t + 1) * P], xh[:, n0 + t, :], ident)
                    last.then_inc(pre0_turned, 1)
                elif stage == "scores":
                    pe.wait_ge(pre0_turned_out, b + 1)
                    pe.wait_ge(wqk0_out, 1)
                    if b >= 1:
                        pe.wait_ge(cross0_shifted, b)
                    for t in range(T):
                        last = mm(bank[2][:, t * KC:(t + 1) * KC], xt[:, b, t * P:(t + 1) * P], wk0[:, b, :])
                    last.then_inc(cross0_scores, 1)
                elif stage == "et":
                    pe.wait_ge(cross0_exp, b + 1)
                    if b >= 1:
                        pe.wait_ge(cross0_exp_out, b)
                    for t in range(T):
                        last = pe.transpose(bank[3][0:KC, t * P:(t + 1) * P], es[:, b, t, :], ident)
                    last.then_inc(cross0_exp_turned, 1)
                elif stage == "mix":
                    pe.wait_ge(cross0_exp_out, b + 1)
                    pe.wait_ge(v0_out, 1)
                    if b >= 2:
                        pe.wait_ge(sel_stats, b - 1)
                    for t in range(T):
                        last = mm(bank[4 + b % 2][:, t * D:(t + 1) * D], et0[:, b, t * P:(t + 1) * P], v0[:, b, :])
                    last.then_inc(cross0_mixed, 1)
                elif stage == "xt2":
                    pe.wait_ge(sel_normed, b + 1)
                    pe.wait_ge(pre0_turned_out, min(b + 3, B))
                    if b >= 2:
                        pe.wait_ge(sel_turned_out, b - 1)
                    for t in range(T):
                        last = pe.transpose(bank[b % 2][:, t * P:(t + 1) * P], xh[:, n0 + t, :], ident)
                    last.then_inc(sel_turned, 1)
                elif stage == "logits":
                    pe.wait_ge(sel_turned_out, b + 1)
                    pe.wait_ge(gates_loaded, 48)
                    if b >= 1:
                        pe.wait_ge(sel_logits_out, b)
                    for t in range(T):
                        last = mm(bank[6][:, t * E:(t + 1) * E], xt[:, b, t * P:(t + 1) * P], wr0[:, :])
                    last.then_inc(sel_logits, 1)

            pe.wait_ge(sel_logits_out, B)
            for t in range(T):
                last = pe.transpose(bank[0][0:B * E, t * P:(t + 1) * P], lg[:, t, :, :].rearrange("p b e -> p (b e)"), ident)
            last.then_inc(logit_rows, 1)
            pe.wait_ge(vo0_loaded, 32)
            for e in range(E):
                last = mm(bank[4 + e // 4][:, (e % 4) * D:(e % 4 + 1) * D], wv0[:, e, :], wo0[:, e, :])
                if e % 4 == 3:
                    last.then_inc(vwo_made, 1)
            pe.wait_ge(layer1_loaded, 128)
            mm(bank[2][:, 0:B * KC], wk1[:, :], ctxt)
            for b in range(B):
                last = mm(bank[3][:, b * D:(b + 1) * D], ctxr[:, b, :, :].rearrange("p r k -> p (r k)"), wv1[:, :])
            last.then_inc(kv1_made, 1)
            pe.wait_ge(slot_rows_made, 1)
            for t in range(T):
                last = pe.transpose(bank[1][:, t * B * E:(t + 1) * B * E], sel[:, t * P:(t + 1) * P], ident[0:B * E, 0:B * E])
            last.then_inc(slot_rows_turned, 1)
            pe.wait_ge(c16_loaded, 32)
            pe.wait_ge(sel_low, B)
            pe.wait_ge(vwo_scaled, 3)
            pe.wait_ge(v1_out, 1)
            for b in range(B):
                g = 3 * (b % 2)
                for t in range(T):
                    n = b * T + t
                    pe.wait_ge(one_hot_made, n + 1)
                    if t == 0 and b >= 2:
                        pe.wait_ge(gathered_out, 2 * (b - 1))
                        pe.wait_ge(trig_out, b - 1)
                    for h, lhs in ((0, xs[:, 0, n, :]), (1, xs[:, 1, n, :]), (2, c16[:, G_TRIG + t * D:G_TRIG + (t + 1) * D])):
                        last = mm(bank[g + h][:, :], lhs, pick[:, n, :], start=t == 0, stop=t == T - 1)
                    if t == T - 1:
                        last.then_inc(gathered, 1)
                    if n >= 2:
                        pe.wait_ge(one_hot_turned_out, n - 1)
                    for p in range(E // 2):
                        last = mm(bank[6 + t % 2][:, p * P:(p + 1) * P], pick[:, n, p * P:(p + 1) * P], ident16)
                    last.then_inc(one_hot_turned, 1)
            pe.wait_ge(trig_out, B)
            pe.wait_ge(gathered_out, 2 * B)
            for q in range(4):
                for u in range(4):
                    e, h = 2 * q + u // 2, u % 2
                    last = mm(bank[q][:, u * P:(u + 1) * P], trg[:, e, 2 * h:2 * h + 2, :].rearrange("p b j -> p (b j)"),
                              c16[:, G_COMB:G_COMB + P])
                last.then_inc(tables_made, 1)

            pe.wait_ge(one_hot_turned_out, NT)
            pe.wait_ge(w_low_done, 4)
            pe.wait_ge(vwo_split, 1)
            for stage, n in skewed(NX, X_EVERY, X_PE):
                q, e, h = n % 4, n // 2, n % 2
                if stage == "project":
                    if n < 2:
                        pe.wait_ge(tables_out, 4)
                    wait(pe, rows_out, n - 1)
                    xa, xb = (xg[:, i, e, 2 * h:2 * h + 2, :].rearrange("p b j -> p (b j)") for i in range(2))
                    c = slice(W_QK + 2 * D * e, W_QK + 2 * D * (e + 1))
                    for c0, w, wa, wb in ((0, 2 * D, wh[:, c], wl[:, c]), (2 * D, D + 1, vwh[:, e, :], vwl[:, e, :])):
                        o = bank[n % 2][:, c0:c0 + w]
                        mm(o, xa, wa, True, False)
                        mm(o, xa, wb, False, False)
                        last = mm(o, xb, wa, False, True)
                    last.then_inc(qkv_made, 1)
                elif stage == "turn":
                    pe.wait_ge(rope_done, n + 1)
                    pe.wait_ge(rows_out, n + 1)
                    wait(pe, qk_turned_out, n - 1)
                    for i in range(2):
                        last = pe.transpose(bank[2 + n % 2][:, i * P:(i + 1) * P], qk[:, q, i, :], ident)
                    last.then_inc(qk_turned, 1)
                elif stage == "scores":
                    pe.wait_ge(qk_turned_out, n + 1)
                    wait(pe, slot_exp_out, n - 1)
                    o = bank[4 + n % 2][:, 0:P]
                    mm(o, identbf, causal, True, False)
                    mm(o, qkt[:, q, 0:P], qkt[:, q, P:2 * P], False, True).then_inc(slot_scores, 1)
                elif stage == "et":
                    pe.wait_ge(slot_scaled, n + 1)
                    pe.transpose(bank[4 + n % 2][:, P:2 * P], esl[:, q, :], ident).then_inc(slot_exp_turned, 1)
                elif stage == "mix":
                    g = n // 4
                    pe.wait_ge(slot_exp_out, n + 1)
                    if q == 0:
                        wait(pe, mixed_low, g - 1)
                    for i in range(2):
                        b = 2 * h + i
                        last = mm(bank[6 + g % 2][J * (e % 2):J * (e % 2 + 1), b * D:(b + 1) * D],
                                  etl[:, q, i * J:(i + 1) * J], vv[:, q, :])
                    last.then_inc(slot_mixed, 1)

            pe.wait_ge(mask_done, 1)
            pe.wait_ge(v_blocks_done, B)
            pe.wait_ge(mixed_low, E // 2)
            for stage, t in skewed(NT, C_EVERY, C_PE):
                b = t // T
                if stage == "scatter" and t % T == 0:
                    wait(pe, pre1_stats, b - 1)
                    for u in range(T):
                        o = bank[6 + b % 2][:, u * D:(u + 1) * D]
                        for g in range(E // 2):
                            mm(o, pickt[:, t + u, g, :], yh[:, g, b, :], g == 0, False)
                            last = mm(o, pickt[:, t + u, g, :], yl[:, g, b, :], False, g == E // 2 - 1)
                    last.then_inc(scattered, 1)
                elif stage == "keys" and t == 0:
                    pe.wait_ge(slot_exp_out, NX)
                    for c in range(B):
                        pe.wait_ge(k_blocks_done, c + 1)
                        wait(pe, wqk1_out, c - 1)
                        mm(bank[4 + c % 2][:, :], wq1[:, :], kbl[:, c, :]).then_inc(wqk1_made, 1)
                elif stage == "w":
                    pe.wait_ge(cross1_turned_out, t + 1)
                    wait(pe, cross1_added, t)
                    mm(bank[5][:, 0:D], ont[:, t % 2, :], wo1[:, :]).then_inc(cross1_projected, 1)
                elif stage == "ot":
                    pe.wait_ge(cross1_over_sum, t + 1)
                    wait(pe, cross1_turned_out, t)
                    pe.transpose(bank[4][:, 0:P], on[:, t % 2, :], ident).then_inc(cross1_turned, 1)
                elif stage == "pv":
                    pe.wait_ge(cross1_exp_out, t + 1)
                    wait(pe, cross1_over_sum, t)
                    for c in range(NC):
                        n = HC * (HD + 1)
                        last = mm(bank[3][:, c * n:(c + 1) * n], e1t[:, t % 2, c * P:(c + 1) * P],
                                  vblk[:, t // T, c * HC:(c + 1) * HC, :].rearrange("p h d -> p (h d)"))
                    last.then_inc(cross1_mixed, 1)
                elif stage == "et":
                    pe.wait_ge(cross1_exp, t + 1)
                    wait(pe, cross1_exp_out, t)
                    for c in range(NC):
                        last = pe.transpose(bank[2][:, c * P:(c + 1) * P], e1[:, t % 2, c * P:(c + 1) * P], ident)
                    last.then_inc(cross1_exp_turned, 1)
                elif stage == "scores":
                    pe.wait_ge(pre1_turned_out, t + 1)
                    pe.wait_ge(wqk1_out, B)
                    wait(pe, cross1_shifted, t)
                    mm(bank[1][:, :], identbf, maskbf[:, t % T:t % T + 1, :].to_broadcast((P, H, KC)), True, False)
                    mm(bank[1][:, :], xtc[:, t % 2, :], a1[:, t // T, :], False, True).then_inc(cross1_scores, 1)
                elif stage == "xt":
                    pe.wait_ge(pre1_normed, t // T + 1)
                    wait(pe, pre1_turned_out, t)
                    pe.transpose(bank[0][:, 0:P], xh[:, t, :], ident).then_inc(pre1_turned, 1)
                elif stage == "turn" and t % T == T - 1:
                    wait(pe, slots_ready, b)
                    wait(pe, routed_marked, b)
                    pe.wait_ge(pre1_stats, B)
                    for h, s in ((0, ffn_high), (1, ffn_low)):
                        pe.wait_ge(s, b + 1)
                        for u in range(T):
                            w = pay[:, b * T + u, h * (D // 2):(h + 1) * (D // 2)].bitcast(F16)
                            last = mm(bank[6 + h][:, u * P:(u + 1) * P], w, ident16)
                        last.then_inc(ffn_turned, 1)
                elif stage == "logits" and t % T == T - 1:
                    pe.wait_ge(ffn_turned_out, 2 * b + 2)
                    pe.wait_ge(router_split, 1)
                    for u in range(T):
                        c = slice(b * S + u * P, b * S + (u + 1) * P)
                        o = bank[6][:, u * E:(u + 1) * E]
                        mm(o, ntt[:, 0, c], router16[:, 0, :], True, False)
                        mm(o, ntt[:, 0, c], router16[:, 1, :], False, False)
                        last = mm(o, ntt[:, 1, c], router16[:, 0, :], False, True)
                    last.then_inc(route_logits, 1)
                elif stage == "rank" and t % T == T - 1:
                    pe.wait_ge(routed_marked, b + 1)
                    tri, one = c16[:, G_TRI:G_TRI + P], c16[:, G_ONE:G_ONE + P]
                    for u in range(T):
                        o = bank[7][:, u * E:(u + 1) * E]
                        mm(o, tri, msel[:, b * T + u, :], True, False)
                        for v in range(u):
                            mm(o, one, msel[:, b * T + v, :], False, False)
                        last = mm(o, one, base[:, b, :], False, True)
                    last.then_inc(route_ranks, 1)
                    if b == B - 1:
                        mm(bank[6][:, 0:E], one, base[:, B, :]).then_inc(counts_made, 1)

            def shared_pe(b0, b1):
                for b in range(b0, b1 + 1):
                    if b < b1:
                        wait(pe, sh_hidden, b - 1)
                        for c in range(2):
                            w = slice(W_SG + c * D, W_SG + (c + 1) * D)
                            o, n = bank[2 * (b % 2) + c][:, :], slice(b * S, (b + 1) * S)
                            mm(o, wh[:, w], ntt[:, 0, n], True, False)
                            mm(o, wh[:, w], ntt[:, 1, n], False, False)
                            mm(o, wl[:, w], ntt[:, 0, n], False, True).then_inc(sh_gate_up, 1)
                    if b > b0:
                        c = b - 1
                        pe.wait_ge(sh_low, b)
                        wait(pe, sh_added, c - 1)
                        for t in range(T):
                            o = bank[4 + c % 2][:, t * D:(t + 1) * D]
                            hi = hsp[:, c % 2, t * P:(t + 1) * P]
                            lo = hsp[:, c % 2, S + t * P:S + (t + 1) * P]
                            mm(o, hi, wh[:, W_SD:W_SD + D], True, False)
                            mm(o, hi, wl[:, W_SD:W_SD + D], False, False)
                            last = mm(o, lo, wh[:, W_SD:W_SD + D], False, True)
                        last.then_inc(sh_down, 1)

            pe.wait_ge(w_low_done, CHUNKS)
            shared_pe(0, SH)
            window = pe.alloc_register("window")

            def load_window(i):
                pe.reg_load(window, te_i[0:1, ds(i, 1)])

            def experts():
                word = pe.snap(window, min_val=0, max_val=8 ** 8 - 1)
                return [(word >> (3 * j)) & (E - 1) for j in range(8)]

            gu_w = [w[:, W_GU:W_DN].rearrange("p (e n) -> p e n", e=E) for w in (wh, wl)]
            dn_w = [w[:, W_DN:W_SG].rearrange("p (e n) -> p e n", e=E) for w in (wh, wl)]

            def step_pe(s, u, expert, expert3):
                static = isinstance(s, int)
                if not static or 0 <= s + 4 < TILES:
                    pe.wait_ge(rows_loaded[u], (s + 4 - u) * 4 + 16)
                    wait(pe, rows_turned_out, s + 4)
                    for h in range(2):
                        w = xd[:, u, h * (D // 2):(h + 1) * (D // 2)].bitcast(F16)
                        last = pe.transpose(xt_ps[:, h * P:(h + 1) * P], w, ident16)
                    last.then_inc(rows_turned, 1)
                if not static or 0 <= s + 3 < TILES:
                    pe.wait_ge(rows_turned_out, s + 4)
                    wait(pe, hidden_done, s + 2)
                    v = (u + 3) % 2
                    xa, xb = xdt[:, v, 0:P], xdt[:, v, P:2 * P]
                    for i in range(2):
                        o = bank[2 * v + i][:, 0:FF]
                        wa, wb = (w[:, ds(expert3, 1), i * FF:(i + 1) * FF].rearrange("p e n -> p (e n)") for w in gu_w)
                        mm(o, xa, wa, True, False)
                        mm(o, xa, wb, False, False)
                        last = mm(o, xb, wa, False, True)
                    last.then_inc(gate_up_made, 1)
                if not static or 0 <= s + 1 < TILES:
                    pe.wait_ge(hidden_low, s + 2)
                    wait(pe, hidden_turned_out, s + 1)
                    for i in range(2 * FC):
                        last = pe.transpose(ht_ps[:, i * P:(i + 1) * P], hsplit[:, (u + 1) % 2, i * P:(i + 1) * P], ident16)
                    last.then_inc(hidden_turned, 1)
                if not static or 0 <= s < TILES:
                    pe.wait_ge(hidden_turned_out, s + 1)
                    wait(pe, rows_ready, s - 1)
                    o = bank[6 + u % 2][:, 0:D]
                    for i in range(FC):
                        wa, wb = (w[:, ds(expert, 1), i * D:(i + 1) * D].rearrange("p e n -> p (e n)") for w in dn_w)
                        hi = hidt[:, u % 2, i * P:(i + 1) * P]
                        lo = hidt[:, u % 2, FF + i * P:FF + (i + 1) * P]
                        mm(o, hi, wa, i == 0, False)
                        mm(o, hi, wb, False, False)
                        last = mm(o, lo, wa, False, i == FC - 1)
                    last.then_inc(down_made, 1)

            pe.wait_ge(tiles, 3)
            load_window(0)
            e = experts()
            load_window(1)
            for s in range(-4, 4):
                step_pe(s, s % 4, e[max(s, 0)], e[max(s + 3, 0)])

            def round_pe(i, ahead):
                e = experts()
                for u in range(4 if ahead else 5):
                    step_pe(4 * i + u, u % 4, e[u], e[u + 3])
                    if ahead and u == 1:
                        load_window(i + 1)

            round_pe(1, True)
            with pe.Fori(2, TILES // 4 - 1) as i:
                round_pe(i, True)
            round_pe(TILES // 4 - 1, False)
            pe.wait_ge(hidden_done, TILES)
            pe.wait_ge(rows_turned_out, TILES)
            pe.wait_ge(hidden_turned_out, TILES)
            shared_pe(SH, B)


def constants():
    p = np.arange(P)
    c32 = np.zeros((P, C_END), np.float32)
    c32[:, C_ID:C_ID + P] = np.eye(P)
    c32[:, C_HM:C_HM + H] = p[:, None] // HD == np.arange(H)
    c32[:, C_HR:C_HR + H] = p[:, None] // KC == np.arange(H) % HC
    c32[:, C_S:C_S + TTAB] = np.arange(TTAB)
    c32[:, C_S128:C_S128 + TTAB] = P * np.arange(TTAB)
    c32[:, C_EREG:C_EREG + E] = REG * np.arange(E)
    c32[:, C_I8:C_I8 + E] = np.arange(E)
    c32[:, C_2T:C_2T + NT] = 2 * (p[:, None] + P * np.arange(NT))
    c32[:, C_P8:C_P8 + 8] = 8.0 ** np.arange(8)
    half = NROT // 2
    inv = (1.0 / 10000.0 ** (np.arange(half, dtype=np.float32) * np.float32(2.0) / np.float32(NROT))).astype(np.float32)
    ang = np.arange(S, dtype=np.float32)[:, None] * inv
    trig = np.zeros((S, 4 * half), np.float16)
    for i, f in enumerate((np.cos, np.sin)):
        v = f(ang.astype(np.float64)).astype(np.float32)
        hi = v.astype(np.float16)
        trig[:, 2 * i * half:(2 * i + 1) * half] = hi
        trig[:, (2 * i + 1) * half:(2 * i + 2) * half] = v - hi.astype(np.float32)
    c16 = np.zeros((P, G_END), np.float16)
    c16[:, G_ID:G_ID + P] = np.eye(P)
    c16[:, G_IOTA:G_IOTA + J] = 1 + np.arange(J)
    c16[:, G_TRIG:G_TRIG + S] = trig.reshape(T, P, P).transpose(1, 0, 2).reshape(P, S)
    r = p % half
    comb = np.zeros((P, P))
    for c in range(P):
        kind, f = c // half, c % half
        comb[:, c] = (r == f) * (p // (2 * half) == (kind >= 2)) * (-1 if kind == 2 else 1)
    c16[:, G_COMB:G_COMB + P] = comb
    c16[:, G_TRI:G_TRI + P] = p[:, None] < p
    c16[:, G_ONE:G_ONE + P] = 1
    cbf = np.zeros((P, 2 * P), mybir.dt.np(BF16))
    cbf[:, 0:P] = np.eye(P)
    cbf[:, P:2 * P] = np.where((p[:, None] // J == p // J) & (p[:, None] >= p), 0.0, -1e30)
    pad = np.zeros((P, PAY_W), np.float32)
    pad[:, D] = 2 * B * S + p
    pad[:, D + 1] = -1
    pad[:, D + 2] = 1
    return c32, c16, cbf, pad


def laid_out(i):
    a = {k: np.asarray(v) for k, v in i.items()}
    ctxt = a["ctx_1024"].transpose(2, 0, 1)
    wqkv = a["L0_ffn_Wqkv"]
    qkc = np.concatenate([wqkv[:, :, 0:NROT], wqkv[:, :, D:D + NROT], wqkv[:, :, NROT:D], wqkv[:, :, D + NROT:2 * D]], 2)
    big = np.concatenate([
        qkc.transpose(1, 0, 2).reshape(P, -1),
        a["L1_ffn_gate_up_w"].transpose(2, 0, 1).reshape(P, -1),
        a["L1_ffn_down_w"].reshape(E, D, FC, P).transpose(3, 0, 2, 1).reshape(P, -1),
        a["L1_ffn_shared_gate_up_w"].T, a["L1_ffn_shared_down_w"].T], 1)
    c32, c16, cbf, pad = constants()
    return [
        a["x"], np.broadcast_to(ctxt[:, :, None, :], (P, B, HC, KC)),
        a["mask_SxS2_bk0"].reshape(T, P, KC).transpose(1, 0, 2),
        a["g_xattn"], a["g_ffn"], a["L0_xattn_Wq"].T, a["L0_xattn_Wkv"], a["L0_ffn_Wr"].T,
        wqkv[:, :, 2 * D:].transpose(2, 0, 1), a["L0_ffn_Wo"].transpose(1, 0, 2),
        a["L1_xattn_Wk"].T, a["L1_xattn_Wq"], a["L1_xattn_Wv"].T, a["L1_xattn_Wo"].T,
        a["L1_ffn_ln_gamma"], a["L1_ffn_ln_beta"], a["L1_ffn_router_w"].T, big, c32, c16, cbf, pad]


def kernel(**inputs):
    import concourse.bacc as bacc
    from concourse.bass_utils import run_bass_kernel_spmd

    nc = bacc.Bacc("TRN2", target_bir_lowering=False, num_devices=1)
    arrays, args = {}, []
    for n, v in enumerate(laid_out(inputs)):
        v = np.ascontiguousarray(v)
        arrays[f"in{n}"] = v
        args.append(nc.dram_tensor(f"in{n}", v.shape, mybir.dt.from_np(v.dtype), kind="ExternalInput").ap())
    args.append(nc.dram_tensor("out", (B, S, D), F32, kind="ExternalOutput").ap())
    build(nc, *args)
    return run_bass_kernel_spmd(nc, [arrays], core_ids=[0]).results[0]["out"]
```
